# Optimizing a Trainium2 kernel written in Bass

```python
import numpy as np
import jax
import jax.numpy as jnp

def _softmax(x, axis=-1):
    return jax.nn.softmax(x, axis=axis)

def _gelu(x):
    return jax.nn.gelu(x, approximate=True)

def _silu(x):
    return jax.nn.silu(x)

def _sigmoid(x):
    return jax.nn.sigmoid(x)

def _layernorm(x, axis=-1, eps=1e-05):
    m = jnp.mean(x, axis=axis, keepdims=True)
    v = jnp.var(x, axis=axis, keepdims=True)
    return (x - m) / jnp.sqrt(v + eps)

def _scatter_add(tgt, idx, src, axis=0):
    return tgt.at[idx].add(src)

def _segment_sum(src, seg, n):
    return jax.ops.segment_sum(src, seg, n)
kernel_name = 'mk_cond_seq_d4_seqx_r4_5204da'

def setup_inputs(seed: int=0):
    np.random.seed(seed)
    _w = jnp.asarray

    def _rec_inputs():
        import jax
        import jax.numpy as jnp
        _rk = jax.random.key(seed)
        x = -0.0005207 + 1.001 * jax.random.normal(jax.random.fold_in(_rk, 1), (16, 256, 256), jnp.float32)
        _lenS = 256 - jax.random.randint(jax.random.fold_in(_rk, 7), (16,), 0, max(1, 256 // 4) + 1, jnp.int32)
        _lenS2 = 256 - jax.random.randint(jax.random.fold_in(_rk, 8), (16,), 0, max(1, 256 // 4) + 1, jnp.int32)
        itok_B_34_63 = jax.random.randint(jax.random.fold_in(_rk, 12), (16,), 34, 64, jnp.int32)
        fside_Bx16xSxS_0 = -1.47943e-05 + 1.00017 * jax.random.normal(jax.random.fold_in(_rk, 13), (16, 16, 256, 256), jnp.float32)
        itok_B_0_7 = jax.random.randint(jax.random.fold_in(_rk, 14), (16,), 0, 8, jnp.int32)
        condB_t = jax.random.uniform(jax.random.fold_in(_rk, 15), (16,), jnp.float32, 0.0, 0.983423)
        itok_B_0_15 = jax.random.randint(jax.random.fold_in(_rk, 16), (16,), 0, 16, jnp.int32)
        _validS = jnp.arange(256)[None, :] < _lenS[:, None]
        _validS2 = jnp.arange(256)[None, :] < _lenS2[:, None]
        _causal = jnp.tril(jnp.ones((256, 256), dtype=bool))
        mask_Bx1xSxS_bk0 = jnp.logical_not(jnp.broadcast_to(_validS[:, None, None, :], (16, 1, 256, 256)))
        return (x, itok_B_34_63, fside_Bx16xSxS_0, itok_B_0_7, condB_t, itok_B_0_15, mask_Bx1xSxS_bk0)
    x, itok_B_34_63, fside_Bx16xSxS_0, itok_B_0_7, condB_t, itok_B_0_15, mask_Bx1xSxS_bk0 = _rec_inputs()

    def _L0_cond_setup():
        import jax, jax.numpy as jnp
        import numpy as np
        import math
        D_MODEL = 256
        N_HEAD = 16
        HEAD_DIM = D_MODEL // N_HEAD
        D_FF = 1024
        NUM_STEPS = 100.0
        RESCALE = 4000.0
        EPS = 1e-05

        def _sin_emb(t):
            half = D_MODEL // 2
            x = t.astype(jnp.float32) / NUM_STEPS * RESCALE
            freqs = jnp.exp(jnp.arange(half, dtype=jnp.float32) * (-math.log(10000.0) / (half - 1)))
            e = x[:, None] * freqs[None, :]
            return jnp.concatenate([jnp.sin(e), jnp.cos(e)], axis=-1)

        def _ln(x):
            m = jnp.mean(x, axis=-1, keepdims=True)
            v = jnp.var(x, axis=-1, keepdims=True)
            return (x - m) / jnp.sqrt(v + EPS)

        def _gelu2(x):
            return x * jax.nn.sigmoid(1.702 * x)
        key = jax.random.key(seed)
        ks = jax.random.split(key, 24)
        B, S, D, F = (4, 128, D_MODEL, D_FF)
        std = 0.02
        inp = {'src': jax.random.normal(ks[0], (B, S, D), dtype=jnp.float32), 'src_mask': jax.random.randint(ks[1], (B, 1, S, S), 0, 2).astype(bool), 'timestep': jax.random.randint(ks[2], (B,), 0, 100, dtype=jnp.int32), 'attention_bias': jax.random.normal(ks[3], (B, N_HEAD, S, S), dtype=jnp.float32), 'W_ada': jax.random.normal(ks[4], (D, 2 * D), dtype=jnp.float32) * std, 'b_ada': jnp.zeros((2 * D,), dtype=jnp.float32), 'Wq': jax.random.normal(ks[5], (D, D), dtype=jnp.float32) * std, 'bq': jnp.zeros((D,), dtype=jnp.float32), 'Wk': jax.random.normal(ks[6], (D, D), dtype=jnp.float32) * std, 'bk': jnp.zeros((D,), dtype=jnp.float32), 'Wv': jax.random.normal(ks[7], (D, D), dtype=jnp.float32) * std, 'bv': jnp.zeros((D,), dtype=jnp.float32), 'Wo': jax.random.normal(ks[8], (D, D), dtype=jnp.float32) * std, 'bo': jnp.zeros((D,), dtype=jnp.float32), 'W1': jax.random.normal(ks[9], (D, F), dtype=jnp.float32) * std, 'b1': jnp.zeros((F,), dtype=jnp.float32), 'W2': jax.random.normal(ks[10], (F, D), dtype=jnp.float32) * std, 'b2': jnp.zeros((D,), dtype=jnp.float32), 'g2': jnp.ones((D,), dtype=jnp.float32), 'beta2': jnp.zeros((D,), dtype=jnp.float32)}
        return inp
    _L0_cond_all = _L0_cond_setup()
    _L0_cond_in = {k: v for k, v in _L0_cond_all.items() if k in ('W_ada', 'b_ada', 'Wq', 'bq', 'Wk', 'bk', 'Wv', 'bv', 'Wo', 'bo', 'W1', 'b1', 'W2', 'b2', 'g2', 'beta2')}
    del _L0_cond_all

    def _L1_cond_setup():
        import jax, jax.numpy as jnp
        import numpy as np
        E, H, I = (8, 256, 1024)
        B, S = (4, 256)
        LN_EPS = 1e-12
        key = jax.random.key(seed)
        ks = jax.random.split(key, 8)
        x = jax.random.normal(ks[0], (B, S, H), dtype=jnp.float32)
        expert_idx = jax.random.randint(ks[1], (B,), 0, E, dtype=jnp.int64)
        Wi = jax.random.normal(ks[2], (E, H, I), dtype=jnp.float32) * 0.02
        bi = jnp.zeros((E, I), dtype=jnp.float32)
        Wo = jax.random.normal(ks[3], (E, I, H), dtype=jnp.float32) * 0.02
        bo = jnp.zeros((E, H), dtype=jnp.float32)
        gamma = jnp.ones((E, H), dtype=jnp.float32)
        beta = jnp.zeros((E, H), dtype=jnp.float32)
        return {'input_tensor': x, 'expert_idx': expert_idx, 'Wi': Wi, 'bi': bi, 'Wo': Wo, 'bo': bo, 'gamma': gamma, 'beta': beta}
    _L1_cond_all = _L1_cond_setup()
    _L1_cond_in = {k: v for k, v in _L1_cond_all.items() if k in ('Wi', 'bi', 'Wo', 'bo', 'gamma', 'beta')}
    del _L1_cond_all

    def _L2_cond_setup():
        import jax, jax.numpy as jnp
        import numpy as np
        import math
        B, S, D, E = (32, 256, 256, 128)

        def _layer_norm(x, gamma, beta, eps=1e-05):
            mean = jnp.mean(x, axis=(-2, -1), keepdims=True)
            var = jnp.mean(jnp.square(x - mean), axis=(-2, -1), keepdims=True)
            return (x - mean) * jax.lax.rsqrt(var + eps) * gamma + beta

        def _noise_encoding(t, channels):
            half = channels // 2
            freqs = jnp.exp(jnp.arange(half, dtype=jnp.float32) * (-math.log(10000.0) / (half - 1)))
            emb = 5000.0 * t[:, None] * freqs[None, :]
            return jnp.concatenate([jnp.sin(emb), jnp.cos(emb)], axis=1)
        key = jax.random.key(seed)
        ks = jax.random.split(key, 20)

        def lin(k, fan_in, shape):
            return jax.random.normal(k, shape, jnp.float32) / np.sqrt(fan_in)
        inp = {'x': jax.random.normal(ks[0], (B, S, D), jnp.float32), 't': jax.random.uniform(ks[1], (B,), jnp.float32), 'W1': lin(ks[2], E, (E, 4 * E)), 'b1': jnp.zeros((4 * E,), jnp.float32), 'W2': lin(ks[3], 4 * E, (4 * E, 4 * E)), 'b2': jnp.zeros((4 * E,), jnp.float32), 'Wsc': lin(ks[4], 4 * E, (4 * E, D)), 'bsc': jnp.zeros((D,), jnp.float32), 'Wsh': lin(ks[5], 4 * E, (4 * E, D)), 'bsh': jnp.zeros((D,), jnp.float32), 'gamma': jnp.ones((S, D), jnp.float32), 'beta': jnp.zeros((S, D), jnp.float32), 'W_in': lin(ks[6], D, (D, D)), 'b_in': jnp.zeros((D,), jnp.float32), 'W_out': lin(ks[7], D, (D, D)), 'b_out': jnp.zeros((D,), jnp.float32)}
        return inp
    _L2_cond_all = _L2_cond_setup()
    _L2_cond_in = {k: v for k, v in _L2_cond_all.items() if k in ('W1', 'b1', 'W2', 'b2', 'Wsc', 'bsc', 'Wsh', 'bsh', 'gamma', 'beta', 'W_in', 'b_in', 'W_out', 'b_out')}
    del _L2_cond_all

    def _L3_cond_setup():
        import jax, jax.numpy as jnp
        import numpy as np
        B, S, D = (32, 256, 256)
        A = 64
        E = 16
        LN_EPS = 1e-05
        key = jax.random.key(seed)
        ks = jax.random.split(key, 10)
        s = lambda fan_in: 1.0 / np.sqrt(fan_in)
        return {'hidden_states': jax.random.normal(ks[0], (B, S, D), dtype=jnp.float32), 'domain_id': jax.random.randint(ks[1], (B,), 0, E, dtype=jnp.int64), 'down_W': jax.random.uniform(ks[2], (A, D), jnp.float32, -s(D), s(D)), 'down_b': jax.random.uniform(ks[3], (A,), jnp.float32, -s(D), s(D)), 'up_W': jax.random.uniform(ks[4], (D, A), jnp.float32, -s(A), s(A)), 'up_b': jax.random.uniform(ks[5], (D,), jnp.float32, -s(A), s(A)), 'expert_W': jax.random.uniform(ks[6], (E, A, A), jnp.float32, -s(A), s(A)), 'expert_b': jax.random.uniform(ks[7], (E, A), jnp.float32, -s(A), s(A)), 'domain_emb': jax.random.normal(ks[8], (E, A), dtype=jnp.float32), 'ln_gamma': jnp.ones((D,), jnp.float32), 'ln_beta': jnp.zeros((D,), jnp.float32)}
    _L3_cond_all = _L3_cond_setup()
    _L3_cond_in = {k: v for k, v in _L3_cond_all.items() if k in ('down_W', 'down_b', 'up_W', 'up_b', 'expert_W', 'expert_b', 'domain_emb', 'ln_gamma', 'ln_beta')}
    del _L3_cond_all
    return {'x': x, 'itok_B_34_63': itok_B_34_63, 'fside_Bx16xSxS_0': fside_Bx16xSxS_0, 'itok_B_0_7': itok_B_0_7, 'condB_t': condB_t, 'itok_B_0_15': itok_B_0_15, 'mask_Bx1xSxS_bk0': mask_Bx1xSxS_bk0, 'L0_cond_W_ada': _L0_cond_in['W_ada'], 'L0_cond_b_ada': _L0_cond_in['b_ada'], 'L0_cond_Wq': _L0_cond_in['Wq'], 'L0_cond_bq': _L0_cond_in['bq'], 'L0_cond_Wk': _L0_cond_in['Wk'], 'L0_cond_bk': _L0_cond_in['bk'], 'L0_cond_Wv': _L0_cond_in['Wv'], 'L0_cond_bv': _L0_cond_in['bv'], 'L0_cond_Wo': _L0_cond_in['Wo'], 'L0_cond_bo': _L0_cond_in['bo'], 'L0_cond_W1': _L0_cond_in['W1'], 'L0_cond_b1': _L0_cond_in['b1'], 'L0_cond_W2': _L0_cond_in['W2'], 'L0_cond_b2': _L0_cond_in['b2'], 'L0_cond_g2': _L0_cond_in['g2'], 'L0_cond_beta2': _L0_cond_in['beta2'], 'L1_cond_Wi': _L1_cond_in['Wi'], 'L1_cond_bi': _L1_cond_in['bi'], 'L1_cond_Wo': _L1_cond_in['Wo'], 'L1_cond_bo': _L1_cond_in['bo'], 'L1_cond_gamma': _L1_cond_in['gamma'], 'L1_cond_beta': _L1_cond_in['beta'], 'L2_cond_W1': _L2_cond_in['W1'], 'L2_cond_b1': _L2_cond_in['b1'], 'L2_cond_W2': _L2_cond_in['W2'], 'L2_cond_b2': _L2_cond_in['b2'], 'L2_cond_Wsc': _L2_cond_in['Wsc'], 'L2_cond_bsc': _L2_cond_in['bsc'], 'L2_cond_Wsh': _L2_cond_in['Wsh'], 'L2_cond_bsh': _L2_cond_in['bsh'], 'L2_cond_gamma': _L2_cond_in['gamma'], 'L2_cond_beta': _L2_cond_in['beta'], 'L2_cond_W_in': _L2_cond_in['W_in'], 'L2_cond_b_in': _L2_cond_in['b_in'], 'L2_cond_W_out': _L2_cond_in['W_out'], 'L2_cond_b_out': _L2_cond_in['b_out'], 'L3_cond_down_W': _L3_cond_in['down_W'], 'L3_cond_down_b': _L3_cond_in['down_b'], 'L3_cond_up_W': _L3_cond_in['up_W'], 'L3_cond_up_b': _L3_cond_in['up_b'], 'L3_cond_expert_W': _L3_cond_in['expert_W'], 'L3_cond_expert_b': _L3_cond_in['expert_b'], 'L3_cond_domain_emb': _L3_cond_in['domain_emb'], 'L3_cond_ln_gamma': _L3_cond_in['ln_gamma'], 'L3_cond_ln_beta': _L3_cond_in['ln_beta']}

def reference(x, itok_B_34_63, fside_Bx16xSxS_0, itok_B_0_7, condB_t, itok_B_0_15, mask_Bx1xSxS_bk0, L0_cond_W_ada, L0_cond_b_ada, L0_cond_Wq, L0_cond_bq, L0_cond_Wk, L0_cond_bk, L0_cond_Wv, L0_cond_bv, L0_cond_Wo, L0_cond_bo, L0_cond_W1, L0_cond_b1, L0_cond_W2, L0_cond_b2, L0_cond_g2, L0_cond_beta2, L1_cond_Wi, L1_cond_bi, L1_cond_Wo, L1_cond_bo, L1_cond_gamma, L1_cond_beta, L2_cond_W1, L2_cond_b1, L2_cond_W2, L2_cond_b2, L2_cond_Wsc, L2_cond_bsc, L2_cond_Wsh, L2_cond_bsh, L2_cond_gamma, L2_cond_beta, L2_cond_W_in, L2_cond_b_in, L2_cond_W_out, L2_cond_b_out, L3_cond_down_W, L3_cond_down_b, L3_cond_up_W, L3_cond_up_b, L3_cond_expert_W, L3_cond_expert_b, L3_cond_domain_emb, L3_cond_ln_gamma, L3_cond_ln_beta):
    import jax
    import jax.numpy as jnp

    def _L0_cond_ref(src, src_mask, timestep, attention_bias, W_ada, b_ada, Wq, bq, Wk, bk, Wv, bv, Wo, bo, W1, b1, W2, b2, g2, beta2):
        import jax, jax.numpy as jnp
        import numpy as np
        import math
        D_MODEL = 256
        N_HEAD = 16
        HEAD_DIM = D_MODEL // N_HEAD
        D_FF = 1024
        NUM_STEPS = 100.0
        RESCALE = 4000.0
        EPS = 1e-05

        def _sin_emb(t):
            half = D_MODEL // 2
            x = t.astype(jnp.float32) / NUM_STEPS * RESCALE
            freqs = jnp.exp(jnp.arange(half, dtype=jnp.float32) * (-math.log(10000.0) / (half - 1)))
            e = x[:, None] * freqs[None, :]
            return jnp.concatenate([jnp.sin(e), jnp.cos(e)], axis=-1)

        def _ln(x):
            m = jnp.mean(x, axis=-1, keepdims=True)
            v = jnp.var(x, axis=-1, keepdims=True)
            return (x - m) / jnp.sqrt(v + EPS)

        def _gelu2(x):
            return x * jax.nn.sigmoid(1.702 * x)
        B, S, D = src.shape
        emb = jax.nn.silu(_sin_emb(timestep)) @ W_ada + b_ada
        scale, shift = jnp.split(emb[:, None, :], 2, axis=-1)
        x = _ln(src) * (1.0 + scale) + shift
        q = (x @ Wq + bq).reshape(B, S, N_HEAD, HEAD_DIM).transpose(0, 2, 1, 3)
        k = (x @ Wk + bk).reshape(B, S, N_HEAD, HEAD_DIM).transpose(0, 2, 1, 3)
        v = (x @ Wv + bv).reshape(B, S, N_HEAD, HEAD_DIM).transpose(0, 2, 1, 3)
        scores = jnp.einsum('bhqd,bhkd->bhqk', q / math.sqrt(HEAD_DIM), k)
        scores = scores + attention_bias
        scores = jnp.where(src_mask, -jnp.inf, scores.astype(jnp.float32))
        probs = jax.nn.softmax(scores, axis=-1).astype(v.dtype)
        ctx = jnp.einsum('bhqk,bhkd->bhqd', probs, v)
        ctx = ctx.transpose(0, 2, 1, 3).reshape(B, S, D)
        x = x + (ctx @ Wo + bo)
        h = _ln(x) * g2 + beta2
        ff = _gelu2(h @ W1 + b1) @ W2 + b2
        return x + ff

    def _L1_cond_ref(input_tensor, expert_idx, Wi, bi, Wo, bo, gamma, beta):
        import jax, jax.numpy as jnp
        import numpy as np
        E, H, I = (8, 256, 1024)
        B, S = (4, 256)
        LN_EPS = 1e-12
        Wi_b = Wi[expert_idx]
        bi_b = bi[expert_idx]
        Wo_b = Wo[expert_idx]
        bo_b = bo[expert_idx]
        g_b = gamma[expert_idx]
        be_b = beta[expert_idx]
        h = jax.nn.gelu(jnp.einsum('bsh,bhi->bsi', input_tensor, Wi_b) + bi_b[:, None, :], approximate=False)
        o = jnp.einsum('bsi,bih->bsh', h, Wo_b) + bo_b[:, None, :]
        r = o + input_tensor
        mu = jnp.mean(r, axis=-1, keepdims=True)
        var = jnp.mean(jnp.square(r - mu), axis=-1, keepdims=True)
        y = (r - mu) * jax.lax.rsqrt(var + LN_EPS)
        return y * g_b[:, None, :] + be_b[:, None, :]

    def _L2_cond_ref(x, t, W1, b1, W2, b2, Wsc, bsc, Wsh, bsh, gamma, beta, W_in, b_in, W_out, b_out):
        import jax, jax.numpy as jnp
        import numpy as np
        import math
        B, S, D, E = (32, 256, 256, 128)

        def _layer_norm(x, gamma, beta, eps=1e-05):
            mean = jnp.mean(x, axis=(-2, -1), keepdims=True)
            var = jnp.mean(jnp.square(x - mean), axis=(-2, -1), keepdims=True)
            return (x - mean) * jax.lax.rsqrt(var + eps) * gamma + beta

        def _noise_encoding(t, channels):
            half = channels // 2
            freqs = jnp.exp(jnp.arange(half, dtype=jnp.float32) * (-math.log(10000.0) / (half - 1)))
            emb = 5000.0 * t[:, None] * freqs[None, :]
            return jnp.concatenate([jnp.sin(emb), jnp.cos(emb)], axis=1)
        h = _noise_encoding(t, E)
        h = jax.nn.silu(h @ W1 + b1)
        h = h @ W2 + b2
        scale = (h @ Wsc + bsc)[:, None, :]
        shift = (h @ Wsh + bsh)[:, None, :]
        out = jax.nn.silu(scale * _layer_norm(x, gamma, beta) + shift)
        out = out @ W_in + b_in
        out = jax.nn.silu(scale * _layer_norm(out, gamma, beta) + shift)
        out = out @ W_out + b_out
        return out + x

    def _L3_cond_ref(hidden_states, domain_id, down_W, down_b, up_W, up_b, expert_W, expert_b, domain_emb, ln_gamma, ln_beta):
        import jax, jax.numpy as jnp
        import numpy as np
        B, S, D = (32, 256, 256)
        A = 64
        E = 16
        LN_EPS = 1e-05
        residual = hidden_states
        hidden = jnp.einsum('bsd,ad->bsa', hidden_states, down_W) + down_b
        hidden = jax.nn.gelu(hidden, approximate=False)
        valid = (domain_id >= 0) & (domain_id < E)
        idx = jnp.clip(domain_id, 0, E - 1)
        Wsel = expert_W[idx]
        bsel = expert_b[idx]
        expert_out = jnp.einsum('bsa,boa->bso', hidden, Wsel) + bsel[:, None, :]
        domain_output = jnp.where(valid[:, None, None], expert_out, hidden)
        hidden = domain_output + domain_emb[idx][:, None, :]
        hidden = jnp.einsum('bsa,da->bsd', hidden, up_W) + up_b
        x = hidden + residual
        mu = jnp.mean(x, axis=-1, keepdims=True)
        var = jnp.mean(jnp.square(x - mu), axis=-1, keepdims=True)
        return (x - mu) * jax.lax.rsqrt(var + LN_EPS) * ln_gamma + ln_beta
    x = _L0_cond_ref(x, mask_Bx1xSxS_bk0, itok_B_34_63, fside_Bx16xSxS_0, L0_cond_W_ada, L0_cond_b_ada, L0_cond_Wq, L0_cond_bq, L0_cond_Wk, L0_cond_bk, L0_cond_Wv, L0_cond_bv, L0_cond_Wo, L0_cond_bo, L0_cond_W1, L0_cond_b1, L0_cond_W2, L0_cond_b2, L0_cond_g2, L0_cond_beta2)
    x = _L1_cond_ref(x, itok_B_0_7, L1_cond_Wi, L1_cond_bi, L1_cond_Wo, L1_cond_bo, L1_cond_gamma, L1_cond_beta)
    x = _L2_cond_ref(x, condB_t, L2_cond_W1, L2_cond_b1, L2_cond_W2, L2_cond_b2, L2_cond_Wsc, L2_cond_bsc, L2_cond_Wsh, L2_cond_bsh, L2_cond_gamma, L2_cond_beta, L2_cond_W_in, L2_cond_b_in, L2_cond_W_out, L2_cond_b_out)
    x = _L3_cond_ref(x, itok_B_0_15, L3_cond_down_W, L3_cond_down_b, L3_cond_up_W, L3_cond_up_b, L3_cond_expert_W, L3_cond_expert_b, L3_cond_domain_emb, L3_cond_ln_gamma, L3_cond_ln_beta)
    return x

_drawn_inputs = setup_inputs


def setup_inputs(seed=0):
    import zlib

    import numpy as np

    out = dict(_drawn_inputs(seed))
    spreads = {'L0_cond_b_ada': (0.0, 0.1),
     'L0_cond_bq': (0.0, 0.8),
     'L0_cond_bk': (0.0, 0.8),
     'L0_cond_bv': (0.0, 0.318),
     'L0_cond_bo': (0.0, 0.1),
     'L0_cond_b1': (0.0, 0.274),
     'L0_cond_b2': (0.0, 0.1),
     'L0_cond_g2': (1.0, 0.6),
     'L0_cond_beta2': (0.0, 0.8),
     'L1_cond_bi': (0.0, 0.28),
     'L1_cond_bo': (0.0, 0.1),
     'L1_cond_gamma': (1.0, 0.2),
     'L1_cond_beta': (0.0, 0.1),
     'L2_cond_b1': (0.0, 0.1),
     'L2_cond_b2': (0.0, 0.1),
     'L2_cond_bsc': (0.0, 0.1),
     'L2_cond_bsh': (0.0, 0.1),
     'L2_cond_gamma': (1.0, 0.2),
     'L2_cond_beta': (0.0, 0.317),
     'L2_cond_b_in': (0.0, 0.1),
     'L2_cond_b_out': (0.0, 0.1),
     'L3_cond_ln_gamma': (1.0, 0.2),
     'L3_cond_ln_beta': (0.0, 0.1)}
    factors = {'fside_Bx16xSxS_0': 7.899,
     'L0_cond_Wq': 8.0,
     'L0_cond_Wk': 8.0,
     'L0_cond_Wv': 3.467,
     'L3_cond_down_b': 8.0}
    for name, (base, spread) in spreads.items():
        noise = np.random.default_rng([zlib.crc32(name.encode()), seed]).standard_normal(out[name].shape)
        drawn = base * np.exp(spread * noise) if base else spread * noise
        out[name] = jnp.asarray(drawn.astype(out[name].dtype))
    for name, factor in factors.items():
        out[name] = (out[name] * factor).astype(out[name].dtype)
    return out
```

```python
from contextlib import ExitStack
import math

import numpy as np

import concourse.bass as bass
from concourse import mybir

F32 = mybir.dt.float32
F32R = mybir.dt.float32r
I32 = mybir.dt.int32
U8 = mybir.dt.uint8
ALU = mybir.AluOpType
ACT = mybir.ActivationFunctionType

B, S, D = 16, 256, 256
H, HD = 16, 16
F = 1024
P = 128
ST = S // P
DT = D // P
FT = F // P
HG = 8
NE1, NE3, A3 = 8, 16, 64
BIG = 3.0e38
MASKED = -1.0e30
DMA = 16
RING = 4

SCHEDULE = {
    0: ["vpad", "rb"],
    1: ["wo", "tr4"],
    2: ["st1"],
    3: ["resid", "tr2", "u1"],
    4: ["fa"],
    5: ["win", "lnp"],
    6: ["fb"],
    7: ["st2", "ff2a"],
    8: ["u2", "ff2b", "trp"],
    9: ["wout", "tr3", "q"],
    10: ["down", "ea"],
    11: ["exp", "k"],
    12: ["tr5", "eb"],
    13: ["up", "v", "e2a"],
    14: ["e2b"],
    15: [],
}
PHASE = {
    "pre": ["lnp", "trp", "q", "k", "v"],
    "att": ["vpad", "resid"],
    "mid": ["rb", "wo", "tr2", "fa", "fb", "ff2a", "ff2b", "tr3", "ea", "eb", "e2a", "e2b"],
    "end": ["tr4", "st1", "u1", "win", "st2", "u2", "wout", "down", "exp", "tr5", "up"],
}
PHASE_OF = {stage: phase for phase, stages in PHASE.items() for stage in stages}

TWO_PI = 2.0 * math.pi
PI_1 = 6.28125
PI_2 = float(np.float32(TWO_PI - PI_1).view(np.uint32) & np.uint32(0xFFFFF000)) if False else 0.001934051513671875
PI_3 = TWO_PI - PI_1 - PI_2
ROUND = 1.5 * 2.0 ** 23
PI_LIMIT = 3.1415925


def need(eng, sem, value):
    if isinstance(value, int) and value <= 0:
        return
    eng.wait_ge(sem, value)


def build(nc, a):
    with ExitStack() as ctx:
        def sb(name, shape, dt=F32):
            return ctx.enter_context(nc.sbuf_tensor(name, shape, dt))

        def bank(name, shape):
            return ctx.enter_context(nc.psum_tensor(name, shape, F32))

        def sem(name):
            return ctx.enter_context(nc.semaphore(name))

        ident = sb("ident", [P, P])
        mean_w = sb("mean_w", [P, P])
        neg_half = sb("neg_half", [P, 2])
        wq, wk, wv, wo = (sb(n, [P, DT, D]) for n in ("wq", "wk", "wv", "wo"))
        w1 = sb("w1", [P, DT, F])
        w2 = sb("w2", [P, FT, D])
        wi = sb("wi", [P, DT, F])
        woe = sb("woe", [P, FT, D])
        w_in, w_out = sb("w_in", [P, DT, D]), sb("w_out", [P, DT, D])
        gam2, bet2 = sb("gam2", [P, DT, S]), sb("bet2", [P, DT, S])
        down_w = sb("down_w", [P, DT, A3])
        up_w = sb("up_w", [A3, D])
        vec = sb("vec", [P, 27])
        VQ, VK, VG2, VBE2, VB1, VBIN, VBOUT, VUPB, VDNB = 0, 2, 4, 6, 8, 16, 18, 20, 22
        qkb = sb("qkb", [P, 2])
        bv_row, b2_row = sb("bv_row", [P, D]), sb("b2_row", [P, D])
        lng_row, lnb_row = sb("lng_row", [P, D]), sb("lnb_row", [P, D])

        x_in = sb("x_in", [P, ST, D])
        xn = sb("xn", [P, ST, D])
        cond_cols = sb("cond_cols", [P, B, 4])
        cond2_cols = sb("cond2_cols", [P, B, 4])
        cols = sb("cols", [P, 4])
        rows = sb("rows", [P, 2 * D])
        x1T = sb("x1T", [P, DT, S])
        qkf = sb("qkf", [P, DT, S])
        q_hi, q_lo, k_hi, k_lo = (sb(n, [P, DT, S], F32R) for n in ("q_hi", "q_lo", "k_hi", "k_lo"))
        q_stack = sb("q_stack", [4 * HD, H, S], F32R)
        k_stack = sb("k_stack", [4 * HD, H, S], F32R)
        GW = HG * (P + HD)
        vpad = sb("vpad", [P, ST, 2, GW])
        bias = sb("bias", [P, RING, 2, ST, S])
        mask_in = sb("mask_in", [P, ST, S], U8)
        mask_add = sb("mask_add", [P, ST, S])
        nmax = sb("nmax", [P, 2, ST])
        probs = sb("probs", [P, 2, ST, S])
        probsT = sb("probsT", [P, 2, ST, S])
        rowsum = sb("rowsum", [P, ST, H])
        rinv = sb("rinv", [P, ST, H])
        rinv_wide = sb("rinv_wide", [P, ST, D])
        rinv_sb = sb("rinv_sb", [P, 2, S])
        ctxT = sb("ctxT", [P, DT, S])
        resid = sb("resid", [P, ST, D])
        x2 = sb("x2", [P, ST, D])
        x2n = sb("x2n", [P, ST, D])
        x2b = sb("x2b", [P, ST, D])
        h1T = sb("h1T", [P, DT, S])
        hT = sb("hT", [P, FT, S])
        x3 = sb("x3", [P, ST, D])
        x3b = sb("x3b", [P, ST, D])
        x3T = sb("x3T", [P, DT, S])
        bo_row = sb("bo_row", [P, D])
        ep = sb("ep", [P, FT + 4])
        x4 = sb("x4", [P, ST, D])
        yn = sb("yn", [P, ST, D])
        x4T = sb("x4T", [P, DT, S])
        cols2 = sb("cols2", [P, 4])
        u = sb("u", [P, DT, S])
        z = sb("z", [P, DT, S])
        y = sb("y", [P, DT, S])
        x5T = sb("x5T", [P, DT, S])
        x5b = sb("x5b", [P, DT, S])
        x5 = sb("x5", [P, ST, D])
        x6 = sb("x6", [P, ST, D])
        hid = sb("hid", [A3, S])
        dom = sb("dom", [A3, S])
        l3 = sb("l3", [A3, A3 + 2])
        idcol = sb("idcol", [A3, 1], I32)
        sel = sb("sel", [A3, 4])
        wsel = sb("wsel", [A3, A3])
        ids = sb("ids", [1, 2 * B], I32)
        ids_ok = sb("ids_ok", [1, 2 * B], I32)

        def stat_tiles(n):
            return (sb(f"bn{n}", [P, ST, 6]), sb(f"mv{n}", [P, ST, 2]), sb(f"ve{n}", [P, ST]), sb(f"rs{n}", [P, ST]))

        stat_p, stat_2, stat_e, stat_f = (stat_tiles(n) for n in "p2ef")
        g_bn, g_mv, g_all, g_ve, g_rs = (sb(n, [P, k]) for n, k in
                                         (("g_bn", 6), ("g_mv", 2), ("g_all", 2), ("g_ve", 2), ("g_rs", 1)))

        w_ada = hT[:, 0:4, :].rearrange("p (k a) n -> p k (a n)", k=2)
        w1c = hT[:, 4:6, :].rearrange("p a n -> p (a n)")
        w2c = woe[:, :, :].rearrange("p (k a) n -> p k (a n)", k=4)
        wsc = wi[:, 0, :].rearrange("p (k n) -> p k n", k=4)
        wsh = wi[:, 1, :].rearrange("p (k n) -> p k n", k=4)
        ang = u[:, 0, 0:48].rearrange("p (t b) -> p t b", t=3)
        red = u[:, 0, 48:96].rearrange("p (t b) -> p t b", t=3)
        kk = u[:, 0, 96:144].rearrange("p (t b) -> p t b", t=3)
        emb = u[:, 0, 144:192].rearrange("p (t b) -> p t b", t=3)
        fq = u[:, 1, 0:6]
        ph2 = u[:, 1, 6:9]
        t_f = u[:, 1, 16:48].rearrange("p (t b) -> p t b", t=2)
        h1c = u[:, 1, 48:112].rearrange("p (m b) -> p m b", m=4)
        h2c = u[:, 1, 112:176].rearrange("p (m b) -> p m b", m=4)
        cvec = z[:, 0, 0:16]
        t_i = z[:, 0, 16:32].bitcast(I32)
        ada_row = z[0:B, 1, :]
        ada_b = y[0:B, :, :].rearrange("p a n -> p (a n)")
        ada_c = x5T[0:B, :, :].rearrange("p a n -> p (a n)")
        emb_rows = x5b[0:B, :, :].rearrange("p a n -> p (a n)")

        sc_ps = [bank(f"sc_ps{i}", [P, ST, S]) for i in range(2)]
        pt_ps = bank("pt_ps", [P, ST, S])
        ctx_ps = bank("ctx_ps", [P, 2, S])
        pre_ps = bank("pre_ps", [P, 2, S])
        mid_ps = [bank(f"mid_ps{i}", [P, 2, S]) for i in range(2)]
        end_ps = bank("end_ps", [P, 2, S])

        names = """settled w_cond w_cond2 w_vec w_qkv w_mid w_end w_id consts_v consts_p pro_v pro_a pro_p rows_out
        x_loaded cols_loaded rows_loaded mask_loaded wi_loaded woe_loaded ep_loaded bo_loaded cols2_loaded
        l3_loaded id_loaded out_stored stack0 stack1
        lnp rsq_p trp_pe x1T_done q_pe k_pe v_pe qkf_done hi_done lo_done v_done resid_done
        scored negated masked maxed exped turned turned_sb pv_done rinv_done
        rb_pe rb_sb ctx_done wo_pe ln2 rsq_2 x2b_done tr2_pe h1T_done ff1_pe ff1_done ff2_pe x3_done x3b_done
        tr3_pe x3T_done e1_pe e1_done e2_pe lne rsq_e
        tr4_pe x4T_done l2 st_pe rsq_g z_done win_pe y_done wout_pe x5b_done down_pe hid_done exp_pe dom_done
        sel_done tr5_pe x5_done up_pe lnf rsq_f fin""".split()
        s = {n: sem(n) for n in names}
        s_bias = [sem(f"bias_loaded{i}") for i in range(RING)]
        N = dict(lnp=7, rinv_done=2, x1T_done=2, qkf_done=4, hi_done=2, lo_done=2, v_done=4, resid_done=4,
                 scored=H, masked=H, maxed=2 * H, exped=2 * H, turned=H, turned_sb=H, pv_done=H,
                 ln2=8, x2b_done=2, h1T_done=2, ff1_pe=4, ff1_done=8, ff2_pe=2, x3_done=2, x3b_done=2,
                 e1_pe=4, e1_done=8, e2_pe=2, lne=9, x4T_done=2, l2=18, st_pe=2, rsq_g=2, z_done=4, y_done=2,
                 x5b_done=2, sel_done=6, lnf=8, fin=4)
        for n in ("x_loaded cols_loaded rows_loaded mask_loaded wi_loaded woe_loaded ep_loaded bo_loaded "
                  "cols2_loaded l3_loaded id_loaded out_stored").split():
            N[n] = DMA
        N["stack0"] = N["stack1"] = 8 * DMA

        def at(eng, name, batch, k=None):
            n = N.get(name, 1)
            k = n if k is None else k
            if isinstance(batch, int) and batch >= B:
                batch, k = B - 1, n
            need(eng, s[name], batch * n + k)
            if eng is nc.sync and not isinstance(batch, int):
                settle(eng)

        def settle(eng):
            eng.sem_inc(s["settled"], 1)

        x_v = a["x"].rearrange("b (t p) d -> b p t d", p=P)
        out_v = a["out"].rearrange("b (t p) d -> b p t d", p=P)
        f_v = a["fside"].rearrange("b h (t p) k -> b p h t k", p=P)
        mask_v = a["mask"].rearrange("b o (t p) k -> b p (o t) k", p=P)
        wi_v = a["Wi"].rearrange("e (k p) n -> e p k n", p=P)
        woe_v = a["Woe"].rearrange("e (k p) n -> e p k n", p=P)
        rows_d = nc.dram_tensor("rows_scratch", (B, 2 * D), F32, kind="Internal").ap()

        def k_tiles(w):
            return w.rearrange("(k p) n -> p k n", p=P)

        def drive(eng, head, stages, before=None):
            def iteration(it, phases):
                for slot in range(H):
                    head(it, slot, "att" in phases, "pre" in phases)
                    for stage in SCHEDULE[slot]:
                        if stage in stages and PHASE_OF[stage] in phases:
                            stages[stage](it)
                    if before and slot in before:
                        before[slot](it, phases)

            def active(it):
                on = {"pre": 0 <= it + 1 < B, "att": 0 <= it < B, "mid": 0 <= it - 1 < B, "end": 0 <= it - 2 < B}
                return [p for p, yes in on.items() if yes]

            for it in (-1, 0, 1, 2):
                iteration(it, active(it))
            with eng.Fori(3, B - 1) as it:
                iteration(it, active(3))
            for it in (B - 1, B, B + 1):
                iteration(it, active(it))

        block = ctx.enter_context(nc.Block())

        @block.sync
        def _(sp):
            def load(dst, src, name):
                sp.dma_start(dst, src).then_inc(s[name], DMA)

            load(fq, a["freqs"], "w_cond")
            load(t_i, a["timestep"].partition_broadcast(P), "w_cond")
            load(t_f[:, 1, :], a["t2"].partition_broadcast(P), "w_cond")
            load(cvec, a["cvec"], "w_cond")
            load(ident[:], a["ident"], "w_id")
            load(ids[:, 0:B], a["id1"].partition_broadcast(1), "w_cond")
            load(ids[:, B:], a["id3"].partition_broadcast(1), "w_cond")
            load(vec[:], a["vec"], "w_vec")
            load(w_ada, k_tiles(a["W_ada"]), "w_cond2")
            load(ada_b, a["b_ada"].partition_broadcast(B), "w_cond2")
            load(ada_c[:, D:], a["bo"].partition_broadcast(B), "w_cond2")
            load(mask_in[:], mask_v[0], "mask_loaded")
            load(wq[:], k_tiles(a["Wq"]), "w_qkv")
            load(wk[:], k_tiles(a["Wk"]), "w_qkv")
            load(wv[:], k_tiles(a["Wv"]), "w_qkv")
            load(bv_row[:], a["bv"].partition_broadcast(P), "w_qkv")
            for pair in range(RING):
                sp.dma_start(bias[:, pair], f_v[0][:, 2 * pair:2 * pair + 2]).then_inc(s_bias[pair], DMA)
            load(w1c, a["W1c"], "w_end")
            load(w2c, k_tiles(a["W2c"]), "w_end")
            load(wsc, k_tiles(a["Wsc"]), "w_end")
            load(wsh, k_tiles(a["Wsh"]), "w_end")
            load(wo[:], k_tiles(a["Wo"]), "w_mid")
            load(w1[:], k_tiles(a["W1"]), "w_mid")
            load(w2[:], k_tiles(a["W2"]), "w_mid")
            load(b2_row[:], a["b2"].partition_broadcast(P), "w_mid")
            load(w_in[:], k_tiles(a["W_in"]), "w_mid")
            load(w_out[:], k_tiles(a["W_out"]), "w_mid")
            load(gam2[:], k_tiles(a["gamT"]), "w_mid")
            load(bet2[:], k_tiles(a["betT"]), "w_mid")
            load(down_w[:], k_tiles(a["down_wT"]), "w_mid")
            load(up_w[:], a["up_wT"], "w_mid")
            load(lng_row[:], a["ln_g"].partition_broadcast(P), "w_mid")
            load(lnb_row[:], a["ln_b"].partition_broadcast(P), "w_mid")
            sp.wait_ge(s["pro_v"], PRO_ROWS)
            load(rows_d, emb_rows, "rows_out")
            sp.wait_ge(s["rows_out"], DMA)

            def expert(batch, base, last):
                index = sp.value_load(ids_ok[0:1, bass.ds(base + batch, 1)], min_val=0, max_val=last)
                return index

            def head(it, slot, att, pre):
                if att and slot % 2 == 0:
                    pair = slot // 2 + RING
                    if pair < H // 2 or pre:
                        at(sp, "exped", it, 2 * (slot + 2))
                        batch = it if pair < H // 2 else it + 1
                        pair %= H // 2
                        sp.dma_start(bias[:, pair % RING], f_v[batch][:, 2 * pair:2 * pair + 2])\
                            .then_inc(s_bias[pair % RING], DMA)

            def loads0(it, phases):
                if "pre" in phases:
                    at(sp, "lnp", it)
                    load(x_in[:], x_v[it + 1], "x_loaded")
                    at(sp, "x1T_done", it)
                    if isinstance(it, int) and it < 0:
                        sp.wait_ge(s["pro_v"], PRO_COLS)
                    load(cols[:], cond_cols[:, it + 1, :], "cols_loaded")
                    if not (isinstance(it, int) and it < 0):
                        at(sp, "negated", it)
                        load(mask_in[:], mask_v[it + 1], "mask_loaded")
                if "att" in phases:
                    at(sp, "resid_done", it - 1)
                    load(rows[:], rows_d[it].partition_broadcast(P), "rows_loaded")
                if "end" in phases:
                    if isinstance(it, int) and it == 2:
                        sp.wait_ge(s["pro_v"], PRO_COLS2)
                    at(sp, "z_done", it - 3)
                    load(cols2[:], cond2_cols[:, it - 2, :], "cols2_loaded")

            def loads2(it, phases):
                if "mid" in phases:
                    e = expert(it - 1, 0, NE1 - 1)
                    at(sp, "x4T_done", it - 2)
                    load(ep[:], a["ep"][e], "ep_loaded")
                    at(sp, "x3b_done", it - 2)
                    load(bo_row[:], a["boe"][e].partition_broadcast(P), "bo_loaded")
                if "end" in phases:
                    e = expert(it - 2, B, NE3 - 1)
                    at(sp, "dom_done", it - 3)
                    load(l3[:], a["l3"][e], "l3_loaded")
                    load(idcol[:], a["id3"][bass.ds(it - 2, 1)].partition_broadcast(A3), "id_loaded")

            def loads12(it, phases):
                if "pre" in phases:
                    stack(it, 0)

            def stack(it, t):
                at(sp, "lo_done", it + 1)
                at(sp, "scored", it, HG * (t + 1))
                for dst, parts in ((q_stack, (q_hi, q_hi, q_lo, q_lo)), (k_stack, (k_hi, k_lo, k_hi, k_lo))):
                    for j, part in enumerate(parts):
                        load(dst[HD * j:HD * j + HD, HG * t:HG * t + HG, :].bitcast(F32), part[:, t, :].bitcast(F32), f"stack{t}")

            def loads13(it, phases):
                if "att" in phases:
                    at(sp, "e1_pe", it - 1)
                    if isinstance(it, int) and it == 0:
                        sp.wait_ge(s["pro_p"], PRO_PE_ALL)
                    load(wi[:], wi_v[expert(it, 0, NE1 - 1)], "wi_loaded")

            def loads15(it, phases):
                if "att" in phases:
                    at(sp, "e2_pe", it - 1)
                    load(woe[:], woe_v[expert(it, 0, NE1 - 1)], "woe_loaded")
                if "pre" in phases:
                    stack(it, 1)
                if "end" in phases:
                    at(sp, "fin", it - 2)
                    load(out_v[it - 2], x6[:], "out_stored")

            drive(sp, head, {}, {0: loads0, 2: loads2, 12: loads12, 13: loads13, 15: loads15})
            sp.wait_ge(s["out_stored"], B * DMA)

        @block.tensor
        def _(pe):
            def turn(dst, src, name):
                for i in range(2):
                    for j in range(2):
                        last = pe.transpose(dst[:, j, i * P:(i + 1) * P], src[:, i, j * P:(j + 1) * P], ident[:])
                last.then_inc(s[name], 1)

            def product(dst, lhsT, rhs, kt):
                for k in range(kt):
                    last = pe.matmul(dst, lhsT(k), rhs(k), start=(k == 0), stop=(k == kt - 1))
                return last

            pe.wait_ge(s["w_cond2"], 3 * DMA)
            pe.wait_ge(s["pro_a"], 2)
            for m in range(4):
                last = product(sc_ps[0][:, 0, m * B:(m + 1) * B], lambda k: w_ada[:, k, m * P:(m + 1) * P],
                               lambda k: emb[:, k, :], 2)
            last.then_inc(s["pro_p"], 1)
            product(sc_ps[1][0:B, :, :].rearrange("p a n -> p (a n)"), lambda k: emb[:, k, :],
                    lambda k: w_ada[:, k, :], 2).then_inc(s["pro_p"], 1)
            pe.wait_ge(s["w_end"], 4 * DMA)
            for m in range(4):
                last = product(mid_ps[0][:, 0, m * B:(m + 1) * B], lambda k: w1c[:, m * P:(m + 1) * P],
                               lambda k: emb[:, 2, :], 1)
            last.then_inc(s["pro_p"], 1)
            pe.wait_ge(s["pro_a"], 6)
            for m in range(4):
                last = product(mid_ps[1][:, 0, m * B:(m + 1) * B], lambda k: w2c[:, k, m * P:(m + 1) * P],
                               lambda k: h1c[:, k, :], 4)
            last.then_inc(s["pro_p"], 1)
            pe.wait_ge(s["pro_a"], 10)
            for i, w in enumerate((wsc, wsh)):
                for m in range(2):
                    product(end_ps[:, 0, (2 * i + m) * B:(2 * i + m + 1) * B],
                            lambda k: w[:, k, m * P:(m + 1) * P], lambda k: h2c[:, k, :], 4).then_inc(s["pro_p"], 1)
            pe.wait_ge(s["w_id"], DMA)

            def scores(batch, h):
                at(pe, f"stack{h // HG}", batch)
                at(pe, "maxed", batch, 2 * h - 2)
                for t in range(ST):
                    last = pe.matmul(sc_ps[h % 2][:, t, :], q_stack[:, h, t * P:(t + 1) * P], k_stack[:, h, :],
                                     start=True, stop=True)
                last.then_inc(s["scored"], 1)

            def head(it, slot, att, pre):
                if att and slot < H - 1:
                    scores(it, slot + 1)
                if pre and slot == H - 1:
                    if isinstance(it, int) and it < 0:
                        pe.wait_ge(s["pro_v"], PRO_COLS)
                    scores(it + 1, 0)
                if att:
                    at(pe, "exped", it, 2 * slot + 2)
                    at(pe, "turned_sb", it, slot)
                    turn(pt_ps, probs[:, slot % 2], "turned")

            def pv(it, slot):
                at(pe, "turned_sb", it, slot + 1)
                if slot == 0:
                    at(pe, "v_done", it)
                    at(pe, "ctx_done", it - 1)
                g, j = divmod(slot, HG)
                for k in range(ST):
                    last = pe.matmul(ctx_ps[:, g, :], vpad[:, k, g, j * P:(j + 1) * P], probsT[:, slot % 2, k, :],
                                     start=(j == 0 and k == 0), stop=(j == HG - 1 and k == ST - 1))
                last.then_inc(s["pv_done"], 1)

            def trp(it):
                at(pe, "lnp", it + 1)
                at(pe, "l2", it - 2, 12)
                at(pe, "x1T_done", it)
                turn(end_ps, xn, "trp_pe")

            def project(w, name):
                for m in range(DT):
                    last = product(pre_ps[:, m, :], lambda k: w[:, k, m * P:(m + 1) * P], lambda k: x1T[:, k, :], DT)
                last.then_inc(s[name], 1)

            def q(it):
                if isinstance(it, int) and it < 0:
                    pe.wait_ge(s["w_qkv"], 4 * DMA)
                at(pe, "x1T_done", it + 1)
                at(pe, "v_done", it)
                project(wq, "q_pe")

            def k_(it):
                at(pe, "qkf_done", it + 1, 2)
                project(wk, "k_pe")

            def v(it):
                at(pe, "qkf_done", it + 1, 4)
                for t in range(ST):
                    last = product(pre_ps[:, t, :], lambda k: x1T[:, k, t * P:(t + 1) * P], lambda k: wv[:, k, :], DT)
                last.then_inc(s["v_pe"], 1)

            def rb(it):
                at(pe, "rinv_done", it - 1)
                at(pe, "lne", it - 2, 2)
                if isinstance(it, int) and it == 1:
                    pe.wait_ge(s["w_mid"], 12 * DMA)
                    pe.wait_ge(s["pro_v"], PRO_COLS2)
                for g in range(2):
                    for t in range(ST):
                        last = pe.matmul(mid_ps[0][:, g, t * P:(t + 1) * P],
                                         rinv_wide[:, t, g * P:(g + 1) * P], ident[:], start=True, stop=True)
                last.then_inc(s["rb_pe"], 1)

            def rows_product(dst, t, xT, w, kt):
                return product(dst[:, t, :], lambda k: xT[:, k, t * P:(t + 1) * P], lambda k: w[:, k, :], kt)

            def cols_product(dst, m, w, n, xT):
                return product(dst[:, m, :], lambda k: w[:, k, n * P:(n + 1) * P], lambda k: xT[:, k, :], DT)

            def wo_(it):
                at(pe, "ctx_done", it - 1)
                at(pe, "lne", it - 2, 2)
                for t in range(ST):
                    last = rows_product(mid_ps[1], t, ctxT, wo, DT)
                last.then_inc(s["wo_pe"], 1)

            def tr2(it):
                at(pe, "ln2", it - 1)
                at(pe, "rb_sb", it - 1)
                turn(mid_ps[0], x2n, "tr2_pe")

            def up_product(it, half, w, xT, done, count, bank_read):
                for c in range(2):
                    b = mid_ps[(c + 1) % 2]
                    if c == 0 and half == 0:
                        at(pe, *bank_read)
                    elif half == 1:
                        at(pe, done, it - 1, 2 * c + 2)
                    for j in range(2):
                        last = cols_product(b, j, w, 4 * half + 2 * c + j, xT)
                    last.then_inc(s[count], 1)

            def fa(it):
                at(pe, "h1T_done", it - 1)
                up_product(it, 0, w1, h1T, "ff1_done", "ff1_pe", ("ln2", it - 1, 1))

            def fb(it):
                up_product(it, 1, w1, h1T, "ff1_done", "ff1_pe", None)

            def ff2(it, t):
                at(pe, "ff1_done", it - 1)
                rows_product(mid_ps[1 - t], t, hT, w2, FT).then_inc(s["ff2_pe"], 1)

            def tr3(it):
                at(pe, "x3_done", it - 1)
                turn(mid_ps[0], x3, "tr3_pe")

            def ea(it):
                at(pe, "x3T_done", it - 1)
                at(pe, "wi_loaded", it - 1)
                up_product(it, 0, wi, x3T, "e1_done", "e1_pe", ("x3_done", it - 1))

            def eb(it):
                up_product(it, 1, wi, x3T, "e1_done", "e1_pe", None)

            def e2(it, t):
                at(pe, "e1_done", it - 1)
                at(pe, "woe_loaded", it - 1)
                rows_product(mid_ps[1 - t], t, hT, woe, FT).then_inc(s["e2_pe"], 1)

            def tr4(it):
                at(pe, "lne", it - 2)
                at(pe, "lnf", it - 3, 1)
                at(pe, "x1T_done", it)
                turn(end_ps, yn, "tr4_pe")

            def st(it, n):
                at(pe, "l2", it - 2, 3 + 8 * n)
                pe.matmul(end_ps[:, 0, 0:2], mean_w[:], g_mv[:], start=True, stop=True).then_inc(s["st_pe"], 1)

            def win(it):
                at(pe, "z_done", it - 2, 2)
                for m in range(DT):
                    last = cols_product(end_ps, m, w_in, m, z)
                last.then_inc(s["win_pe"], 1)

            def wout(it):
                at(pe, "z_done", it - 2, 4)
                at(pe, "x1T_done", it + 1)
                for m in range(DT):
                    last = cols_product(end_ps, m, w_out, m, z)
                last.then_inc(s["wout_pe"], 1)

            def down(it):
                at(pe, "l2", it - 2)
                product(end_ps[0:A3, 0, :], lambda k: down_w[:, k, :], lambda k: x5T[:, k, :], DT)\
                    .then_inc(s["down_pe"], 1)

            def exp_(it):
                at(pe, "hid_done", it - 2)
                at(pe, "sel_done", it - 2)
                settle(pe)
                product(end_ps[0:A3, 0, :], lambda k: wsel[:], lambda k: hid[:], 1).then_inc(s["exp_pe"], 1)

            def tr5(it):
                at(pe, "x5b_done", it - 2)
                at(pe, "dom_done", it - 2)
                turn(end_ps, x5b, "tr5_pe")

            def up(it):
                at(pe, "x5_done", it - 2)
                for t in range(ST):
                    last = product(end_ps[:, t, :], lambda k: dom[:, t * P:(t + 1) * P], lambda k: up_w[:], 1)
                last.then_inc(s["up_pe"], 1)

            stages = dict(trp=trp, q=q, k=k_, v=v, rb=rb, wo=wo_, tr2=tr2, fa=fa, fb=fb,
                          ff2a=lambda it: ff2(it, 0), ff2b=lambda it: ff2(it, 1), tr3=tr3, ea=ea, eb=eb,
                          e2a=lambda it: e2(it, 0), e2b=lambda it: e2(it, 1), tr4=tr4,
                          st1=lambda it: st(it, 0), st2=lambda it: st(it, 1), win=win, wout=wout, down=down,
                          exp=exp_, tr5=tr5, up=up)

            def finish(slot):
                return lambda it, phases: pv(it, slot) if "att" in phases else None

            drive(pe, head, stages, {slot: finish(slot) for slot in range(H)})

        @block.scalar
        def _(act):
            def line(dst, src, func, bias, scale, name):
                act.activation(dst, src, func, bias=bias, scale=scale).then_inc(s[name], 1)

            act.wait_ge(s["pro_v"], PRO_ANGLE)
            line(emb, red, ACT.Sin, 0.0, 1.0, "pro_a")
            act.wait_ge(s["pro_a"], 1)
            act.activation(emb[:, 0:2, :], emb[:, 0:2, :], ACT.Silu).then_inc(s["pro_a"], 1)
            act.wait_ge(s["pro_p"], 3)
            for m in range(4):
                line(h1c[:, m, :], mid_ps[0][:, 0, m * B:(m + 1) * B], ACT.Silu, cvec[:, 4 + m:5 + m], 1.0, "pro_a")
            act.wait_ge(s["pro_p"], 4)
            for m in range(4):
                line(h2c[:, m, :], mid_ps[1][:, 0, m * B:(m + 1) * B], ACT.Identity, cvec[:, 8 + m:9 + m], 1.0, "pro_a")
            act.wait_ge(s["w_vec"], DMA)

            def softmax(batch, h):
                if h == 0:
                    at(act, "rinv_done", batch - 1, 1)
                at(act, "turned", batch, h - 1)
                for t in range(ST):
                    at(act, "maxed", batch, 2 * h + t + 1)
                    act.activation(probs[:, h % 2, t, :], bias[:, h // 2 % RING, h % 2, t, :], ACT.Exp,
                                   bias=nmax[:, h % 2, t:t + 1], scale=-1.0,
                                   accum_out=rowsum[:, t, h:h + 1]).then_inc(s["exped"], 1)

            def head(it, slot, att, pre):
                if att and slot < H - 1:
                    softmax(it, slot + 1)
                if pre and slot == H - 1:
                    softmax(it + 1, 0)

            def modulate(dst, src, tile_, c0, name):
                for m in range(DT):
                    line(dst[:, m, :], src[:, m, :], ACT.Identity, tile_[:, c0 + DT + m:c0 + DT + m + 1],
                         tile_[:, c0 + m:c0 + m + 1], name)

            def trp(it):
                at(act, "trp_pe", it + 1)
                at(act, "cols_loaded", it + 1)
                at(act, "v_pe", it)
                modulate(x1T, end_ps, cols, 0, "x1T_done")

            def qk(it, n, pe_done, vec_bias, scale):
                at(act, pe_done, it + 1)
                at(act, "lo_done", it + n, 1 + (1 - n))
                for m in range(DT):
                    line(qkf[:, m, :], pre_ps[:, m, :], ACT.Identity, vec_bias[:, m:m + 1], scale, "qkf_done")

            def rb(it):
                at(act, "rb_pe", it - 1)
                at(act, "ctx_done", it - 2)
                act.activation(rinv_sb[:], mid_ps[0][:], ACT.Copy).then_inc(s["rb_sb"], 1)

            def tr2(it):
                at(act, "tr2_pe", it - 1)
                modulate(h1T, mid_ps[0], vec, VG2, "h1T_done")

            def hidden(it, half, func, bias_tile, b0, pe_name, name):
                for c in range(2):
                    at(act, pe_name, it - 1, 2 * half + c + 1)
                    for j in range(2):
                        f = 4 * half + 2 * c + j
                        line(hT[:, f, :], mid_ps[(c + 1) % 2][:, j, :], func, bias_tile[:, b0 + f:b0 + f + 1], 1.0, name)

            def tr3(it):
                at(act, "tr3_pe", it - 1)
                act.activation(x3T[:], mid_ps[0][:], ACT.Copy).then_inc(s["x3T_done"], 1)

            def ea(it):
                at(act, "ep_loaded", it - 1)
                hidden(it, 0, ACT.Gelu, ep, 0, "e1_pe", "e1_done")

            def tr4(it):
                at(act, "tr4_pe", it - 2)
                modulate(x4T, end_ps, ep, FT, "x4T_done")

            def silu(it, n):
                at(act, "l2", it - 2, 8 + 8 * n)
                at(act, "cols2_loaded", it - 2)
                for m in range(DT):
                    line(z[:, m, :], u[:, m, :], ACT.Silu, cols2[:, DT + m:DT + m + 1], cols2[:, m:m + 1], "z_done")

            def win(it):
                at(act, "win_pe", it - 2)
                for m in range(DT):
                    line(y[:, m, :], end_ps[:, m, :], ACT.Identity, vec[:, VBIN + m:VBIN + m + 1], 1.0, "y_done")

            def down(it):
                at(act, "down_pe", it - 2)
                line(hid[:], end_ps[0:A3, 0, :], ACT.Gelu, vec[0:A3, VDNB:VDNB + 1], 1.0, "hid_done")

            def exp_(it):
                at(act, "exp_pe", it - 2)
                line(dom[:], end_ps[0:A3, 0, :], ACT.Identity, sel[:, 3:4], 1.0, "dom_done")

            def tr5(it):
                at(act, "tr5_pe", it - 2)
                act.activation(x5[:], end_ps[:], ACT.Copy).then_inc(s["x5_done"], 1)

            stages = dict(
                trp=trp, q=lambda it: qk(it, 0, "q_pe", qkb[:], 0.25),
                k=lambda it: qk(it, 1, "k_pe", vec[:, VK:VK + 2], 1.0),
                rb=rb, tr2=tr2,
                fa=lambda it: hidden(it, 0, ACT.Gelu_apprx_sigmoid, vec, VB1, "ff1_pe", "ff1_done"),
                fb=lambda it: hidden(it, 1, ACT.Gelu_apprx_sigmoid, vec, VB1, "ff1_pe", "ff1_done"),
                tr3=tr3, ea=ea, eb=lambda it: hidden(it, 1, ACT.Gelu, ep, 0, "e1_pe", "e1_done"),
                tr4=tr4, u1=lambda it: silu(it, 0), u2=lambda it: silu(it, 1), win=win, down=down, exp=exp_, tr5=tr5)
            drive(act, head, stages)

        @block.vector
        def _(dve):
            dve.memset(mean_w[:], 1.0 / P).then_inc(s["consts_v"], 1)
            dve.memset(vpad[:, 0], 0.0).then_inc(s["consts_v"], 1)
            dve.memset(vpad[:, 1], 0.0).then_inc(s["consts_v"], 1)
            pro = [0]

            def step(ins):
                pro[0] += 1
                ins.then_inc(s["pro_v"], 1)
                dve.wait_ge(s["pro_v"], pro[0])

            dve.wait_ge(s["w_cond"], 6 * DMA)
            step(dve.tensor_copy(t_f[:, 0, :], t_i))
            step(dve.tensor_scalar(ang[:, 0, :], t_f[:, 0, :], 40.0, None, ALU.mult))
            step(dve.tensor_scalar(ang[:, 1, :], t_f[:, 0, :], 40.0, None, ALU.mult))
            step(dve.tensor_scalar(ang[:, 2, :], t_f[:, 1, :], 5000.0, None, ALU.mult))
            wide = [P, 3, B]
            step(dve.tensor_tensor(ang, ang, fq[:, 0:3].unsqueeze(2).to_broadcast(wide), ALU.mult))
            step(dve.scalar_tensor_tensor(out=kk, in0=ang, scalar=1.0 / TWO_PI,
                                          in1=fq[:, 3:6].unsqueeze(2).to_broadcast(wide), op0=ALU.mult, op1=ALU.add))
            step(dve.tensor_scalar(kk, kk, ROUND, None, ALU.add))
            step(dve.tensor_scalar(kk, kk, ROUND, None, ALU.subtract))
            step(dve.scalar_tensor_tensor(out=red, in0=kk, scalar=-PI_1, in1=ang, op0=ALU.mult, op1=ALU.add))
            step(dve.scalar_tensor_tensor(out=red, in0=kk, scalar=-PI_2, in1=red, op0=ALU.mult, op1=ALU.add))
            step(dve.scalar_tensor_tensor(out=red, in0=kk, scalar=-PI_3, in1=red, op0=ALU.mult, op1=ALU.add))
            step(dve.tensor_scalar(ph2, fq[:, 3:6], TWO_PI, None, ALU.mult))
            step(dve.tensor_tensor(red, red, ph2.unsqueeze(2).to_broadcast(wide), ALU.add))
            step(dve.tensor_scalar(red, red, -PI_LIMIT, PI_LIMIT, ALU.max, ALU.min))
            assert pro[0] == PRO_ANGLE
            step(dve.tensor_scalar(ids_ok[:, 0:B], ids[:, 0:B], 0, NE1 - 1, ALU.max, ALU.min))
            step(dve.tensor_scalar(ids_ok[:, B:], ids[:, B:], 0, NE3 - 1, ALU.max, ALU.min))
            dve.wait_ge(s["w_vec"], DMA)
            step(dve.tensor_scalar(qkb[:], vec[:, VQ:VQ + 2], 0.25, None, ALU.mult))
            dve.wait_ge(s["pro_p"], 1)
            for m in range(4):
                step(dve.tensor_scalar(cond_cols[:, :, m], sc_ps[0][:, 0, m * B:(m + 1) * B], cvec[:, m:m + 1],
                                       1.0 if m < 2 else 0.0, ALU.add, ALU.add))
            assert pro[0] == PRO_COLS
            dve.wait_ge(s["pro_p"], 2)
            dve.wait_ge(s["w_cond2"], 3 * DMA)
            step(dve.memset(ada_c[:, 0:D], 1.0))
            step(dve.tensor_tensor(emb_rows, sc_ps[1][0:B, :, :].rearrange("p a n -> p (a n)"), ada_b, ALU.add))
            step(dve.tensor_tensor(emb_rows, emb_rows, ada_c, ALU.add))
            assert pro[0] == PRO_ROWS
            dve.wait_ge(s["pro_p"], PRO_PE_ALL)
            for m in range(4):
                step(dve.tensor_scalar(cond2_cols[:, :, m], end_ps[:, 0, m * B:(m + 1) * B],
                                       cvec[:, 12 + m:13 + m], None, ALU.add))
            assert pro[0] == PRO_COLS2
            dve.wait_ge(s["consts_v"], 3)

            def maxima(batch, h):
                at(dve, "scored", batch, h + 1)
                at(dve, "masked", batch, h + 1)
                at(dve, "exped", batch, 2 * h - 2)
                settle(dve)
                for t in range(ST):
                    b = bias[:, h // 2 % RING, h % 2, t, :]
                    dve.tensor_tensor_reduce(b, sc_ps[h % 2][:, t, :], b, -1.0, BIG, ALU.add, ALU.min,
                                             nmax[:, h % 2, t:t + 1]).then_inc(s["maxed"], 1)

            def head(it, slot, att, pre):
                if att and slot == H - 1:
                    at(dve, "exped", it)
                    at(dve, "rb_pe", it - 1)
                    dve.reciprocal(rinv[:], rowsum[:]).then_inc(s["rinv_done"], 1)
                    at(dve, "rinv_done", it, 1)
                    dve.tensor_copy(rinv_wide[:].rearrange("p t (h d) -> p (t h) d", d=HD),
                                    rinv[:].rearrange("p t h -> p (t h)").unsqueeze(2)
                                    .to_broadcast([P, ST * H, HD])).then_inc(s["rinv_done"], 1)
                if att and slot < H - 1:
                    maxima(it, slot + 1)
                if pre and slot == H - 1:
                    maxima(it + 1, 0)
                if att:
                    at(dve, "turned", it, slot + 1)
                    at(dve, "pv_done", it, slot - 1)
                    dve.tensor_copy(probsT[:, slot % 2], pt_ps[:]).then_inc(s["turned_sb"], 1)

            def norm_steps(it_batch, src, tiles, name, k, eps, rsq, dst, free=None):
                bn, mv, ve, rs = tiles
                for t in range(ST):
                    at(dve, name, it_batch, k - (1 if ST > 1 and t == 0 else 0)) if False else None
                    dve.bn_stats(bn[:, t, :], src[:, t, :]).then_inc(s[name], 1)
                for t in range(ST):
                    at(dve, name, it_batch, k + t + 1)
                    settle(dve)
                    dve.bn_aggr(mv[:, t, :], bn[:, t, :]).then_inc(s[name], 1)
                at(dve, name, it_batch, k + 4)
                dve.tensor_scalar(ve[:], mv[:, :, 1], eps, None, ALU.add).then_inc(s[name], 1)
                at(dve, rsq, it_batch)
                if free:
                    at(dve, *free)
                for t in range(ST):
                    dve.tensor_scalar(dst[:, t, :], src[:, t, :], mv[:, t, 0:1], rs[:, t:t + 1],
                                      ALU.subtract, ALU.mult).then_inc(s[name], 1)

            def lnp(it):
                at(dve, "x_loaded", it + 1)
                at(dve, "rsq_p", it)
                at(dve, "trp_pe", it)
                norm_steps(it + 1, x_in, stat_p, "lnp", 0, 1e-5, "rsq_p", xn, ("resid_done", it))

            def hi(it, n, dst):
                at(dve, "qkf_done", it + 1, 2 * n + 2)
                if n == 0:
                    at(dve, "stack0", it)
                    at(dve, "stack1", it)
                dve.tensor_copy(dst[:], qkf[:]).then_inc(s["hi_done"], 1)

            def vpad_(it):
                if isinstance(it, int) and it == 0:
                    dve.wait_ge(s["w_qkv"], 4 * DMA)
                at(dve, "v_pe", it)
                at(dve, "pv_done", it - 1)
                for k in range(ST):
                    for g in range(2):
                        cut = slice(g * P, (g + 1) * P)
                        dst = vpad[:, k, g, :].rearrange("p (h x) -> p h x", x=P + HD)[:, :, 0:HD]
                        dve.tensor_tensor(dst, pre_ps[:, k, cut].rearrange("p (h d) -> p h d", d=HD),
                                          bv_row[:, cut].rearrange("p (h d) -> p h d", d=HD), ALU.add)\
                            .then_inc(s["v_done"], 1)

            def rb(it):
                at(dve, "rb_sb", it - 1)
                at(dve, "pv_done", it - 1)
                at(dve, "wo_pe", it - 2)
                dve.tensor_tensor(ctxT[:], ctx_ps[:], rinv_sb[:], ALU.mult).then_inc(s["ctx_done"], 1)

            def wo_(it):
                at(dve, "wo_pe", it - 1)
                at(dve, "resid_done", it - 1)
                at(dve, "x2b_done", it - 2)
                dve.tensor_tensor(x2[:], mid_ps[1][:], resid[:], ALU.add).then_inc(s["ln2"], 1)
                at(dve, "ln2", it - 1, 1)
                norm_steps(it - 1, x2, stat_2, "ln2", 1, 1e-5, "rsq_2", x2n)

            def ff2(it, t):
                at(dve, "ff2_pe", it - 1, t + 1)
                at(dve, "x2b_done", it - 1, t + 1)
                at(dve, "x3b_done", it - 2)
                dve.tensor_tensor(x3[:, t, :], mid_ps[1 - t][:, t, :], x2b[:, t, :], ALU.add).then_inc(s["x3_done"], 1)

            def e2(it, t):
                at(dve, "e2_pe", it - 1, t + 1)
                at(dve, "x3b_done", it - 1, t + 1)
                dve.tensor_tensor(x4[:, t, :], mid_ps[1 - t][:, t, :], x3b[:, t, :], ALU.add).then_inc(s["lne"], 1)
                if t == 1:
                    at(dve, "lne", it - 1, 2)
                    norm_steps(it - 1, x4, stat_e, "lne", 2, 1e-12, "rsq_e", yn)

            def matrix_stats(it, n, src, ready):
                at(dve, *ready)
                k = 8 * n
                at(dve, "st_pe", it - 2 - (1 - n), 1 if n else 2)
                dve.bn_stats(g_bn[:], src[:].rearrange("p a n -> p (a n)")).then_inc(s["l2"], 1)
                at(dve, "l2", it - 2, k + 1)
                settle(dve)
                dve.bn_aggr(g_mv[:], g_bn[:]).then_inc(s["l2"], 1)
                at(dve, "l2", it - 2, k + 2)
                dve.scalar_tensor_tensor(out=g_mv[:, 1:2], in0=g_mv[:, 0:1], scalar=g_mv[:, 0:1], in1=g_mv[:, 1:2],
                                         op0=ALU.mult, op1=ALU.add).then_inc(s["l2"], 1)

            def matrix_norm(it, n, src):
                k = 8 * n
                at(dve, "st_pe", it - 2, n + 1)
                dve.tensor_copy(g_all[:], end_ps[:, 0, 0:2]).then_inc(s["l2"], 1)
                at(dve, "l2", it - 2, k + 4)
                dve.scalar_tensor_tensor(out=g_ve[:, 0:1], in0=g_all[:, 0:1], scalar=g_all[:, 0:1],
                                         in1=g_all[:, 1:2], op0=ALU.mult, op1=ALU.subtract).then_inc(s["l2"], 1)
                at(dve, "l2", it - 2, k + 5)
                dve.tensor_scalar(g_ve[:, 1:2], g_ve[:, 0:1], -1.0, 1e-5, ALU.mult, ALU.add).then_inc(s["l2"], 1)
                at(dve, "z_done", it - 2, 2 * n)
                dve.scalar_tensor_tensor(out=u[:], in0=src[:], scalar=g_all[:, 0:1], in1=gam2[:],
                                         op0=ALU.subtract, op1=ALU.mult).then_inc(s["l2"], 1)
                at(dve, "l2", it - 2, k + 7)
                at(dve, "rsq_g", it - 2, n + 1)
                dve.scalar_tensor_tensor(out=u[:], in0=u[:], scalar=g_rs[:, 0:1], in1=bet2[:],
                                         op0=ALU.mult, op1=ALU.add).then_inc(s["l2"], 1)

            def wout(it):
                at(dve, "wout_pe", it - 2)
                at(dve, "x5b_done", it - 3)
                for m in range(DT):
                    dve.scalar_tensor_tensor(out=x5T[:, m, :], in0=end_ps[:, m, :],
                                             scalar=vec[:, VBOUT + m:VBOUT + m + 1], in1=x4T[:, m, :],
                                             op0=ALU.add, op1=ALU.add).then_inc(s["l2"], 1)

            def select(it):
                at(dve, "l3_loaded", it - 2)
                at(dve, "id_loaded", it - 2)
                b = it - 2
                dve.tensor_scalar(sel[:, 0:1], idcol[:], 0.0, None, ALU.is_ge).then_inc(s["sel_done"], 1)
                at(dve, "sel_done", b, 1)
                dve.scalar_tensor_tensor(out=sel[:, 1:2], in0=idcol[:], scalar=float(NE3), in1=sel[:, 0:1],
                                         op0=ALU.is_lt, op1=ALU.mult).then_inc(s["sel_done"], 1)
                at(dve, "sel_done", b, 2)
                dve.tensor_scalar(sel[:, 2:3], sel[:, 1:2], -1.0, 1.0, ALU.mult, ALU.add).then_inc(s["sel_done"], 1)
                at(dve, "sel_done", b, 3)
                dve.tensor_scalar(wsel[:], ident[0:A3, 0:A3], sel[:, 2:3], None, ALU.mult).then_inc(s["sel_done"], 1)
                at(dve, "sel_done", b, 4)
                dve.scalar_tensor_tensor(out=wsel[:], in0=l3[:, 0:A3], scalar=sel[:, 1:2], in1=wsel[:],
                                         op0=ALU.mult, op1=ALU.add).then_inc(s["sel_done"], 1)
                dve.scalar_tensor_tensor(out=sel[:, 3:4], in0=l3[:, A3:A3 + 1], scalar=sel[:, 1:2],
                                         in1=l3[:, A3 + 1:A3 + 2], op0=ALU.mult, op1=ALU.add)\
                    .then_inc(s["sel_done"], 1)

            def up(it):
                at(dve, "up_pe", it - 2)
                at(dve, "x5_done", it - 2)
                at(dve, "out_stored", it - 3)
                dve.tensor_tensor(x6[:], end_ps[:], x5[:], ALU.add).then_inc(s["lnf"], 1)
                at(dve, "lnf", it - 2, 1)
                norm_steps(it - 2, x6, stat_f, "lnf", 1, 1e-5, "rsq_f", x6)

            stages = dict(
                lnp=lnp, q=lambda it: hi(it, 0, q_hi), k=lambda it: hi(it, 1, k_hi), vpad=vpad_, rb=rb, wo=wo_,
                ff2a=lambda it: ff2(it, 0), ff2b=lambda it: ff2(it, 1),
                e2a=lambda it: e2(it, 0), e2b=lambda it: e2(it, 1),
                st1=lambda it: matrix_stats(it, 0, x4T, ("x4T_done", it - 2)), u1=lambda it: matrix_norm(it, 0, x4T),
                st2=lambda it: matrix_stats(it, 1, y, ("y_done", it - 2)), u2=lambda it: matrix_norm(it, 1, y),
                wout=wout, down=select, up=up)
            drive(dve, head, stages)

        @block.gpsimd
        def _(pool):
            pool.memset(neg_half[:], -0.5).then_inc(s["consts_p"], 1)
            pool.wait_ge(s["consts_p"], 1)

            def negate(batch):
                at(pool, "mask_loaded", batch)
                at(pool, "masked", batch - 1)
                settle(pool)
                pool.tensor_scalar(mask_add[:], mask_in[:], MASKED, None, ALU.mult).then_inc(s["negated"], 1)

            def add_mask(batch, h):
                pair = h // 2
                at(pool, "negated", batch)
                need(pool, s_bias[pair % RING], batch * 2 * DMA + DMA * (pair // RING + 1))
                b = bias[:, pair % RING, h % 2]
                pool.tensor_tensor(b, b, mask_add[:], ALU.add).then_inc(s["masked"], 1)

            def head(it, slot, att, pre):
                ahead = slot + 3
                if ahead < H:
                    if att:
                        add_mask(it, ahead)
                elif pre:
                    if ahead == H:
                        negate(it + 1)
                    add_mask(it + 1, ahead - H)

            def inv_sqrt(batch, name, k, rsq, ve, rs):
                at(pool, name, batch, k)
                pool.tensor_tensor(rs, ve, neg_half[:, 0:ve.shape[1]], ALU.pow).then_inc(s[rsq], 1)

            def lo(it, n, dst, hi):
                at(pool, "hi_done", it + 1, n + 1)
                pool.tensor_tensor(dst[:], qkf[:], hi[:].bitcast(F32), ALU.subtract).then_inc(s["lo_done"], 1)

            def resid_(it):
                at(pool, "rows_loaded", it)
                at(pool, "lnp", it)
                at(pool, "ln2", it - 1, 1)
                for t in range(ST):
                    pool.tensor_tensor(resid[:, t, :], xn[:, t, :], rows[:, 0:D], ALU.mult)\
                        .then_inc(s["resid_done"], 1)
                for t in range(ST):
                    at(pool, "resid_done", it, t + 1)
                    pool.tensor_tensor(resid[:, t, :], resid[:, t, :], rows[:, D:], ALU.add)\
                        .then_inc(s["resid_done"], 1)

            def add_row(batch, dst, src, row, name):
                for t in range(ST):
                    pool.tensor_tensor(dst[:, t, :], src[:, t, :], row[:], ALU.add).then_inc(s[name], 1)

            def wo_(it):
                inv_sqrt(it - 1, "ln2", 6, "rsq_2", stat_2[2][:], stat_2[3][:])
                at(pool, "x3_done", it - 2)
                add_row(it - 1, x2b, x2, b2_row, "x2b_done")

            def ff2b(it):
                at(pool, "x3_done", it - 1)
                at(pool, "bo_loaded", it - 1)
                at(pool, "lne", it - 2, 2)
                add_row(it - 1, x3b, x3, bo_row, "x3b_done")

            def wout(it):
                at(pool, "l2", it - 2)
                at(pool, "tr5_pe", it - 3)
                settle(pool)
                for m in range(DT):
                    pool.tensor_scalar(x5b[:, m, :], x5T[:, m, :], vec[:, VUPB + m:VUPB + m + 1], None, ALU.add)\
                        .then_inc(s["x5b_done"], 1)

            def up(it):
                inv_sqrt(it - 2, "lnf", 6, "rsq_f", stat_f[2][:], stat_f[3][:])
                for t in range(ST):
                    at(pool, "lnf", it - 2, 7 + t)
                    pool.tensor_tensor(x6[:, t, :], x6[:, t, :], lng_row[:], ALU.mult).then_inc(s["fin"], 1)
                for t in range(ST):
                    at(pool, "fin", it - 2, t + 1)
                    pool.tensor_tensor(x6[:, t, :], x6[:, t, :], lnb_row[:], ALU.add).then_inc(s["fin"], 1)

            stages = dict(
                lnp=lambda it: inv_sqrt(it + 1, "lnp", 5, "rsq_p", stat_p[2][:], stat_p[3][:]),
                q=lambda it: lo(it, 0, q_lo, q_hi), k=lambda it: lo(it, 1, k_lo, k_hi), resid=resid_,
                wo=wo_, ff2b=ff2b,
                e2b=lambda it: inv_sqrt(it - 1, "lne", 7, "rsq_e", stat_e[2][:], stat_e[3][:]),
                u1=lambda it: inv_sqrt(it - 2, "l2", 6, "rsq_g", g_ve[:, 1:2], g_rs[:]),
                u2=lambda it: inv_sqrt(it - 2, "l2", 14, "rsq_g", g_ve[:, 1:2], g_rs[:]),
                wout=wout, up=up)
            drive(pool, head, stages)


PRO_PE_ALL = 8
PRO_ANGLE = 14
PRO_COLS = PRO_ANGLE + 3 + 4
PRO_ROWS = PRO_COLS + 3
PRO_COLS2 = PRO_ROWS + 4


def kernel(**inputs):
    import concourse.bacc as bacc
    from concourse.bass_utils import run_bass_kernel_spmd

    g = {k: np.asarray(v) for k, v in inputs.items()}

    def columns(v):
        return v.reshape(-1, P).T

    def head_order(w):
        return w.reshape(w.shape[:-1] + (DT, HG, HD)).swapaxes(-1, -2).reshape(w.shape)

    half0, half2 = D // 2, 64
    freq0 = np.exp(np.arange(half0, dtype=np.float32) * np.float32(-math.log(10000.0) / (half0 - 1)))
    freq2 = np.exp(np.arange(half2, dtype=np.float32) * np.float32(-math.log(10000.0) / (half2 - 1)))
    freqs = np.zeros((P, 6), np.float32)
    freqs[:, 0] = freqs[:, 1] = freq0
    freqs[:, 2] = np.concatenate([freq2, freq2])
    freqs[:, 4] = 0.25
    freqs[half2:, 5] = 0.25
    L0, L1, L2, L3 = (f"L{i}_cond_" for i in range(4))
    down_b = np.zeros((P, 1), np.float32)
    down_b[:A3, 0] = g[L3 + "down_b"]
    vec = np.concatenate([columns(head_order(g[L0 + "bq"])), columns(head_order(g[L0 + "bk"])),
                          columns(g[L0 + "g2"]), columns(g[L0 + "beta2"]), columns(g[L0 + "b1"]),
                          columns(g[L2 + "b_in"]), columns(g[L2 + "b_out"]), columns(g[L3 + "up_b"]), down_b,
                          np.zeros((P, 4), np.float32)], axis=1)
    cvec = np.concatenate([columns(g[L0 + "b_ada"]), columns(g[L2 + "b1"]), columns(g[L2 + "b2"]),
                           columns(g[L2 + "bsc"]), columns(g[L2 + "bsh"])], axis=1)
    ep = np.concatenate([g[L1 + n].reshape(NE1, -1, P).transpose(0, 2, 1) for n in ("bi", "gamma", "beta")], axis=2)
    l3 = np.concatenate([g[L3 + "expert_W"].transpose(0, 2, 1), g[L3 + "expert_b"][:, :, None],
                         g[L3 + "domain_emb"][:, :, None]], axis=2)
    data = {
        "x": g["x"], "fside": g["fside_Bx16xSxS_0"], "mask": g["mask_Bx1xSxS_bk0"],
        "timestep": g["itok_B_34_63"], "id1": g["itok_B_0_7"], "id3": g["itok_B_0_15"], "t2": g["condB_t"],
        "freqs": freqs, "ident": np.eye(P, dtype=np.float32), "vec": vec, "cvec": cvec,
        "W_ada": g[L0 + "W_ada"], "b_ada": g[L0 + "b_ada"], "bo": g[L0 + "bo"],
        "Wq": head_order(g[L0 + "Wq"]), "Wk": head_order(g[L0 + "Wk"]), "Wv": g[L0 + "Wv"], "bv": g[L0 + "bv"],
        "Wo": g[L0 + "Wo"], "W1": g[L0 + "W1"], "W2": g[L0 + "W2"], "b2": g[L0 + "b2"],
        "Wi": g[L1 + "Wi"], "Woe": g[L1 + "Wo"], "boe": g[L1 + "bo"], "ep": ep,
        "W1c": g[L2 + "W1"], "W2c": g[L2 + "W2"], "Wsc": g[L2 + "Wsc"], "Wsh": g[L2 + "Wsh"],
        "W_in": g[L2 + "W_in"], "W_out": g[L2 + "W_out"], "gamT": g[L2 + "gamma"].T, "betT": g[L2 + "beta"].T,
        "down_wT": g[L3 + "down_W"].T, "up_wT": g[L3 + "up_W"].T, "l3": l3,
        "ln_g": g[L3 + "ln_gamma"], "ln_b": g[L3 + "ln_beta"],
    }
    nc = bacc.Bacc("TRN2", target_bir_lowering=False, num_devices=1)
    arrays, args = {}, {}
    for name, value in data.items():
        value = np.ascontiguousarray(value)
        arrays[f"in_{name}"] = value
        args[name] = nc.dram_tensor(f"in_{name}", value.shape, mybir.dt.from_np(value.dtype), kind="ExternalInput").ap()
    args["out"] = nc.dram_tensor("out_0", (B, S, D), F32, kind="ExternalOutput").ap()
    build(nc, args)
    result = run_bass_kernel_spmd(nc, [arrays], core_ids=[0])
    return result.results[0]["out_0"]
```

```python
from contextlib import ExitStack
import math

import numpy as np

import concourse.bass as bass
from concourse import mybir

F32 = mybir.dt.float32
F32R = mybir.dt.float32r
I32 = mybir.dt.int32
U8 = mybir.dt.uint8
ALU = mybir.AluOpType
ACT = mybir.ActivationFunctionType

B, S, D = 16, 256, 256
H, HD = 16, 16
F = 1024
P = 128
ST = S // P
DT = D // P
FT = F // P
HG = 8
NE1, NE3, A3 = 8, 16, 64
BIG = 3.0e38
MASKED = -1.0e30
DMA = 16
RING = 4
QUADS = 4

SCHEDULE = {
    0: ["vpad", "rb", "h1"],
    1: ["wo"],
    2: ["resid", "lnp", "h2"],
    3: ["n2", "h3", "tr2", "np"],
    4: ["f0", "trp", "ne", "f1"],
    5: ["q", "tr4", "f2"],
    6: ["s1", "k", "f3", "st1"],
    7: ["u1", "g0", "g1"],
    8: ["g2", "win"],
    9: ["s2", "g3", "st2"],
    10: ["u2", "v", "tr3"],
    11: ["e0", "wout"],
    12: ["down", "e1"],
    13: ["e2", "exp"],
    14: ["tr5", "e3", "up"],
    15: ["nf", "h0"],
}
PHASE = {
    "pre": ["lnp", "np", "trp", "q", "k", "v"],
    "att": ["vpad", "resid"],
    "mid": ["rb", "wo", "n2", "tr2", "f0", "f1", "f2", "f3", "g0", "g1", "g2", "g3", "tr3",
            "e0", "e1", "e2", "e3", "h0"],
    "end": ["h1", "h2", "h3", "ne", "tr4", "s1", "st1", "u1", "win", "s2", "st2", "u2", "wout", "down", "exp", "tr5", "up", "nf"],
}
PHASE_OF = {stage: phase for phase, stages in PHASE.items() for stage in stages}

TWO_PI = 2.0 * math.pi
PI_1 = 6.28125
PI_2 = 0.001934051513671875
PI_3 = TWO_PI - PI_1 - PI_2
ROUND = 1.5 * 2.0 ** 23
PI_LIMIT = 3.1415925


def place(h):
    g, r = divmod(h, HG)
    half, quad = divmod(r, QUADS)
    return g, quad, half


def need(eng, sem, value):
    if isinstance(value, int) and value <= 0:
        return
    eng.wait_ge(sem, value)


def build(nc, a):
    with ExitStack() as ctx:
        def sb(name, shape, dt=F32):
            return ctx.enter_context(nc.sbuf_tensor(name, shape, dt))

        def bank(name, shape):
            return ctx.enter_context(nc.psum_tensor(name, shape, F32))

        def sem(name):
            return ctx.enter_context(nc.semaphore(name))

        ident = sb("ident", [P, P])
        mean_w = sb("mean_w", [P, P])
        neg_half = sb("neg_half", [P, 2])
        wq, wk, wv, wo = (sb(n, [P, DT, D]) for n in ("wq", "wk", "wv", "wo"))
        w1 = sb("w1", [P, DT, F])
        w2 = sb("w2", [P, FT, D])
        wi = sb("wi", [P, DT, F])
        woe = sb("woe", [P, FT, D])
        w_in, w_out = sb("w_in", [P, DT, D]), sb("w_out", [P, DT, D])
        gam2, bet2 = sb("gam2", [P, DT, S]), sb("bet2", [P, DT, S])
        down_w = sb("down_w", [P, DT, A3])
        up_w = sb("up_w", [A3, D])
        vec = sb("vec", [P, 27])
        VQ, VK, VG2, VBE2, VB1, VBIN, VBOUT, VUPB, VDNB = 0, 2, 4, 6, 8, 16, 18, 20, 22
        qkb = sb("qkb", [P, 2])
        bv_row, b2_row = sb("bv_row", [P, D]), sb("b2_row", [P, D])
        lng_row, lnb_row = sb("lng_row", [P, D]), sb("lnb_row", [P, D])

        x_in = sb("x_in", [P, ST, D])
        xn = sb("xn", [P, ST, D])
        cond_cols = sb("cond_cols", [P, B, 4])
        cond2_cols = sb("cond2_cols", [P, B, 4])
        cols = sb("cols", [P, 4])
        rows = sb("rows", [P, 2 * D])
        x1T = sb("x1T", [P, DT, S])
        qkf = sb("qkf", [P, DT, S])
        q_hi, q_lo, k_hi, k_lo = (sb(n, [P, DT, S], F32R) for n in ("q_hi", "q_lo", "k_hi", "k_lo"))
        q_stack = sb("q_stack", [4 * HD, H, S], F32R)
        k_stack = sb("k_stack", [4 * HD, H, S], F32R)
        vpad = sb("vpad", [P, ST, H, 2 * HD])
        bias = sb("bias", [P, RING, 2, ST, S])
        mask_in = sb("mask_in", [P, ST, S], U8)
        mask_add = sb("mask_add", [P, ST, S])
        nmax = sb("nmax", [P, 2, ST])
        probs = sb("probs", [P, 2, ST, S])
        probsT = sb("probsT", [P, 2 * QUADS, ST, S])
        rowsum = sb("rowsum", [P, ST, H])
        rinv = sb("rinv", [P, ST, H])
        rinv_wide = sb("rinv_wide", [P, ST, D])
        rinv_sb = sb("rinv_sb", [P, 2, S])
        ctxT = sb("ctxT", [P, DT, S])
        resid = sb("resid", [P, ST, D])
        x2 = sb("x2", [P, ST, D])
        x2n = sb("x2n", [P, ST, D])
        x2b = sb("x2b", [P, ST, D])
        h1T = sb("h1T", [P, DT, S])
        hT = sb("hT", [P, FT, S])
        x3 = sb("x3", [P, ST, D])
        x3b = sb("x3b", [P, ST, D])
        x3T = sb("x3T", [P, DT, S])
        bo_row = sb("bo_row", [P, D])
        ep = sb("ep", [P, FT + 4])
        x4 = sb("x4", [P, ST, D])
        yn = sb("yn", [P, ST, D])
        x4T = sb("x4T", [P, DT, S])
        cols2 = sb("cols2", [P, 4])
        u = sb("u", [P, DT, S])
        z = sb("z", [P, DT, S])
        y = sb("y", [P, DT, S])
        x5T = sb("x5T", [P, DT, S])
        x5b = sb("x5b", [P, DT, S])
        x5 = sb("x5", [P, ST, D])
        x6 = sb("x6", [P, ST, D])
        hid = sb("hid", [A3, S])
        dom = sb("dom", [A3, S])
        l3 = sb("l3", [A3, A3 + 2])
        idcol = sb("idcol", [A3, 1], I32)
        sel = sb("sel", [A3, 4])
        wsel = sb("wsel", [A3, A3])
        ids = sb("ids", [1, 2 * B], I32)
        ids_ok = sb("ids_ok", [1, 2 * B], I32)

        def stat_tiles(n):
            return (sb(f"bn{n}", [P, ST, 6]), sb(f"mv{n}", [P, ST, 2]), sb(f"ve{n}", [P, ST]), sb(f"rs{n}", [P, ST]))

        stat_p, stat_2, stat_e, stat_f = (stat_tiles(n) for n in "p2ef")
        g_bn, g_mv, g_all, g_ve, g_rs = (sb(n, [P, k]) for n, k in
                                         (("g_bn", 6), ("g_mv", 2), ("g_all", 2), ("g_ve", 2), ("g_rs", 1)))

        w_ada = hT[:, 0:4, :].rearrange("p (k a) n -> p k (a n)", k=2)
        w1c = hT[:, 4:6, :].rearrange("p a n -> p (a n)")
        w2c = woe[:, :, :].rearrange("p (k a) n -> p k (a n)", k=4)
        wsc = wi[:, 0, :].rearrange("p (k n) -> p k n", k=4)
        wsh = wi[:, 1, :].rearrange("p (k n) -> p k n", k=4)
        ang = u[:, 0, 0:48].rearrange("p (t b) -> p t b", t=3)
        red = u[:, 0, 48:96].rearrange("p (t b) -> p t b", t=3)
        kk = u[:, 0, 96:144].rearrange("p (t b) -> p t b", t=3)
        emb = u[:, 0, 144:192].rearrange("p (t b) -> p t b", t=3)
        fq = u[:, 1, 0:6]
        ph2 = u[:, 1, 6:9]
        t_f = u[:, 1, 16:48].rearrange("p (t b) -> p t b", t=2)
        h1c = u[:, 1, 48:112].rearrange("p (m b) -> p m b", m=4)
        h2c = u[:, 1, 112:176].rearrange("p (m b) -> p m b", m=4)
        cvec = z[:, 0, 0:16]
        t_i = z[:, 0, 16:32].bitcast(I32)
        ada_b = y[0:B, :, :].rearrange("p a n -> p (a n)")
        ada_c = x5T[0:B, :, :].rearrange("p a n -> p (a n)")
        emb_rows = x5b[0:B, :, :].rearrange("p a n -> p (a n)")

        sc_ps = [bank(f"sc_ps{i}", [P, ST, S]) for i in range(2)]
        pt_ps = bank("pt_ps", [P, ST, S])
        ctx_ps = bank("ctx_ps", [P, 2, S])
        pre_ps = bank("pre_ps", [P, 2, S])
        mid_ps = [bank(f"mid_ps{i}", [P, 2, S]) for i in range(2)]
        end_ps = bank("end_ps", [P, 2, S])

        names = """settled w_cond w_cond2 w_vec w_qkv w_mid w_end w_id consts_v consts_p pro_v pro_a pro_p rows_out
        x_loaded cols_loaded rows_loaded mask_loaded wi_loaded woe_loaded ep_loaded bo_loaded cols2_loaded
        l3_loaded id_loaded out_stored stack0 stack1
        lnp rsq_p trp_pe x1T_done q_pe k_pe v_pe qkf_done hi_done lo_done v_done resid_done
        scored negated masked maxed exped turned turned_sb pv_done rinv_done
        rb_pe rb_sb ctx_done wo_pe ln2 rsq_2 x2b_done tr2_pe h1T_done ff1_pe ff1_done ff2_pe x3_done x3b_done
        tr3_pe x3T_done e1_pe e1_done e2_pe lne rsq_e
        tr4_pe x4T_done l2 st_pe rsq_g z_done win_pe y_done wout_pe x5b_done down_pe hid_done exp_pe dom_done
        sel_done tr5_pe x5_done up_pe lnf rsq_f fin""".split()
        s = {n: sem(n) for n in names}
        s_bias = [sem(f"bias_loaded{i}") for i in range(RING)]
        N = dict(lnp=7, rinv_done=2, x1T_done=2, qkf_done=4, hi_done=2, lo_done=2, v_done=4, resid_done=4,
                 scored=H, masked=H, maxed=2 * H, exped=2 * H, turned=H, turned_sb=H, pv_done=H,
                 ln2=8, x2b_done=2, h1T_done=2, ff1_pe=4, ff1_done=8, ff2_pe=2, x3_done=2, x3b_done=2,
                 e1_pe=4, e1_done=8, e2_pe=2, lne=9, x4T_done=2, l2=18, st_pe=2, rsq_g=2, z_done=4, y_done=2,
                 x5b_done=2, sel_done=6, lnf=8, fin=4)
        for n in ("x_loaded cols_loaded rows_loaded mask_loaded wi_loaded woe_loaded ep_loaded bo_loaded "
                  "cols2_loaded l3_loaded id_loaded out_stored").split():
            N[n] = DMA
        N["stack0"] = N["stack1"] = 8 * DMA

        def at(eng, name, batch, k=None):
            n = N.get(name, 1)
            k = n if k is None else k
            if isinstance(batch, int) and batch >= B:
                batch, k = B - 1, n
            need(eng, s[name], batch * n + k)
            if eng is nc.sync and not isinstance(batch, int):
                settle(eng)

        def settle(eng):
            eng.sem_inc(s["settled"], 1)

        x_v = a["x"].rearrange("b (t p) d -> b p t d", p=P)
        out_v = a["out"].rearrange("b (t p) d -> b p t d", p=P)
        f_v = a["fside"].rearrange("b h (t p) k -> b p h t k", p=P)
        mask_v = a["mask"].rearrange("b o (t p) k -> b p (o t) k", p=P)
        wi_v = a["Wi"].rearrange("e (k p) n -> e p k n", p=P)
        woe_v = a["Woe"].rearrange("e (k p) n -> e p k n", p=P)
        rows_d = nc.dram_tensor("rows_scratch", (B, 2 * D), F32, kind="Internal").ap()

        def k_tiles(w):
            return w.rearrange("(k p) n -> p k n", p=P)

        def drive(eng, head, stages, before=None):
            def iteration(it, phases):
                for slot in range(H):
                    head(it, slot, "att" in phases, "pre" in phases)
                    for stage in SCHEDULE[slot]:
                        if stage in stages and PHASE_OF[stage] in phases:
                            stages[stage](it)
                    if before and slot in before:
                        before[slot](it, phases)

            def active(it):
                on = {"pre": 0 <= it + 1 < B, "att": 0 <= it < B, "mid": 0 <= it - 1 < B, "end": 0 <= it - 2 < B}
                return [p for p, yes in on.items() if yes]

            for it in (-1, 0, 1, 2):
                iteration(it, active(it))
            with eng.Fori(3, B - 1) as it:
                iteration(it, active(3))
            for it in (B - 1, B, B + 1):
                iteration(it, active(it))

        block = ctx.enter_context(nc.Block())

        @block.sync
        def _(sp):
            def load(dst, src, name):
                sp.dma_start(dst, src).then_inc(s[name], DMA)

            load(fq, a["freqs"], "w_cond")
            load(t_i, a["timestep"].partition_broadcast(P), "w_cond")
            load(t_f[:, 1, :], a["t2"].partition_broadcast(P), "w_cond")
            load(cvec, a["cvec"], "w_cond")
            load(ident[:], a["ident"], "w_id")
            load(ids[:, 0:B], a["id1"].partition_broadcast(1), "w_cond")
            load(ids[:, B:], a["id3"].partition_broadcast(1), "w_cond")
            load(vec[:], a["vec"], "w_vec")
            load(w_ada, k_tiles(a["W_ada"]), "w_cond2")
            load(ada_b, a["b_ada"].partition_broadcast(B), "w_cond2")
            load(ada_c[:, D:], a["bo"].partition_broadcast(B), "w_cond2")
            load(mask_in[:], mask_v[0], "mask_loaded")
            load(wq[:], k_tiles(a["Wq"]), "w_qkv")
            load(wk[:], k_tiles(a["Wk"]), "w_qkv")
            load(wv[:], k_tiles(a["Wv"]), "w_qkv")
            load(bv_row[:], a["bv"].partition_broadcast(P), "w_qkv")
            for pair in range(RING):
                sp.dma_start(bias[:, pair], f_v[0][:, 2 * pair:2 * pair + 2]).then_inc(s_bias[pair], DMA)
            load(w1c, a["W1c"], "w_end")
            load(w2c, k_tiles(a["W2c"]), "w_end")
            load(wsc, k_tiles(a["Wsc"]), "w_end")
            load(wsh, k_tiles(a["Wsh"]), "w_end")
            load(wo[:], k_tiles(a["Wo"]), "w_mid")
            load(w1[:], k_tiles(a["W1"]), "w_mid")
            load(w2[:], k_tiles(a["W2"]), "w_mid")
            load(b2_row[:], a["b2"].partition_broadcast(P), "w_mid")
            load(w_in[:], k_tiles(a["W_in"]), "w_mid")
            load(w_out[:], k_tiles(a["W_out"]), "w_mid")
            load(gam2[:], k_tiles(a["gamT"]), "w_mid")
            load(bet2[:], k_tiles(a["betT"]), "w_mid")
            load(down_w[:], k_tiles(a["down_wT"]), "w_mid")
            load(up_w[:], a["up_wT"], "w_mid")
            load(lng_row[:], a["ln_g"].partition_broadcast(P), "w_mid")
            load(lnb_row[:], a["ln_b"].partition_broadcast(P), "w_mid")
            sp.wait_ge(s["pro_v"], PRO_ROWS)
            load(rows_d, emb_rows, "rows_out")
            sp.wait_ge(s["rows_out"], DMA)

            def expert(batch, base, last):
                index = sp.value_load(ids_ok[0:1, bass.ds(base + batch, 1)], min_val=0, max_val=last)
                return index

            def head(it, slot, att, pre):
                if att and slot % 2 == 0:
                    pair = slot // 2 + RING
                    if pair < H // 2 or pre:
                        at(sp, "exped", it, 2 * (slot + 2))
                        batch = it if pair < H // 2 else it + 1
                        pair %= H // 2
                        sp.dma_start(bias[:, pair % RING], f_v[batch][:, 2 * pair:2 * pair + 2])\
                            .then_inc(s_bias[pair % RING], DMA)

            def loads0(it, phases):
                if "pre" in phases:
                    at(sp, "lnp", it)
                    load(x_in[:], x_v[it + 1], "x_loaded")
                    at(sp, "x1T_done", it)
                    if isinstance(it, int) and it < 0:
                        sp.wait_ge(s["pro_v"], PRO_COLS)
                    load(cols[:], cond_cols[:, it + 1, :], "cols_loaded")
                    if not (isinstance(it, int) and it < 0):
                        at(sp, "negated", it)
                        load(mask_in[:], mask_v[it + 1], "mask_loaded")
                if "att" in phases:
                    at(sp, "resid_done", it - 1)
                    load(rows[:], rows_d[it].partition_broadcast(P), "rows_loaded")
                if "end" in phases:
                    if isinstance(it, int) and it == 2:
                        sp.wait_ge(s["pro_v"], PRO_COLS2)
                    at(sp, "z_done", it - 3)
                    load(cols2[:], cond2_cols[:, it - 2, :], "cols2_loaded")

            def loads6(it, phases):
                if "mid" in phases:
                    e = expert(it - 1, 0, NE1 - 1)
                    at(sp, "x4T_done", it - 2)
                    load(ep[:], a["ep"][e], "ep_loaded")
                    at(sp, "x3b_done", it - 2)
                    load(bo_row[:], a["boe"][e].partition_broadcast(P), "bo_loaded")
                if "end" in phases:
                    e = expert(it - 2, B, NE3 - 1)
                    at(sp, "dom_done", it - 3)
                    load(l3[:], a["l3"][e], "l3_loaded")
                    load(idcol[:], a["id3"][bass.ds(it - 2, 1)].partition_broadcast(A3), "id_loaded")

            def loads12(it, phases):
                if "pre" in phases:
                    stack(it, 0)

            def stack(it, t):
                at(sp, "lo_done", it + 1)
                at(sp, "scored", it, HG * (t + 1))
                for dst, parts in ((q_stack, (q_hi, q_hi, q_lo, q_lo)), (k_stack, (k_hi, k_lo, k_hi, k_lo))):
                    for j, part in enumerate(parts):
                        load(dst[HD * j:HD * j + HD, HG * t:HG * t + HG, :].bitcast(F32), part[:, t, :].bitcast(F32), f"stack{t}")

            def loads14(it, phases):
                if "att" in phases:
                    at(sp, "e1_pe", it - 1)
                    if isinstance(it, int) and it == 0:
                        sp.wait_ge(s["pro_p"], PRO_PE_ALL)
                    load(wi[:], wi_v[expert(it, 0, NE1 - 1)], "wi_loaded")

            def loads4(it, phases):
                if "mid" in phases:
                    at(sp, "e2_pe", it - 2)
                    load(woe[:], woe_v[expert(it - 1, 0, NE1 - 1)], "woe_loaded")

            def loads15(it, phases):
                if "pre" in phases:
                    stack(it, 1)
                if "end" in phases:
                    at(sp, "fin", it - 2)
                    load(out_v[it - 2], x6[:], "out_stored")

            drive(sp, head, {}, {0: loads0, 4: loads4, 6: loads6, 12: loads12, 14: loads14, 15: loads15})
            sp.wait_ge(s["out_stored"], B * DMA)

        @block.tensor
        def _(pe):
            def turn(dst, src, name):
                for i in range(2):
                    for j in range(2):
                        last = pe.transpose(dst[:, j, i * P:(i + 1) * P], src[:, i, j * P:(j + 1) * P], ident[:])
                last.then_inc(s[name], 1)

            def product(dst, lhsT, rhs, kt):
                for k in range(kt):
                    last = pe.matmul(dst, lhsT(k), rhs(k), start=(k == 0), stop=(k == kt - 1))
                return last

            pe.wait_ge(s["w_cond2"], 3 * DMA)
            pe.wait_ge(s["pro_a"], 2)
            for m in range(4):
                last = product(sc_ps[0][:, 0, m * B:(m + 1) * B], lambda k: w_ada[:, k, m * P:(m + 1) * P],
                               lambda k: emb[:, k, :], 2)
            last.then_inc(s["pro_p"], 1)
            product(sc_ps[1][0:B, :, :].rearrange("p a n -> p (a n)"), lambda k: emb[:, k, :],
                    lambda k: w_ada[:, k, :], 2).then_inc(s["pro_p"], 1)
            pe.wait_ge(s["w_end"], 4 * DMA)
            for m in range(4):
                last = product(mid_ps[0][:, 0, m * B:(m + 1) * B], lambda k: w1c[:, m * P:(m + 1) * P],
                               lambda k: emb[:, 2, :], 1)
            last.then_inc(s["pro_p"], 1)
            pe.wait_ge(s["pro_a"], 6)
            for m in range(4):
                last = product(mid_ps[1][:, 0, m * B:(m + 1) * B], lambda k: w2c[:, k, m * P:(m + 1) * P],
                               lambda k: h1c[:, k, :], 4)
            last.then_inc(s["pro_p"], 1)
            pe.wait_ge(s["pro_a"], 10)
            for i, w in enumerate((wsc, wsh)):
                for m in range(2):
                    product(end_ps[:, 0, (2 * i + m) * B:(2 * i + m + 1) * B],
                            lambda k: w[:, k, m * P:(m + 1) * P], lambda k: h2c[:, k, :], 4).then_inc(s["pro_p"], 1)
            pe.wait_ge(s["w_id"], DMA)

            def scores(batch, h):
                at(pe, f"stack{h // HG}", batch)
                at(pe, "maxed", batch, 2 * h - 2)
                for t in range(ST):
                    last = pe.matmul(sc_ps[h % 2][:, t, :], q_stack[:, h, t * P:(t + 1) * P], k_stack[:, h, :],
                                     start=True, stop=True)
                last.then_inc(s["scored"], 1)

            def head(it, slot, att, pre):
                if att and slot < H - 1:
                    scores(it, slot + 1)
                if pre and slot == H - 1:
                    if isinstance(it, int) and it < 0:
                        pe.wait_ge(s["pro_v"], PRO_COLS)
                    scores(it + 1, 0)
                if att:
                    at(pe, "exped", it, 2 * slot + 2)
                    at(pe, "turned_sb", it, slot)
                    turn(pt_ps, probs[:, slot % 2], "turned")

            def pv(it, first):
                at(pe, "turned_sb", it, first + QUADS)
                if first == 0:
                    at(pe, "v_done", it)
                    at(pe, "ctx_done", it - 1)
                for k in range(ST):
                    for h in range(first, first + QUADS):
                        g, quad, half = place(h)
                        mm = pe.matmul(ctx_ps[32 * quad:32 * quad + 32, g, :], vpad[:, k, h, :],
                                       probsT[:, h % (2 * QUADS), k, :],
                                       start=(half == 0 and k == 0), stop=(half == 1 and k == ST - 1))
                        if k == ST - 1:
                            mm.then_inc(s["pv_done"], 1)

            def trp(it):
                at(pe, "lnp", it + 1)
                at(pe, "lnf", it - 3, 1)
                at(pe, "x1T_done", it)
                turn(end_ps, xn, "trp_pe")

            def project(w, name):
                for m in range(DT):
                    last = product(pre_ps[:, m, :], lambda k: w[:, k, m * P:(m + 1) * P], lambda k: x1T[:, k, :], DT)
                last.then_inc(s[name], 1)

            def q(it):
                if isinstance(it, int) and it < 0:
                    pe.wait_ge(s["w_qkv"], 4 * DMA)
                at(pe, "x1T_done", it + 1)
                at(pe, "v_done", it)
                project(wq, "q_pe")

            def k_(it):
                at(pe, "qkf_done", it + 1, 2)
                project(wk, "k_pe")

            def v(it):
                at(pe, "qkf_done", it + 1, 4)
                for t in range(ST):
                    last = product(pre_ps[:, t, :], lambda k: x1T[:, k, t * P:(t + 1) * P], lambda k: wv[:, k, :], DT)
                last.then_inc(s["v_pe"], 1)

            def rb(it):
                at(pe, "rinv_done", it - 1)
                at(pe, "e1_done", it - 2)
                if isinstance(it, int) and it == 1:
                    pe.wait_ge(s["w_mid"], 12 * DMA)
                    pe.wait_ge(s["pro_v"], PRO_COLS2)
                turn(mid_ps[0], rinv_wide, "rb_pe")

            def rows_product(dst, t, xT, w):
                return product(dst[:, t, :], lambda k: xT[:, k, t * P:(t + 1) * P], lambda k: w[:, k, :], DT)

            def long_product(part, xT, w, name):
                t, half = divmod(part, 2)
                for k in range(FT // 2 * half, FT // 2 * (half + 1)):
                    last = pe.matmul(mid_ps[1 - t][:, t, :], xT[:, k, t * P:(t + 1) * P], w[:, k, :],
                                     start=(k == 0), stop=(k == FT - 1))
                if half:
                    last.then_inc(s[name], 1)

            def cols_product(dst, m, w, n, xT):
                return product(dst[:, m, :], lambda k: w[:, k, n * P:(n + 1) * P], lambda k: xT[:, k, :], DT)

            def wo_(it):
                at(pe, "ctx_done", it - 1)
                at(pe, "rb_sb", it - 1)
                for t in range(ST):
                    last = rows_product(mid_ps[0], t, ctxT, wo)
                last.then_inc(s["wo_pe"], 1)

            def tr2(it):
                at(pe, "ln2", it - 1)
                at(pe, "lne", it - 2, 1)
                turn(mid_ps[1], x2n, "tr2_pe")

            def up_product(it, c, w, xT, name):
                for j in range(2):
                    last = cols_product(mid_ps[(c + 1) % 2], j, w, 2 * c + j, xT)
                last.then_inc(s[name], 1)

            def f(it, c):
                if c == 0:
                    at(pe, "h1T_done", it - 1)
                elif c == 1:
                    at(pe, "lne", it - 2, 2)
                else:
                    at(pe, "ff1_done", it - 1, 2 * c - 2)
                up_product(it, c, w1, h1T, "ff1_pe")

            def g(it, part):
                if part == 0:
                    at(pe, "ff1_done", it - 1)
                long_product(part, hT, w2, "ff2_pe")

            def tr3(it):
                at(pe, "x3_done", it - 1)
                turn(mid_ps[0], x3, "tr3_pe")

            def e(it, c):
                if c == 0:
                    at(pe, "wi_loaded", it - 1)
                    at(pe, "x3_done", it - 1)
                if c < 2:
                    at(pe, "x3T_done", it - 1)
                else:
                    at(pe, "e1_done", it - 1, 2 * c - 2)
                up_product(it, c, wi, x3T, "e1_pe")

            def h(batch, part):
                if part == 0:
                    at(pe, "e1_done", batch)
                    at(pe, "woe_loaded", batch)
                if part == 2:
                    at(pe, "ln2", batch + 1, 1)
                long_product(part, hT, woe, "e2_pe")

            def tr4(it):
                at(pe, "lne", it - 2)
                at(pe, "lnf", it - 3, 1)
                at(pe, "x1T_done", it + 1)
                turn(end_ps, yn, "tr4_pe")

            def st(it, n):
                at(pe, "l2", it - 2, 3 + 8 * n)
                pe.matmul(end_ps[:, 0, 0:2], mean_w[:], g_mv[:], start=True, stop=True).then_inc(s["st_pe"], 1)

            def win(it):
                at(pe, "z_done", it - 2, 2)
                for m in range(DT):
                    last = cols_product(end_ps, m, w_in, m, z)
                last.then_inc(s["win_pe"], 1)

            def wout(it):
                at(pe, "z_done", it - 2, 4)
                for m in range(DT):
                    last = cols_product(end_ps, m, w_out, m, z)
                last.then_inc(s["wout_pe"], 1)

            def down(it):
                at(pe, "l2", it - 2)
                product(end_ps[0:A3, 0, :], lambda k: down_w[:, k, :], lambda k: x5T[:, k, :], DT)\
                    .then_inc(s["down_pe"], 1)

            def exp_(it):
                at(pe, "hid_done", it - 2)
                at(pe, "sel_done", it - 2)
                settle(pe)
                product(end_ps[0:A3, 0, :], lambda k: wsel[:], lambda k: hid[:], 1).then_inc(s["exp_pe"], 1)

            def tr5(it):
                at(pe, "x5b_done", it - 2)
                at(pe, "dom_done", it - 2)
                turn(end_ps, x5b, "tr5_pe")

            def up(it):
                at(pe, "x5_done", it - 2)
                for t in range(ST):
                    last = product(end_ps[:, t, :], lambda k: dom[:, t * P:(t + 1) * P], lambda k: up_w[:], 1)
                last.then_inc(s["up_pe"], 1)

            stages = dict(trp=trp, q=q, k=k_, v=v, rb=rb, wo=wo_, tr2=tr2, tr3=tr3, tr4=tr4,
                          st1=lambda it: st(it, 0), st2=lambda it: st(it, 1), win=win, wout=wout, down=down,
                          exp=exp_, tr5=tr5, up=up, h0=lambda it: h(it - 1, 0))
            for c in range(4):
                stages[f"f{c}"] = lambda it, c=c: f(it, c)
                stages[f"g{c}"] = lambda it, c=c: g(it, c)
                stages[f"e{c}"] = lambda it, c=c: e(it, c)
                if c:
                    stages[f"h{c}"] = lambda it, c=c: h(it - 2, c)

            def finish(slot):
                return lambda it, phases: pv(it, slot + 1 - QUADS) if "att" in phases else None

            drive(pe, head, stages, {slot: finish(slot) for slot in range(QUADS - 1, H, QUADS)})

        @block.scalar
        def _(act):
            def line(dst, src, func, bias, scale, name):
                act.activation(dst, src, func, bias=bias, scale=scale).then_inc(s[name], 1)

            act.wait_ge(s["pro_v"], PRO_ANGLE)
            line(emb, red, ACT.Sin, 0.0, 1.0, "pro_a")
            act.wait_ge(s["pro_a"], 1)
            act.activation(emb[:, 0:2, :], emb[:, 0:2, :], ACT.Silu).then_inc(s["pro_a"], 1)
            act.wait_ge(s["pro_p"], 3)
            for m in range(4):
                line(h1c[:, m, :], mid_ps[0][:, 0, m * B:(m + 1) * B], ACT.Silu, cvec[:, 4 + m:5 + m], 1.0, "pro_a")
            act.wait_ge(s["pro_p"], 4)
            for m in range(4):
                line(h2c[:, m, :], mid_ps[1][:, 0, m * B:(m + 1) * B], ACT.Identity, cvec[:, 8 + m:9 + m], 1.0, "pro_a")
            act.wait_ge(s["w_vec"], DMA)

            def softmax(batch, h):
                if h == 0:
                    at(act, "rinv_done", batch - 1, 1)
                at(act, "turned", batch, h - 1)
                g, quad, half = place(h)
                col = g * HG + 2 * quad + half
                for t in range(ST):
                    at(act, "maxed", batch, 2 * h + t + 1)
                    act.activation(probs[:, h % 2, t, :], bias[:, h // 2 % RING, h % 2, t, :], ACT.Exp,
                                   bias=nmax[:, h % 2, t:t + 1], scale=-1.0,
                                   accum_out=rowsum[:, t, col:col + 1]).then_inc(s["exped"], 1)

            def head(it, slot, att, pre):
                if att and slot < H - 1:
                    softmax(it, slot + 1)
                if pre and slot == H - 1:
                    softmax(it + 1, 0)

            def modulate(dst, src, tile_, c0, name):
                for m in range(DT):
                    line(dst[:, m, :], src[:, m, :], ACT.Identity, tile_[:, c0 + DT + m:c0 + DT + m + 1],
                         tile_[:, c0 + m:c0 + m + 1], name)

            def trp(it):
                at(act, "trp_pe", it + 1)
                at(act, "cols_loaded", it + 1)
                at(act, "v_pe", it)
                modulate(x1T, end_ps, cols, 0, "x1T_done")

            def qk(it, n, pe_done, vec_bias, scale):
                at(act, pe_done, it + 1)
                at(act, "lo_done", it + n, 1 + (1 - n))
                for m in range(DT):
                    line(qkf[:, m, :], pre_ps[:, m, :], ACT.Identity, vec_bias[:, m:m + 1], scale, "qkf_done")

            def rb(it):
                at(act, "rb_pe", it - 1)
                at(act, "ctx_done", it - 2)
                act.activation(rinv_sb[:], mid_ps[0][:], ACT.Copy).then_inc(s["rb_sb"], 1)

            def tr2(it):
                at(act, "tr2_pe", it - 1)
                modulate(h1T, mid_ps[1], vec, VG2, "h1T_done")

            def hidden(it, half, func, bias_tile, b0, pe_name, name):
                for c in range(2):
                    at(act, pe_name, it - 1, 2 * half + c + 1)
                    for j in range(2):
                        f = 4 * half + 2 * c + j
                        line(hT[:, f, :], mid_ps[(c + 1) % 2][:, j, :], func, bias_tile[:, b0 + f:b0 + f + 1], 1.0, name)

            def tr3(it):
                at(act, "tr3_pe", it - 1)
                act.activation(x3T[:], mid_ps[0][:], ACT.Copy).then_inc(s["x3T_done"], 1)

            def expert_hidden(it, half):
                if half == 0:
                    at(act, "ep_loaded", it - 1)
                hidden(it, half, ACT.Gelu, ep, 0, "e1_pe", "e1_done")

            def tr4(it):
                at(act, "tr4_pe", it - 2)
                modulate(x4T, end_ps, ep, FT, "x4T_done")

            def silu(it, n):
                at(act, "l2", it - 2, 8 + 8 * n)
                at(act, "cols2_loaded", it - 2)
                for m in range(DT):
                    line(z[:, m, :], u[:, m, :], ACT.Silu, cols2[:, DT + m:DT + m + 1], cols2[:, m:m + 1], "z_done")

            def win(it):
                at(act, "win_pe", it - 2)
                for m in range(DT):
                    line(y[:, m, :], end_ps[:, m, :], ACT.Identity, vec[:, VBIN + m:VBIN + m + 1], 1.0, "y_done")

            def down(it):
                at(act, "down_pe", it - 2)
                line(hid[:], end_ps[0:A3, 0, :], ACT.Gelu, vec[0:A3, VDNB:VDNB + 1], 1.0, "hid_done")

            def exp_(it):
                at(act, "exp_pe", it - 2)
                line(dom[:], end_ps[0:A3, 0, :], ACT.Identity, sel[:, 3:4], 1.0, "dom_done")

            def tr5(it):
                at(act, "tr5_pe", it - 2)
                act.activation(x5[:], end_ps[:], ACT.Copy).then_inc(s["x5_done"], 1)

            stages = dict(
                trp=trp, q=lambda it: qk(it, 0, "q_pe", qkb[:], 0.25),
                k=lambda it: qk(it, 1, "k_pe", vec[:, VK:VK + 2], 1.0),
                rb=rb, tr2=tr2,
                f1=lambda it: hidden(it, 0, ACT.Gelu_apprx_sigmoid, vec, VB1, "ff1_pe", "ff1_done"),
                f3=lambda it: hidden(it, 1, ACT.Gelu_apprx_sigmoid, vec, VB1, "ff1_pe", "ff1_done"),
                tr3=tr3, e1=lambda it: expert_hidden(it, 0), e3=lambda it: expert_hidden(it, 1),
                tr4=tr4, u1=lambda it: silu(it, 0), u2=lambda it: silu(it, 1), win=win, down=down, exp=exp_, tr5=tr5)
            drive(act, head, stages)

        @block.vector
        def _(dve):
            dve.memset(mean_w[:], 1.0 / P).then_inc(s["consts_v"], 1)
            dve.memset(vpad[:, 0], 0.0).then_inc(s["consts_v"], 1)
            dve.memset(vpad[:, 1], 0.0).then_inc(s["consts_v"], 1)
            pro = [0]

            def step(ins):
                pro[0] += 1
                ins.then_inc(s["pro_v"], 1)
                dve.wait_ge(s["pro_v"], pro[0])

            dve.wait_ge(s["w_cond"], 6 * DMA)
            step(dve.tensor_copy(t_f[:, 0, :], t_i))
            step(dve.tensor_scalar(ang[:, 0, :], t_f[:, 0, :], 40.0, None, ALU.mult))
            step(dve.tensor_scalar(ang[:, 1, :], t_f[:, 0, :], 40.0, None, ALU.mult))
            step(dve.tensor_scalar(ang[:, 2, :], t_f[:, 1, :], 5000.0, None, ALU.mult))
            wide = [P, 3, B]
            step(dve.tensor_tensor(ang, ang, fq[:, 0:3].unsqueeze(2).to_broadcast(wide), ALU.mult))
            step(dve.scalar_tensor_tensor(out=kk, in0=ang, scalar=1.0 / TWO_PI,
                                          in1=fq[:, 3:6].unsqueeze(2).to_broadcast(wide), op0=ALU.mult, op1=ALU.add))
            step(dve.tensor_scalar(kk, kk, ROUND, None, ALU.add))
            step(dve.tensor_scalar(kk, kk, ROUND, None, ALU.subtract))
            step(dve.scalar_tensor_tensor(out=red, in0=kk, scalar=-PI_1, in1=ang, op0=ALU.mult, op1=ALU.add))
            step(dve.scalar_tensor_tensor(out=red, in0=kk, scalar=-PI_2, in1=red, op0=ALU.mult, op1=ALU.add))
            step(dve.scalar_tensor_tensor(out=red, in0=kk, scalar=-PI_3, in1=red, op0=ALU.mult, op1=ALU.add))
            step(dve.tensor_scalar(ph2, fq[:, 3:6], TWO_PI, None, ALU.mult))
            step(dve.tensor_tensor(red, red, ph2.unsqueeze(2).to_broadcast(wide), ALU.add))
            step(dve.tensor_scalar(red, red, -PI_LIMIT, PI_LIMIT, ALU.max, ALU.min))
            assert pro[0] == PRO_ANGLE
            step(dve.tensor_scalar(ids_ok[:, 0:B], ids[:, 0:B], 0, NE1 - 1, ALU.max, ALU.min))
            step(dve.tensor_scalar(ids_ok[:, B:], ids[:, B:], 0, NE3 - 1, ALU.max, ALU.min))
            dve.wait_ge(s["w_vec"], DMA)
            step(dve.tensor_scalar(qkb[:], vec[:, VQ:VQ + 2], 0.25, None, ALU.mult))
            dve.wait_ge(s["pro_p"], 1)
            for m in range(4):
                step(dve.tensor_scalar(cond_cols[:, :, m], sc_ps[0][:, 0, m * B:(m + 1) * B], cvec[:, m:m + 1],
                                       1.0 if m < 2 else 0.0, ALU.add, ALU.add))
            assert pro[0] == PRO_COLS
            dve.wait_ge(s["pro_p"], 2)
            dve.wait_ge(s["w_cond2"], 3 * DMA)
            step(dve.memset(ada_c[:, 0:D], 1.0))
            step(dve.tensor_tensor(emb_rows, sc_ps[1][0:B, :, :].rearrange("p a n -> p (a n)"), ada_b, ALU.add))
            step(dve.tensor_tensor(emb_rows, emb_rows, ada_c, ALU.add))
            assert pro[0] == PRO_ROWS
            dve.wait_ge(s["pro_p"], PRO_PE_ALL)
            for m in range(4):
                step(dve.tensor_scalar(cond2_cols[:, :, m], end_ps[:, 0, m * B:(m + 1) * B],
                                       cvec[:, 12 + m:13 + m], None, ALU.add))
            assert pro[0] == PRO_COLS2
            dve.wait_ge(s["consts_v"], 3)

            def maxima(batch, h):
                at(dve, "scored", batch, h + 1)
                at(dve, "masked", batch, h + 1)
                at(dve, "exped", batch, 2 * h - 2)
                settle(dve)
                for t in range(ST):
                    b = bias[:, h // 2 % RING, h % 2, t, :]
                    dve.tensor_tensor_reduce(b, sc_ps[h % 2][:, t, :], b, -1.0, BIG, ALU.add, ALU.min,
                                             nmax[:, h % 2, t:t + 1]).then_inc(s["maxed"], 1)

            def head(it, slot, att, pre):
                if att and slot < H - 1:
                    maxima(it, slot + 1)
                if pre and slot == H - 1:
                    maxima(it + 1, 0)
                if att:
                    at(dve, "turned", it, slot + 1)
                    at(dve, "pv_done", it, QUADS * (slot // QUADS - 1))
                    dve.tensor_copy(probsT[:, slot % (2 * QUADS)], pt_ps[:]).then_inc(s["turned_sb"], 1)
                if att and slot == H - 1:
                    at(dve, "exped", it)
                    at(dve, "rb_pe", it - 1)
                    dve.reciprocal(rinv[:], rowsum[:]).then_inc(s["rinv_done"], 1)
                    at(dve, "rinv_done", it, 1)
                    dve.tensor_copy(rinv_wide[:].rearrange("p t (h d) -> p (t h) d", d=HD),
                                    rinv[:].rearrange("p t h -> p (t h)").unsqueeze(2)
                                    .to_broadcast([P, ST * H, HD])).then_inc(s["rinv_done"], 1)

            def row_stats(batch, src, tiles, name, k, eps):
                bn, mv, ve, rs = tiles
                for t in range(ST):
                    dve.bn_stats(bn[:, t, :], src[:, t, :]).then_inc(s[name], 1)
                for t in range(ST):
                    at(dve, name, batch, k + t + 1)
                    settle(dve)
                    dve.bn_aggr(mv[:, t, :], bn[:, t, :]).then_inc(s[name], 1)
                at(dve, name, batch, k + 4)
                dve.tensor_scalar(ve[:], mv[:, :, 1], eps, None, ALU.add).then_inc(s[name], 1)

            def row_norm(batch, src, tiles, name, rsq, dst):
                bn, mv, ve, rs = tiles
                at(dve, rsq, batch)
                for t in range(ST):
                    dve.tensor_scalar(dst[:, t, :], src[:, t, :], mv[:, t, 0:1], rs[:, t:t + 1],
                                      ALU.subtract, ALU.mult).then_inc(s[name], 1)

            def lnp(it):
                at(dve, "x_loaded", it + 1)
                row_stats(it + 1, x_in, stat_p, "lnp", 0, 1e-5)

            def np_(it):
                at(dve, "resid_done", it)
                at(dve, "trp_pe", it)
                row_norm(it + 1, x_in, stat_p, "lnp", "rsq_p", xn)

            def hi(it, n, dst):
                at(dve, "qkf_done", it + 1, 2 * n + 2)
                if n == 0:
                    at(dve, "stack0", it)
                    at(dve, "stack1", it)
                dve.tensor_copy(dst[:], qkf[:]).then_inc(s["hi_done"], 1)

            def vpad_(it):
                if isinstance(it, int) and it == 0:
                    dve.wait_ge(s["w_qkv"], 4 * DMA)
                at(dve, "v_pe", it)
                at(dve, "pv_done", it - 1)
                for k in range(ST):
                    for half in range(2):
                        def heads(ap):
                            return ap.rearrange("p (g f j d) -> p g f j d", g=DT, f=2, j=QUADS)[:, :, half]
                        dst = vpad[:, k, :, half * HD:(half + 1) * HD]\
                            .rearrange("p (g f j) d -> p g f j d", g=DT, f=2)[:, :, half]
                        dve.tensor_tensor(dst, heads(pre_ps[:, k, :]), heads(bv_row[:]), ALU.add)\
                            .then_inc(s["v_done"], 1)

            def rb(it):
                at(dve, "rb_sb", it - 1)
                at(dve, "pv_done", it - 1)
                at(dve, "wo_pe", it - 2)
                dve.tensor_tensor(ctxT[:], ctx_ps[:], rinv_sb[:], ALU.mult).then_inc(s["ctx_done"], 1)

            def wo_(it):
                at(dve, "wo_pe", it - 1)
                at(dve, "resid_done", it - 1)
                at(dve, "x2b_done", it - 2)
                dve.tensor_tensor(x2[:], mid_ps[0][:], resid[:], ALU.add).then_inc(s["ln2"], 1)
                at(dve, "ln2", it - 1, 1)
                row_stats(it - 1, x2, stat_2, "ln2", 1, 1e-5)

            def ff2(it, t):
                at(dve, "ff2_pe", it - 1, t + 1)
                at(dve, "x2b_done", it - 1, t + 1)
                at(dve, "x3b_done", it - 2)
                dve.tensor_tensor(x3[:, t, :], mid_ps[1 - t][:, t, :], x2b[:, t, :], ALU.add).then_inc(s["x3_done"], 1)

            def h(it, t):
                at(dve, "e2_pe", it - 2, t + 1)
                at(dve, "x3b_done", it - 2, t + 1)
                dve.tensor_tensor(x4[:, t, :], mid_ps[1 - t][:, t, :], x3b[:, t, :], ALU.add).then_inc(s["lne"], 1)
                if t == 1:
                    at(dve, "lne", it - 2, 2)
                    row_stats(it - 2, x4, stat_e, "lne", 2, 1e-12)

            def matrix_stats(it, n, src, ready):
                at(dve, *ready)
                k = 8 * n
                at(dve, "st_pe", it - 2 - (1 - n), 1 if n else 2)
                dve.bn_stats(g_bn[:], src[:].rearrange("p a n -> p (a n)")).then_inc(s["l2"], 1)
                at(dve, "l2", it - 2, k + 1)
                settle(dve)
                dve.bn_aggr(g_mv[:], g_bn[:]).then_inc(s["l2"], 1)
                at(dve, "l2", it - 2, k + 2)
                dve.scalar_tensor_tensor(out=g_mv[:, 1:2], in0=g_mv[:, 0:1], scalar=g_mv[:, 0:1], in1=g_mv[:, 1:2],
                                         op0=ALU.mult, op1=ALU.add).then_inc(s["l2"], 1)

            def matrix_norm(it, n, src):
                k = 8 * n
                at(dve, "st_pe", it - 2, n + 1)
                dve.tensor_copy(g_all[:], end_ps[:, 0, 0:2]).then_inc(s["l2"], 1)
                at(dve, "l2", it - 2, k + 4)
                dve.scalar_tensor_tensor(out=g_ve[:, 0:1], in0=g_all[:, 0:1], scalar=g_all[:, 0:1],
                                         in1=g_all[:, 1:2], op0=ALU.mult, op1=ALU.subtract).then_inc(s["l2"], 1)
                at(dve, "l2", it - 2, k + 5)
                dve.tensor_scalar(g_ve[:, 1:2], g_ve[:, 0:1], -1.0, 1e-5, ALU.mult, ALU.add).then_inc(s["l2"], 1)
                at(dve, "z_done", it - 2, 2 * n)
                dve.scalar_tensor_tensor(out=u[:], in0=src[:], scalar=g_all[:, 0:1], in1=gam2[:],
                                         op0=ALU.subtract, op1=ALU.mult).then_inc(s["l2"], 1)
                at(dve, "l2", it - 2, k + 7)
                at(dve, "rsq_g", it - 2, n + 1)
                dve.scalar_tensor_tensor(out=u[:], in0=u[:], scalar=g_rs[:, 0:1], in1=bet2[:],
                                         op0=ALU.mult, op1=ALU.add).then_inc(s["l2"], 1)

            def wout(it):
                at(dve, "wout_pe", it - 2)
                at(dve, "x5b_done", it - 3)
                for m in range(DT):
                    dve.scalar_tensor_tensor(out=x5T[:, m, :], in0=end_ps[:, m, :],
                                             scalar=vec[:, VBOUT + m:VBOUT + m + 1], in1=x4T[:, m, :],
                                             op0=ALU.add, op1=ALU.add).then_inc(s["l2"], 1)

            def select(it):
                at(dve, "l3_loaded", it - 2)
                at(dve, "id_loaded", it - 2)
                b = it - 2
                dve.tensor_scalar(sel[:, 0:1], idcol[:], 0.0, None, ALU.is_ge).then_inc(s["sel_done"], 1)
                at(dve, "sel_done", b, 1)
                dve.scalar_tensor_tensor(out=sel[:, 1:2], in0=idcol[:], scalar=float(NE3), in1=sel[:, 0:1],
                                         op0=ALU.is_lt, op1=ALU.mult).then_inc(s["sel_done"], 1)
                at(dve, "sel_done", b, 2)
                dve.tensor_scalar(sel[:, 2:3], sel[:, 1:2], -1.0, 1.0, ALU.mult, ALU.add).then_inc(s["sel_done"], 1)
                at(dve, "sel_done", b, 3)
                dve.tensor_scalar(wsel[:], ident[0:A3, 0:A3], sel[:, 2:3], None, ALU.mult).then_inc(s["sel_done"], 1)
                at(dve, "sel_done", b, 4)
                dve.scalar_tensor_tensor(out=wsel[:], in0=l3[:, 0:A3], scalar=sel[:, 1:2], in1=wsel[:],
                                         op0=ALU.mult, op1=ALU.add).then_inc(s["sel_done"], 1)
                dve.scalar_tensor_tensor(out=sel[:, 3:4], in0=l3[:, A3:A3 + 1], scalar=sel[:, 1:2],
                                         in1=l3[:, A3 + 1:A3 + 2], op0=ALU.mult, op1=ALU.add)\
                    .then_inc(s["sel_done"], 1)

            def up(it):
                at(dve, "up_pe", it - 2)
                at(dve, "x5_done", it - 2)
                at(dve, "out_stored", it - 3)
                dve.tensor_tensor(x6[:], end_ps[:], x5[:], ALU.add).then_inc(s["lnf"], 1)
                at(dve, "lnf", it - 2, 1)
                row_stats(it - 2, x6, stat_f, "lnf", 1, 1e-5)

            stages = dict(
                lnp=lnp, q=lambda it: hi(it, 0, q_hi), k=lambda it: hi(it, 1, k_hi), vpad=vpad_, rb=rb, wo=wo_,
                np=np_, n2=lambda it: row_norm(it - 1, x2, stat_2, "ln2", "rsq_2", x2n),
                g1=lambda it: ff2(it, 0), g3=lambda it: ff2(it, 1), h1=lambda it: h(it, 0), h3=lambda it: h(it, 1),
                ne=lambda it: row_norm(it - 2, x4, stat_e, "lne", "rsq_e", yn),
                nf=lambda it: row_norm(it - 2, x6, stat_f, "lnf", "rsq_f", x6),
                s1=lambda it: matrix_stats(it, 0, x4T, ("x4T_done", it - 2)), u1=lambda it: matrix_norm(it, 0, x4T),
                s2=lambda it: matrix_stats(it, 1, y, ("y_done", it - 2)), u2=lambda it: matrix_norm(it, 1, y),
                wout=wout, down=select, up=up)
            drive(dve, head, stages)

        @block.gpsimd
        def _(pool):
            pool.memset(neg_half[:], -0.5).then_inc(s["consts_p"], 1)
            pool.wait_ge(s["consts_p"], 1)

            def negate(batch):
                at(pool, "mask_loaded", batch)
                at(pool, "masked", batch - 1)
                settle(pool)
                pool.tensor_scalar(mask_add[:], mask_in[:], MASKED, None, ALU.mult).then_inc(s["negated"], 1)

            def add_mask(batch, h):
                pair = h // 2
                at(pool, "negated", batch)
                need(pool, s_bias[pair % RING], batch * 2 * DMA + DMA * (pair // RING + 1))
                b = bias[:, pair % RING, h % 2]
                pool.tensor_tensor(b, b, mask_add[:], ALU.add).then_inc(s["masked"], 1)

            def head(it, slot, att, pre):
                ahead = slot + 3
                if ahead < H:
                    if att:
                        add_mask(it, ahead)
                elif pre:
                    if ahead == H:
                        negate(it + 1)
                    add_mask(it + 1, ahead - H)

            def inv_sqrt(batch, name, k, rsq, ve, rs):
                at(pool, name, batch, k)
                pool.tensor_tensor(rs, ve, neg_half[:, 0:ve.shape[1]], ALU.pow).then_inc(s[rsq], 1)

            def lo(it, n, dst, hi):
                at(pool, "hi_done", it + 1, n + 1)
                pool.tensor_tensor(dst[:], qkf[:], hi[:].bitcast(F32), ALU.subtract).then_inc(s["lo_done"], 1)

            def resid_(it):
                at(pool, "rows_loaded", it)
                at(pool, "lnp", it)
                at(pool, "ln2", it - 1, 1)
                for t in range(ST):
                    pool.tensor_tensor(resid[:, t, :], xn[:, t, :], rows[:, 0:D], ALU.mult)\
                        .then_inc(s["resid_done"], 1)
                for t in range(ST):
                    at(pool, "resid_done", it, t + 1)
                    pool.tensor_tensor(resid[:, t, :], resid[:, t, :], rows[:, D:], ALU.add)\
                        .then_inc(s["resid_done"], 1)

            def add_row(batch, dst, src, row, name):
                for t in range(ST):
                    pool.tensor_tensor(dst[:, t, :], src[:, t, :], row[:], ALU.add).then_inc(s[name], 1)

            def wo_(it):
                inv_sqrt(it - 1, "ln2", 6, "rsq_2", stat_2[2][:], stat_2[3][:])
                at(pool, "x3_done", it - 2)
                add_row(it - 1, x2b, x2, b2_row, "x2b_done")

            def g3(it):
                at(pool, "x3_done", it - 1)
                at(pool, "bo_loaded", it - 1)
                at(pool, "lne", it - 2, 2)
                add_row(it - 1, x3b, x3, bo_row, "x3b_done")

            def wout(it):
                at(pool, "l2", it - 2)
                at(pool, "tr5_pe", it - 3)
                settle(pool)
                for m in range(DT):
                    pool.tensor_scalar(x5b[:, m, :], x5T[:, m, :], vec[:, VUPB + m:VUPB + m + 1], None, ALU.add)\
                        .then_inc(s["x5b_done"], 1)

            def nf(it):
                for t in range(ST):
                    at(pool, "lnf", it - 2, 7 + t)
                    pool.tensor_tensor(x6[:, t, :], x6[:, t, :], lng_row[:], ALU.mult).then_inc(s["fin"], 1)
                for t in range(ST):
                    at(pool, "fin", it - 2, t + 1)
                    pool.tensor_tensor(x6[:, t, :], x6[:, t, :], lnb_row[:], ALU.add).then_inc(s["fin"], 1)

            stages = dict(
                lnp=lambda it: inv_sqrt(it + 1, "lnp", 5, "rsq_p", stat_p[2][:], stat_p[3][:]),
                q=lambda it: lo(it, 0, q_lo, q_hi), k=lambda it: lo(it, 1, k_lo, k_hi), resid=resid_,
                wo=wo_, g3=g3,
                h3=lambda it: inv_sqrt(it - 2, "lne", 7, "rsq_e", stat_e[2][:], stat_e[3][:]),
                u1=lambda it: inv_sqrt(it - 2, "l2", 6, "rsq_g", g_ve[:, 1:2], g_rs[:]),
                u2=lambda it: inv_sqrt(it - 2, "l2", 14, "rsq_g", g_ve[:, 1:2], g_rs[:]),
                wout=wout, up=lambda it: inv_sqrt(it - 2, "lnf", 6, "rsq_f", stat_f[2][:], stat_f[3][:]), nf=nf)
            drive(pool, head, stages)


PRO_PE_ALL = 8
PRO_ANGLE = 14
PRO_COLS = PRO_ANGLE + 3 + 4
PRO_ROWS = PRO_COLS + 3
PRO_COLS2 = PRO_ROWS + 4


def kernel(**inputs):
    import concourse.bacc as bacc
    from concourse.bass_utils import run_bass_kernel_spmd

    g = {k: np.asarray(v) for k, v in inputs.items()}

    def columns(v):
        return v.reshape(-1, P).T

    def head_order(w):
        return w.reshape(w.shape[:-1] + (DT, HG, HD)).swapaxes(-1, -2).reshape(w.shape)

    def place_order(w):
        return w.reshape(DT, 2, QUADS, HD, -1).swapaxes(1, 2).reshape(w.shape)

    half0, half2 = D // 2, 64
    freq0 = np.exp(np.arange(half0, dtype=np.float32) * np.float32(-math.log(10000.0) / (half0 - 1)))
    freq2 = np.exp(np.arange(half2, dtype=np.float32) * np.float32(-math.log(10000.0) / (half2 - 1)))
    freqs = np.zeros((P, 6), np.float32)
    freqs[:, 0] = freqs[:, 1] = freq0
    freqs[:, 2] = np.concatenate([freq2, freq2])
    freqs[:, 4] = 0.25
    freqs[half2:, 5] = 0.25
    L0, L1, L2, L3 = (f"L{i}_cond_" for i in range(4))
    down_b = np.zeros((P, 1), np.float32)
    down_b[:A3, 0] = g[L3 + "down_b"]
    vec = np.concatenate([columns(head_order(g[L0 + "bq"])), columns(head_order(g[L0 + "bk"])),
                          columns(g[L0 + "g2"]), columns(g[L0 + "beta2"]), columns(g[L0 + "b1"]),
                          columns(g[L2 + "b_in"]), columns(g[L2 + "b_out"]), columns(g[L3 + "up_b"]), down_b,
                          np.zeros((P, 4), np.float32)], axis=1)
    cvec = np.concatenate([columns(g[L0 + "b_ada"]), columns(g[L2 + "b1"]), columns(g[L2 + "b2"]),
                           columns(g[L2 + "bsc"]), columns(g[L2 + "bsh"])], axis=1)
    ep = np.concatenate([g[L1 + n].reshape(NE1, -1, P).transpose(0, 2, 1) for n in ("bi", "gamma", "beta")], axis=2)
    l3 = np.concatenate([g[L3 + "expert_W"].transpose(0, 2, 1), g[L3 + "expert_b"][:, :, None],
                         g[L3 + "domain_emb"][:, :, None]], axis=2)
    data = {
        "x": g["x"], "fside": g["fside_Bx16xSxS_0"], "mask": g["mask_Bx1xSxS_bk0"],
        "timestep": g["itok_B_34_63"], "id1": g["itok_B_0_7"], "id3": g["itok_B_0_15"], "t2": g["condB_t"],
        "freqs": freqs, "ident": np.eye(P, dtype=np.float32), "vec": vec, "cvec": cvec,
        "W_ada": g[L0 + "W_ada"], "b_ada": g[L0 + "b_ada"], "bo": g[L0 + "bo"],
        "Wq": head_order(g[L0 + "Wq"]), "Wk": head_order(g[L0 + "Wk"]), "Wv": g[L0 + "Wv"], "bv": g[L0 + "bv"],
        "Wo": place_order(g[L0 + "Wo"]), "W1": g[L0 + "W1"], "W2": g[L0 + "W2"], "b2": g[L0 + "b2"],
        "Wi": g[L1 + "Wi"], "Woe": g[L1 + "Wo"], "boe": g[L1 + "bo"], "ep": ep,
        "W1c": g[L2 + "W1"], "W2c": g[L2 + "W2"], "Wsc": g[L2 + "Wsc"], "Wsh": g[L2 + "Wsh"],
        "W_in": g[L2 + "W_in"], "W_out": g[L2 + "W_out"], "gamT": g[L2 + "gamma"].T, "betT": g[L2 + "beta"].T,
        "down_wT": g[L3 + "down_W"].T, "up_wT": g[L3 + "up_W"].T, "l3": l3,
        "ln_g": g[L3 + "ln_gamma"], "ln_b": g[L3 + "ln_beta"],
    }
    nc = bacc.Bacc("TRN2", target_bir_lowering=False, num_devices=1)
    arrays, args = {}, {}
    for name, value in data.items():
        value = np.ascontiguousarray(value)
        arrays[f"in_{name}"] = value
        args[name] = nc.dram_tensor(f"in_{name}", value.shape, mybir.dt.from_np(value.dtype), kind="ExternalInput").ap()
    args["out"] = nc.dram_tensor("out_0", (B, S, D), F32, kind="ExternalOutput").ap()
    build(nc, args)
    result = run_bass_kernel_spmd(nc, [arrays], core_ids=[0])
    return result.results[0]["out_0"]
```

```python
from contextlib import ExitStack
import math

import numpy as np

import concourse.bass as bass
from concourse import mybir

F32 = mybir.dt.float32
F32R = mybir.dt.float32r
I32 = mybir.dt.int32
U8 = mybir.dt.uint8
ALU = mybir.AluOpType
ACT = mybir.ActivationFunctionType

B, S, D = 16, 256, 256
H, HD = 16, 16
F = 1024
P = 128
ST = S // P
DT = D // P
FT = F // P
HG = 8
NE1, NE3, A3 = 8, 16, 64
BIG = 3.0e38
MASKED = -1.0e30
DMA = 16
RING = 4
EXP_LEAD = 1
SCORE_LEAD = 2
MASK_LEAD = 4
QUADS = 4

SCHEDULE = {
    "SP": [
        ["l_x", "l_bias"],
        ["w_end"],
        ["l_bias"],
        [],
        ["l_bias"],
        [],
        ["l_par", "l_woe", "l_bias", "w_mid"],
        [],
        ["l_bias"],
        [],
        ["l_bias"],
        [],
        ["l_bias"],
        [],
        ["stack0", "l_wi", "w_bias", "l_bias"],
        ["stack1", "l_out"],
    ],
    "PE": [
        ["next", "pv3", "turn", "rb"],
        ["h1", "turn", "next"],
        ["wo", "next", "turn", "h2"],
        ["next", "turn", "h3", "tr2"],
        ["next", "pv0", "turn", "trp", "f0"],
        ["f1", "next", "tr4", "turn"],
        ["q", "f2", "turn", "next", "f3", "k"],
        ["next", "turn"],
        ["next", "st1", "g0", "pv1", "turn", "g1", "g2"],
        ["win", "next", "turn"],
        ["g3", "next", "st2", "turn", "v", "tr3"],
        ["turn", "next", "c1", "wout"],
        ["next", "e0", "c2", "turn", "down"],
        ["e1", "e2", "next", "turn", "exp", "pv2"],
        ["turn", "next"],
        ["tr5", "e3", "c3", "next", "turn", "up", "h0"],
    ],
    "ACT": [
        ["next", "rb"],
        ["next"],
        ["next"],
        ["next", "tr2"],
        ["next", "trp", "f1"],
        ["next", "q"],
        ["tr4", "next", "f3", "k"],
        ["next"],
        ["next", "u1"],
        ["win", "next"],
        ["next", "u2", "tr3"],
        ["c1", "next"],
        ["next", "down", "c2"],
        ["e1", "next", "exp"],
        ["next"],
        ["e3", "next"],
    ],
    "DVE": [
        ["next", "turn", "rb"],
        ["vpad", "turn", "next", "h1", "wo"],
        ["next", "turn", "c0", "lnp"],
        ["next", "n2", "turn", "h3", "np"],
        ["tr2", "split_qkv", "ne", "next", "trp", "turn"],
        ["next", "turn"],
        ["next", "q", "turn", "s1"],
        ["turn", "next"],
        ["k", "u1", "next", "turn"],
        ["g1", "next", "s2", "turn"],
        ["g3", "u2", "next", "turn"],
        ["next", "turn", "wout"],
        ["next", "turn"],
        ["down", "next", "turn"],
        ["split_w1", "next", "turn"],
        ["tr5", "rinv", "c3", "turn", "up", "next", "nf"],
    ],
    "POOL": [
        ["next"],
        ["next", "wo"],
        ["next", "lnp"],
        ["resid", "next"],
        ["h3", "next", "trp"],
        ["tr2", "next"],
        ["next"],
        ["next"],
        ["next"],
        ["q", "u1", "next"],
        ["u2", "k", "next"],
        ["next"],
        ["next", "g3"],
        ["next"],
        ["wout", "next"],
        ["next", "up", "nf"],
    ],
}
PHASE = {
    "pre": ["lnp", "np", "trp", "q", "k", "v", "stack0", "stack1"],
    "att": ["vpad", "turn", "pv0", "pv1", "pv2", "rinv", "resid", "l_wi"],
    "mid": ["pv3", "rb", "wo", "n2", "tr2", "f0", "f1", "f2", "f3", "g0", "g1", "g2", "g3", "tr3",
            "e0", "e1", "e2", "e3", "h0", "l_woe"],
    "start": ["w_bias", "split_qkv"],
    "once": ["c0", "c1", "c2", "c3", "w_end", "w_mid", "split_w1"],
    "end": ["h1", "h2", "h3", "ne", "tr4", "s1", "st1", "u1", "win", "s2", "st2", "u2", "wout", "down", "exp", "tr5",
            "up", "nf", "l_out"],
}
PHASE_OF = {stage: phase for phase, stages in PHASE.items() for stage in stages}

TWO_PI = 2.0 * math.pi
PI_1 = 6.28125
PI_2 = 0.001934051513671875
PI_3 = TWO_PI - PI_1 - PI_2
ROUND = 1.5 * 2.0 ** 23
PI_LIMIT = 3.1415925


def place(h):
    g, r = divmod(h, HG)
    half, quad = divmod(r, QUADS)
    return g, quad, half


def need(eng, sem, value):
    if isinstance(value, int) and value <= 0:
        return
    eng.wait_ge(sem, value)


def build(nc, a):
    with ExitStack() as ctx:
        def sb(name, shape, dt=F32):
            return ctx.enter_context(nc.sbuf_tensor(name, shape, dt))

        def bank(name, shape):
            return ctx.enter_context(nc.psum_tensor(name, shape, F32))

        def sem(name):
            return ctx.enter_context(nc.semaphore(name))

        ident = sb("ident", [P, P])
        mean_w = sb("mean_w", [P, P])
        neg_half = sb("neg_half", [P, 2])
        wq, wk, wv = ([sb(f"{n}_{part}", [P, DT, D], F32R) for part in ("hi", "lo")] for n in ("wq", "wk", "wv"))
        w1 = [sb(f"w1_{part}", [P, DT, F], F32R) for part in ("hi", "lo")]
        wo = sb("wo", [P, DT, D])
        w2 = sb("w2", [P, FT, D])
        wi = sb("wi", [P, DT, F])
        woe = sb("woe", [P, FT, D])
        w_in, w_out = sb("w_in", [P, DT, D]), sb("w_out", [P, DT, D])
        gam2, bet2 = sb("gam2", [P, DT, S]), sb("bet2", [P, DT, S])
        down_w = sb("down_w", [P, DT, A3])
        up_w = sb("up_w", [A3, D])
        vec = sb("vec", [P, 27])
        VQ, VK, VG2, VBE2, VB1, VBIN, VBOUT, VUPB, VDNB = 0, 2, 4, 6, 8, 16, 18, 20, 22
        qkb = sb("qkb", [P, 2])
        bv_row, b2_row = sb("bv_row", [P, D]), sb("b2_row", [P, D])
        lng_row, lnb_row = sb("lng_row", [P, D]), sb("lnb_row", [P, D])

        x_in = sb("x_in", [P, ST, D])
        xn = sb("xn", [P, ST, D])
        cond_cols = sb("cond_cols", [P, B, 4])
        cond2_cols = sb("cond2_cols", [P, B, 4])
        cols = sb("cols", [P, 4])
        rows = sb("rows", [P, 2 * D])
        x1T = sb("x1T", [P, DT, S])
        x1T_parts = [sb(f"x1T_{part}", [P, DT, S], F32R) for part in ("hi", "lo")]
        qkf = sb("qkf", [P, DT, S])
        q_hi, q_lo, k_hi, k_lo = (sb(n, [P, DT, S], F32R) for n in ("q_hi", "q_lo", "k_hi", "k_lo"))
        q_stack = sb("q_stack", [P, HG, S], F32R)
        k_stack = sb("k_stack", [P, HG, S], F32R)
        vpad = sb("vpad", [P, ST, H, 2 * HD])
        bias = sb("bias", [P, RING, 2, ST, S])
        mask_in = sb("mask_in", [P, ST, S], U8)
        mask_add = sb("mask_add", [P, ST, S])
        nmax = sb("nmax", [P, 4, ST])
        probs = sb("probs", [P, 4, ST, S])
        probsT = sb("probsT", [P, 2 * QUADS, ST, S])
        rowsum = sb("rowsum", [P, ST, H])
        rinv = sb("rinv", [P, ST, H])
        ctxT = sb("ctxT", [P, DT, S])
        resid = sb("resid", [P, ST, D])
        x2 = sb("x2", [P, ST, D])
        x2n = sb("x2n", [P, ST, D])
        x2b = sb("x2b", [P, ST, D])
        h1T = sb("h1T", [P, DT, S])
        h1T_parts = [sb(f"h1T_{part}", [P, DT, S], F32R) for part in ("hi", "lo")]
        hT = sb("hT", [P, FT, S])
        x3 = sb("x3", [P, ST, D])
        x3b = sb("x3b", [P, ST, D])
        x3T = sb("x3T", [P, DT, S])
        bo_row = sb("bo_row", [P, D])
        ep = sb("ep", [P, FT + 4])
        x4 = sb("x4", [P, ST, D])
        x4T = sb("x4T", [P, DT, S])
        cols2 = sb("cols2", [P, 4])
        u = sb("u", [P, DT, S])
        z = sb("z", [P, DT, S])
        rinv_sb = z
        y = sb("y", [P, DT, S])
        rinv_wide = y
        x5T = sb("x5T", [P, DT, S])
        x5b = sb("x5b", [P, DT, S])
        x5 = sb("x5", [P, ST, D])
        x6 = sb("x6", [P, ST, D])
        hid = sb("hid", [A3, S])
        dom = sb("dom", [A3, S])
        l3 = sb("l3", [A3, A3 + 2])
        idcol = sb("idcol", [A3, 1], I32)
        sel = sb("sel", [A3, 4])
        wsel = sb("wsel", [A3, A3])
        ids = sb("ids", [1, 2 * B], I32)
        ids_ok = sb("ids_ok", [1, 2 * B], I32)

        def stat_tiles(n):
            return (sb(f"bn{n}", [P, ST, 6]), sb(f"mv{n}", [P, ST, 2]), sb(f"ve{n}", [P, ST]), sb(f"rs{n}", [P, ST]))

        stat_p, stat_2, stat_e, stat_f = (stat_tiles(n) for n in "p2ef")
        g_bn, g_mv, g_all, g_ve, g_rs = (sb(n, [P, k]) for n, k in
                                         (("g_bn", 6), ("g_mv", 2), ("g_all", 2), ("g_ve", 2), ("g_rs", 1)))

        qkv_in = (x2, x2n, x2b)
        w1_in = (x3, x3b, x3T, x4)
        w_ada = hT[:, 0:4, :].rearrange("p (k a) n -> p k (a n)", k=2)
        w1c = hT[:, 4:6, :].rearrange("p a n -> p (a n)")
        w2c = woe[:, :, :].rearrange("p (k a) n -> p k (a n)", k=4)
        wsc = wi[:, 0, :].rearrange("p (k n) -> p k n", k=4)
        wsh = wi[:, 1, :].rearrange("p (k n) -> p k n", k=4)
        ang = u[:, 0, 0:48].rearrange("p (t b) -> p t b", t=3)
        red = u[:, 0, 48:96].rearrange("p (t b) -> p t b", t=3)
        kk = u[:, 0, 96:144].rearrange("p (t b) -> p t b", t=3)
        emb = u[:, 0, 144:192].rearrange("p (t b) -> p t b", t=3)
        fq = u[:, 1, 0:6]
        ph2 = u[:, 1, 6:9]
        t_f = u[:, 1, 16:48].rearrange("p (t b) -> p t b", t=2)
        h1c = u[:, 1, 48:112].rearrange("p (m b) -> p m b", m=4)
        h2c = u[:, 1, 112:176].rearrange("p (m b) -> p m b", m=4)
        cvec = z[:, 0, 0:16]
        t_i = z[:, 0, 16:32].bitcast(I32)
        ada_b = y[0:B, :, :].rearrange("p a n -> p (a n)")
        ada_c = x5T[0:B, :, :].rearrange("p a n -> p (a n)")
        emb_rows = x5b[0:B, :, :].rearrange("p a n -> p (a n)")

        sc_ps = [bank(f"sc_ps{i}", [P, ST, S]) for i in range(2)]
        pt_ps = bank("pt_ps", [P, ST, S])
        ctx_ps = bank("ctx_ps", [P, 2, S])
        pre_ps = bank("pre_ps", [P, 2, S])
        mid_ps = [bank(f"mid_ps{i}", [P, 2, S]) for i in range(2)]
        end_ps = bank("end_ps", [P, 2, S])

        names = """settled w_cond w_cond2 w_vec w_qk w_v w_1 split w_rows w_mid w_end w_id consts_v consts_p
        pro_v pro_a pro_p rows_out
        x_loaded cols_loaded rows_loaded mask_loaded wi_loaded woe_loaded ep_loaded bo_loaded cols2_loaded
        l3_loaded id_loaded out_stored stack0 stack1
        lnp rsq_p trp_pe x1T_done x1h_done x1l_done q_pe k_pe v_pe qkf_done hi_done lo_done v_done resid_done
        scored negated masked maxed exped turned turned_sb pv_done rinv_done
        rb_pe rb_sb ctx_done wo_pe ln2 rsq_2 x2b_done tr2_pe h1T_done h1h_done h1l_done
        ff1_pe ff1_done ff2_pe x3_done x3b_done
        tr3_pe x3T_done e1_pe e1_done e2_pe lne rsq_e
        tr4_pe x4T_done l2 st_pe rsq_g z_done win_pe y_done wout_pe x5b_done down_pe hid_done exp_pe dom_done
        sel_done tr5_pe x5_done up_pe lnf rsq_f fin""".split()
        s = {n: sem(n) for n in names}
        s_bias = [sem(f"bias_loaded{i}") for i in range(RING)]
        N = dict(lnp=7, rinv_done=2, x1T_done=2, qkf_done=4, hi_done=2, lo_done=2, v_done=4, resid_done=4,
                 scored=H, masked=H, maxed=2 * H, exped=2 * H, turned=H, turned_sb=H, pv_done=H,
                 ln2=8, x2b_done=2, h1T_done=2, ff1_pe=4, ff1_done=8, ff2_pe=2, x3_done=2, x3b_done=2,
                 e1_pe=4, e1_done=8, e2_pe=2, lne=9, x4T_done=2, l2=18, st_pe=2, rsq_g=2, z_done=4, y_done=2,
                 x5b_done=2, sel_done=6, lnf=8, fin=4)
        for n in ("x_loaded cols_loaded rows_loaded mask_loaded wi_loaded woe_loaded ep_loaded bo_loaded "
                  "cols2_loaded l3_loaded id_loaded out_stored").split():
            N[n] = DMA
        N["stack0"] = N["stack1"] = 8 * DMA

        def at(eng, name, batch, k=None):
            n = N.get(name, 1)
            k = n if k is None else k
            if isinstance(batch, int) and batch >= B:
                batch, k = B - 1, n
            need(eng, s[name], batch * n + k)
            if eng is nc.sync and not isinstance(batch, int):
                settle(eng)

        def settle(eng):
            eng.sem_inc(s["settled"], 1)

        x_v = a["x"].rearrange("b (t p) d -> b p t d", p=P)
        out_v = a["out"].rearrange("b (t p) d -> b p t d", p=P)
        f_v = a["fside"].rearrange("b h (t p) k -> b p h t k", p=P)
        mask_v = a["mask"].rearrange("b o (t p) k -> b p (o t) k", p=P)
        wi_v = a["Wi"].rearrange("e (k p) n -> e p k n", p=P)
        woe_v = a["Woe"].rearrange("e (k p) n -> e p k n", p=P)
        rows_d = nc.dram_tensor("rows_scratch", (B, 2 * D), F32, kind="Internal").ap()

        def k_tiles(w):
            return w.rearrange("(k p) n -> p k n", p=P)

        def drive(eng, engine, stages, of_head):
            def iteration(it, phases):
                for slot in range(H):
                    for stage in SCHEDULE[engine][slot]:
                        if stage in of_head:
                            of_head[stage](it, slot, phases)
                        elif stage in stages and PHASE_OF[stage] in phases:
                            stages[stage](it)

            def active(it):
                on = {"start": it == -1, "once": it == 0, "pre": 0 <= it + 1 < B, "att": 0 <= it < B,
                      "mid": 0 <= it - 1 < B, "end": 0 <= it - 2 < B}
                return [p for p, yes in on.items() if yes]

            for it in (-1, 0, 1, 2):
                iteration(it, active(it))
            with eng.Fori(3, B - 1) as it:
                iteration(it, active(3))
            for it in (B - 1, B, B + 1):
                iteration(it, active(it))

        block = ctx.enter_context(nc.Block())

        @block.sync
        def _(sp):
            def load(dst, src, name):
                sp.dma_start(dst, src).then_inc(s[name], DMA)

            load(fq, a["freqs"], "w_cond")
            load(t_i, a["timestep"].partition_broadcast(P), "w_cond")
            load(t_f[:, 1, :], a["t2"].partition_broadcast(P), "w_cond")
            load(cvec, a["cvec"], "w_cond")
            load(ids[:, 0:B], a["id1"].partition_broadcast(1), "w_cond")
            load(ids[:, B:], a["id3"].partition_broadcast(1), "w_cond")
            load(x_in[:], x_v[0], "x_loaded")
            load(w_ada, k_tiles(a["W_ada"]), "w_cond2")
            load(ident[:], a["ident"], "w_id")
            load(vec[:], a["vec"], "w_vec")
            load(qkv_in[0][:], k_tiles(a["Wq"]), "w_qk")
            load(qkv_in[1][:], k_tiles(a["Wk"]), "w_qk")
            load(mask_in[:], mask_v[0], "mask_loaded")
            sp.dma_start(bias[:, 0], f_v[0][:, 0:2]).then_inc(s_bias[0], DMA)
            load(qkv_in[2][:], k_tiles(a["Wv"]), "w_v")
            load(bv_row[:], a["bv"].partition_broadcast(P), "w_v")
            load(ada_b, a["b_ada"].partition_broadcast(B), "w_rows")
            load(ada_c[:, D:], a["bo"].partition_broadcast(B), "w_rows")

            def bias_ring(it):
                for pair in range(1, RING):
                    sp.dma_start(bias[:, pair], f_v[0][:, 2 * pair:2 * pair + 2]).then_inc(s_bias[pair], DMA)

            def weights_end(it):
                load(w1c, a["W1c"], "w_end")
                load(w2c, k_tiles(a["W2c"]), "w_end")
                load(wsc, k_tiles(a["Wsc"]), "w_end")
                load(wsh, k_tiles(a["Wsh"]), "w_end")

            def weights_mid(it):
                for c, tile_ in enumerate(w1_in):
                    load(tile_[:], k_tiles(a["W1"])[:, :, c * D:(c + 1) * D], "w_1")
                load(wo[:], k_tiles(a["Wo"]), "w_mid")
                load(w2[:], k_tiles(a["W2"]), "w_mid")
                load(b2_row[:], a["b2"].partition_broadcast(P), "w_mid")
                load(w_in[:], k_tiles(a["W_in"]), "w_mid")
                load(w_out[:], k_tiles(a["W_out"]), "w_mid")
                load(gam2[:], k_tiles(a["gamT"]), "w_mid")
                load(bet2[:], k_tiles(a["betT"]), "w_mid")
                load(down_w[:], k_tiles(a["down_wT"]), "w_mid")
                load(up_w[:], a["up_wT"], "w_mid")
                load(lng_row[:], a["ln_g"].partition_broadcast(P), "w_mid")
                load(lnb_row[:], a["ln_b"].partition_broadcast(P), "w_mid")

            def expert(batch, base, last):
                index = sp.value_load(ids_ok[0:1, bass.ds(base + batch, 1)], min_val=0, max_val=last)
                return index

            def bias_pair(it, slot, phases):
                if "att" in phases:
                    pair = slot // 2 + RING
                    if pair < H // 2 or "pre" in phases:
                        at(sp, "exped", it, 2 * (slot + 2))
                        batch = it if pair < H // 2 else it + 1
                        pair %= H // 2
                        sp.dma_start(bias[:, pair % RING], f_v[batch][:, 2 * pair:2 * pair + 2])\
                            .then_inc(s_bias[pair % RING], DMA)

            def loads_x(it, slot, phases):
                if "pre" in phases and not (isinstance(it, int) and it < 0):
                    at(sp, "lnp", it)
                    load(x_in[:], x_v[it + 1], "x_loaded")
                    at(sp, "x1T_done", it)
                    load(cols[:], cond_cols[:, it + 1, :], "cols_loaded")
                    at(sp, "negated", it)
                    load(mask_in[:], mask_v[it + 1], "mask_loaded")
                if "att" in phases:
                    if isinstance(it, int) and it == 0:
                        sp.wait_ge(s["pro_v"], PRO_ROWS)
                        load(rows_d, emb_rows, "rows_out")
                        sp.wait_ge(s["rows_out"], DMA)
                    at(sp, "resid_done", it - 1)
                    load(rows[:], rows_d[it].partition_broadcast(P), "rows_loaded")
                if "end" in phases:
                    if isinstance(it, int) and it == 2:
                        sp.wait_ge(s["pro_v"], PRO_COLS2)
                    at(sp, "z_done", it - 3)
                    load(cols2[:], cond2_cols[:, it - 2, :], "cols2_loaded")

            def loads_par(it, slot, phases):
                if "mid" in phases:
                    e = expert(it - 1, 0, NE1 - 1)
                    at(sp, "x4T_done", it - 2)
                    load(ep[:], a["ep"][e], "ep_loaded")
                    at(sp, "x3b_done", it - 2)
                    load(bo_row[:], a["boe"][e].partition_broadcast(P), "bo_loaded")
                if "end" in phases:
                    e = expert(it - 2, B, NE3 - 1)
                    at(sp, "dom_done", it - 3)
                    load(l3[:], a["l3"][e], "l3_loaded")
                    load(idcol[:], a["id3"][bass.ds(it - 2, 1)].partition_broadcast(A3), "id_loaded")

            def stack(it, t):
                at(sp, "lo_done", it + 1)
                at(sp, "scored", it, HG * (t + 1))
                for dst, parts in ((q_stack, (q_hi, q_hi, q_lo, q_lo)), (k_stack, (k_hi, k_lo, k_hi, k_lo))):
                    for j, part in enumerate(parts):
                        row = 4 * HD * t + HD * j
                        load(dst[row:row + HD].bitcast(F32), part[:, t, :].bitcast(F32), f"stack{t}")

            def load_wi(it):
                at(sp, "e1_pe", it - 1)
                if isinstance(it, int) and it == 0:
                    sp.wait_ge(s["pro_p"], PRO_PE_ALL)
                load(wi[:], wi_v[expert(it, 0, NE1 - 1)], "wi_loaded")

            def load_woe(it):
                at(sp, "e2_pe", it - 2)
                load(woe[:], woe_v[expert(it - 1, 0, NE1 - 1)], "woe_loaded")

            def store_out(it):
                at(sp, "fin", it - 2)
                load(out_v[it - 2], x6[:], "out_stored")

            stages = dict(l_wi=load_wi, l_woe=load_woe, l_out=store_out,
                          stack0=lambda it: stack(it, 0), stack1=lambda it: stack(it, 1),
                          w_bias=bias_ring, w_end=weights_end, w_mid=weights_mid)
            drive(sp, "SP", stages, dict(l_bias=bias_pair, l_x=loads_x, l_par=loads_par))
            sp.wait_ge(s["out_stored"], B * DMA)

        @block.tensor
        def _(pe):
            def turn(dst, src, name):
                for i in range(2):
                    for j in range(2):
                        last = pe.transpose(dst[:, j, i * P:(i + 1) * P], src[:, i, j * P:(j + 1) * P], ident[:])
                last.then_inc(s[name], 1)

            def product(dst, lhsT, rhs, kt):
                for k in range(kt):
                    last = pe.matmul(dst, lhsT(k), rhs(k), start=(k == 0), stop=(k == kt - 1))
                return last

            def split_product(dst, lhsT, rhs, kt):
                for k in range(kt):
                    for i, j in ((0, 0), (0, 1), (1, 0)):
                        last = pe.matmul(dst, lhsT(k, i), rhs(k, j), start=(k == 0 and i == j),
                                         stop=(k == kt - 1 and i == 1))
                return last

            pe.wait_ge(s["w_cond2"], DMA)
            pe.wait_ge(s["pro_a"], 2)
            for m in range(4):
                last = product(sc_ps[0][:, 0, m * B:(m + 1) * B], lambda k: w_ada[:, k, m * P:(m + 1) * P],
                               lambda k: emb[:, k, :], 2)
            last.then_inc(s["pro_p"], 1)
            product(mid_ps[0][0:B, :, :].rearrange("p a n -> p (a n)"), lambda k: emb[:, k, :],
                    lambda k: w_ada[:, k, :], 2).then_inc(s["pro_p"], 1)

            def c1(it):
                pe.wait_ge(s["w_end"], 4 * DMA)
                for m in range(4):
                    last = product(mid_ps[1][:, 0, m * B:(m + 1) * B], lambda k: w1c[:, m * P:(m + 1) * P],
                                   lambda k: emb[:, 2, :], 1)
                last.then_inc(s["pro_p"], 1)

            def c2(it):
                pe.wait_ge(s["pro_a"], 6)
                for m in range(4):
                    last = product(mid_ps[1][:, 1, m * B:(m + 1) * B], lambda k: w2c[:, k, m * P:(m + 1) * P],
                                   lambda k: h1c[:, k, :], 4)
                last.then_inc(s["pro_p"], 1)

            def c3(it):
                pe.wait_ge(s["pro_a"], 10)
                pe.wait_ge(s["pro_v"], PRO_ROWS)
                for i, w in enumerate((wsc, wsh)):
                    for m in range(2):
                        product(mid_ps[0][:, 0, (2 * i + m) * B:(2 * i + m + 1) * B],
                                lambda k: w[:, k, m * P:(m + 1) * P], lambda k: h2c[:, k, :], 4)\
                            .then_inc(s["pro_p"], 1)

            def scores(batch, h):
                at(pe, f"stack{h // HG}", batch)
                at(pe, "maxed", batch, 2 * h - 2)
                rows_ = slice(4 * HD * (h // HG), 4 * HD * (h // HG) + 4 * HD)
                for t in range(ST):
                    last = pe.matmul(sc_ps[h % 2][:, t, :], q_stack[rows_, h % HG, t * P:(t + 1) * P],
                                     k_stack[rows_, h % HG, :], start=True, stop=True)
                last.then_inc(s["scored"], 1)

            def next_scores(it, slot, phases):
                h = slot + SCORE_LEAD
                if "att" in phases and h < H:
                    scores(it, h)
                if "pre" in phases and h >= H:
                    if isinstance(it, int) and it < 0:
                        pe.wait_ge(s["pro_v"], PRO_COLS)
                    scores(it + 1, h - H)

            def turn_probs(it, slot, phases):
                if "att" in phases:
                    at(pe, "exped", it, 2 * slot + 2)
                    at(pe, "turned_sb", it, slot)
                    turn(pt_ps, probs[:, slot % 4], "turned")

            def pv(it, first):
                at(pe, "turned_sb", it, first + QUADS)
                if first == 0:
                    at(pe, "v_done", it)
                    at(pe, "ctx_done", it - 1)
                for k in range(ST):
                    for h in range(first, first + QUADS):
                        g, quad, half = place(h)
                        mm = pe.matmul(ctx_ps[32 * quad:32 * quad + 32, g, :], vpad[:, k, h, :],
                                       probsT[:, h % (2 * QUADS), k, :],
                                       start=(half == 0 and k == 0), stop=(half == 1 and k == ST - 1))
                        if k == ST - 1:
                            mm.then_inc(s["pv_done"], 1)

            def trp(it):
                if isinstance(it, int) and it < 0:
                    pe.wait_ge(s["w_id"], DMA)
                at(pe, "lnp", it + 1)
                at(pe, "v_done", it)
                turn(pre_ps, xn, "trp_pe")

            def project(w, name):
                for m in range(DT):
                    last = split_product(pre_ps[:, m, :], lambda k, part: w[part][:, k, m * P:(m + 1) * P],
                                         lambda k, part: x1T_parts[part][:, k, :], DT)
                last.then_inc(s[name], 1)

            def q(it):
                if isinstance(it, int) and it < 0:
                    pe.wait_ge(s["split"], 6)
                at(pe, "x1h_done", it + 1)
                at(pe, "x1l_done", it + 1)
                project(wq, "q_pe")

            def k_(it):
                at(pe, "qkf_done", it + 1, 2)
                project(wk, "k_pe")

            def v(it):
                at(pe, "qkf_done", it + 1, 4)
                for t in range(ST):
                    last = split_product(pre_ps[:, t, :], lambda k, part: x1T_parts[part][:, k, t * P:(t + 1) * P],
                                         lambda k, part: wv[part][:, k, :], DT)
                last.then_inc(s["v_pe"], 1)

            def rb(it):
                at(pe, "rinv_done", it - 1)
                at(pe, "e1_done", it - 2)
                if isinstance(it, int) and it == 1:
                    pe.wait_ge(s["w_mid"], 11 * DMA)
                    pe.wait_ge(s["pro_v"], PRO_COLS2)
                turn(mid_ps[0], rinv_wide, "rb_pe")

            def rows_product(dst, t, xT, w):
                return product(dst[:, t, :], lambda k: xT[:, k, t * P:(t + 1) * P], lambda k: w[:, k, :], DT)

            def long_product(part, xT, w, name):
                t, half = divmod(part, 2)
                for k in range(FT // 2 * half, FT // 2 * (half + 1)):
                    last = pe.matmul(mid_ps[1 - t][:, t, :], xT[:, k, t * P:(t + 1) * P], w[:, k, :],
                                     start=(k == 0), stop=(k == FT - 1))
                if half:
                    last.then_inc(s[name], 1)

            def cols_product(dst, m, w, n, xT):
                return product(dst[:, m, :], lambda k: w[:, k, n * P:(n + 1) * P], lambda k: xT[:, k, :], DT)

            def wo_(it):
                at(pe, "ctx_done", it - 1)
                at(pe, "rb_sb", it - 1)
                for t in range(ST):
                    last = rows_product(mid_ps[0], t, ctxT, wo)
                last.then_inc(s["wo_pe"], 1)

            def tr2(it):
                at(pe, "ln2", it - 1)
                at(pe, "lne", it - 2, 1)
                turn(mid_ps[1], x2n, "tr2_pe")

            def up_product(it, c, w, xT, name):
                for j in range(2):
                    last = cols_product(mid_ps[(c + 1) % 2], j, w, 2 * c + j, xT)
                last.then_inc(s[name], 1)

            def f(it, c):
                if c == 0:
                    if isinstance(it, int) and it == 1:
                        pe.wait_ge(s["split"], 14)
                    at(pe, "h1h_done", it - 1)
                    at(pe, "h1l_done", it - 1)
                elif c == 1:
                    at(pe, "lne", it - 2, 2)
                else:
                    at(pe, "ff1_done", it - 1, 2 * c - 2)
                for j in range(2):
                    n = 2 * c + j
                    last = split_product(mid_ps[(c + 1) % 2][:, j, :],
                                         lambda k, part: w1[part][:, k, n * P:(n + 1) * P],
                                         lambda k, part: h1T_parts[part][:, k, :], DT)
                last.then_inc(s["ff1_pe"], 1)

            def g(it, part):
                if part == 0:
                    at(pe, "ff1_done", it - 1)
                long_product(part, hT, w2, "ff2_pe")

            def tr3(it):
                at(pe, "x3_done", it - 1)
                turn(mid_ps[0], x3, "tr3_pe")

            def e(it, c):
                if c == 0:
                    at(pe, "wi_loaded", it - 1)
                    at(pe, "x3_done", it - 1)
                if c < 2:
                    at(pe, "x3T_done", it - 1)
                else:
                    at(pe, "e1_done", it - 1, 2 * c - 2)
                up_product(it, c, wi, x3T, "e1_pe")

            def h(batch, part):
                if part == 0:
                    at(pe, "e1_done", batch)
                    at(pe, "woe_loaded", batch)
                if part == 2:
                    at(pe, "ln2", batch + 1, 1)
                long_product(part, hT, woe, "e2_pe")

            def tr4(it):
                at(pe, "lne", it - 2)
                at(pe, "lnf", it - 3, 1)
                turn(end_ps, x4, "tr4_pe")

            def st(it, n):
                at(pe, "l2", it - 2, 3 + 8 * n)
                pe.matmul(end_ps[:, 0, 0:2], mean_w[:], g_mv[:], start=True, stop=True).then_inc(s["st_pe"], 1)

            def win(it):
                at(pe, "z_done", it - 2, 2)
                for m in range(DT):
                    last = cols_product(end_ps, m, w_in, m, z)
                last.then_inc(s["win_pe"], 1)

            def wout(it):
                at(pe, "z_done", it - 2, 4)
                for m in range(DT):
                    last = cols_product(end_ps, m, w_out, m, z)
                last.then_inc(s["wout_pe"], 1)

            def down(it):
                at(pe, "l2", it - 2)
                product(end_ps[0:A3, 0, :], lambda k: down_w[:, k, :], lambda k: x5T[:, k, :], DT)\
                    .then_inc(s["down_pe"], 1)

            def exp_(it):
                at(pe, "hid_done", it - 2)
                at(pe, "sel_done", it - 2)
                settle(pe)
                product(end_ps[0:A3, 0, :], lambda k: wsel[:], lambda k: hid[:], 1).then_inc(s["exp_pe"], 1)

            def tr5(it):
                at(pe, "x5b_done", it - 2)
                at(pe, "dom_done", it - 2)
                turn(end_ps, x5b, "tr5_pe")

            def up(it):
                at(pe, "x5_done", it - 2)
                for t in range(ST):
                    last = product(end_ps[:, t, :], lambda k: dom[:, t * P:(t + 1) * P], lambda k: up_w[:], 1)
                last.then_inc(s["up_pe"], 1)

            stages = dict(trp=trp, q=q, k=k_, v=v, rb=rb, wo=wo_, tr2=tr2, tr3=tr3, tr4=tr4,
                          st1=lambda it: st(it, 0), st2=lambda it: st(it, 1), win=win, wout=wout, down=down,
                          exp=exp_, tr5=tr5, up=up, h0=lambda it: h(it - 1, 0), c1=c1, c2=c2, c3=c3)
            for c in range(4):
                stages[f"f{c}"] = lambda it, c=c: f(it, c)
                stages[f"g{c}"] = lambda it, c=c: g(it, c)
                stages[f"e{c}"] = lambda it, c=c: e(it, c)
                if c:
                    stages[f"h{c}"] = lambda it, c=c: h(it - 2, c)

            for group in range(H // QUADS):
                stages[f"pv{group}"] = lambda it, group=group: pv(it - group // 3, QUADS * group)
            drive(pe, "PE", stages, {"next": next_scores, "turn": turn_probs})

        @block.scalar
        def _(act):
            def line(dst, src, func, bias, scale, name):
                act.activation(dst, src, func, bias=bias, scale=scale).then_inc(s[name], 1)

            act.wait_ge(s["pro_v"], PRO_ANGLE)
            line(emb, red, ACT.Sin, 0.0, 1.0, "pro_a")
            act.wait_ge(s["pro_a"], 1)
            act.activation(emb[:, 0:2, :], emb[:, 0:2, :], ACT.Silu).then_inc(s["pro_a"], 1)
            act.wait_ge(s["w_vec"], DMA)

            def c1(it):
                act.wait_ge(s["pro_p"], 3)
                for m in range(4):
                    line(h1c[:, m, :], mid_ps[1][:, 0, m * B:(m + 1) * B], ACT.Silu, cvec[:, 4 + m:5 + m], 1.0, "pro_a")

            def c2(it):
                act.wait_ge(s["pro_p"], 4)
                for m in range(4):
                    line(h2c[:, m, :], mid_ps[1][:, 1, m * B:(m + 1) * B], ACT.Identity, cvec[:, 8 + m:9 + m], 1.0,
                         "pro_a")

            def softmax(batch, h):
                if h == 0:
                    at(act, "rinv_done", batch - 1, 1)
                at(act, "turned", batch, h - 3)
                g, quad, half = place(h)
                col = g * HG + 2 * quad + half
                for t in range(ST):
                    at(act, "maxed", batch, 2 * h + t + 1)
                    act.activation(probs[:, h % 4, t, :], bias[:, h // 2 % RING, h % 2, t, :], ACT.Exp,
                                   bias=nmax[:, h % 4, t:t + 1], scale=-1.0,
                                   accum_out=rowsum[:, t, col:col + 1]).then_inc(s["exped"], 1)

            def next_softmax(it, slot, phases):
                h = slot + EXP_LEAD
                if "att" in phases and h < H:
                    softmax(it, h)
                if "pre" in phases and h >= H:
                    softmax(it + 1, h - H)

            def modulate(dst, src, tile_, c0, name):
                for m in range(DT):
                    line(dst[:, m, :], src[:, m, :], ACT.Identity, tile_[:, c0 + DT + m:c0 + DT + m + 1],
                         tile_[:, c0 + m:c0 + m + 1], name)

            def trp(it):
                at(act, "trp_pe", it + 1)
                if isinstance(it, int) and it < 0:
                    act.wait_ge(s["pro_v"], PRO_COLS)
                at(act, "cols_loaded", it)
                at(act, "x1l_done", it)
                first = isinstance(it, int) and it < 0
                modulate(x1T, pre_ps, cond_cols[:, 0, :] if first else cols, 0, "x1T_done")

            def qk(it, n, pe_done, vec_bias, scale):
                at(act, pe_done, it + 1)
                at(act, "lo_done", it + n, 1 + (1 - n))
                for m in range(DT):
                    line(qkf[:, m, :], pre_ps[:, m, :], ACT.Identity, vec_bias[:, m:m + 1], scale, "qkf_done")

            def rb(it):
                at(act, "rb_pe", it - 1)
                at(act, "ctx_done", it - 2)
                act.activation(rinv_sb[:], mid_ps[0][:], ACT.Copy).then_inc(s["rb_sb"], 1)

            def tr2(it):
                at(act, "tr2_pe", it - 1)
                modulate(h1T, mid_ps[1], vec, VG2, "h1T_done")

            def hidden(it, half, func, bias_tile, b0, pe_name, name):
                for c in range(2):
                    at(act, pe_name, it - 1, 2 * half + c + 1)
                    for j in range(2):
                        f = 4 * half + 2 * c + j
                        line(hT[:, f, :], mid_ps[(c + 1) % 2][:, j, :], func, bias_tile[:, b0 + f:b0 + f + 1], 1.0,
                             name)

            def tr3(it):
                at(act, "tr3_pe", it - 1)
                act.activation(x3T[:], mid_ps[0][:], ACT.Copy).then_inc(s["x3T_done"], 1)

            def expert_hidden(it, half):
                if half == 0:
                    at(act, "ep_loaded", it - 1)
                hidden(it, half, ACT.Gelu, ep, 0, "e1_pe", "e1_done")

            def tr4(it):
                at(act, "tr4_pe", it - 2)
                modulate(x4T, end_ps, ep, FT, "x4T_done")

            def silu(it, n):
                at(act, "l2", it - 2, 8 + 8 * n)
                at(act, "cols2_loaded", it - 2)
                for m in range(DT):
                    line(z[:, m, :], u[:, m, :], ACT.Silu, cols2[:, DT + m:DT + m + 1], cols2[:, m:m + 1], "z_done")

            def win(it):
                at(act, "win_pe", it - 2)
                for m in range(DT):
                    line(y[:, m, :], end_ps[:, m, :], ACT.Identity, vec[:, VBIN + m:VBIN + m + 1], 1.0, "y_done")

            def down(it):
                at(act, "down_pe", it - 2)
                line(hid[:], end_ps[0:A3, 0, :], ACT.Gelu, vec[0:A3, VDNB:VDNB + 1], 1.0, "hid_done")

            def exp_(it):
                at(act, "exp_pe", it - 2)
                line(dom[:], end_ps[0:A3, 0, :], ACT.Identity, sel[:, 3:4], 1.0, "dom_done")

            stages = dict(
                trp=trp, q=lambda it: qk(it, 0, "q_pe", qkb[:], 0.25),
                k=lambda it: qk(it, 1, "k_pe", vec[:, VK:VK + 2], 1.0),
                rb=rb, tr2=tr2,
                f1=lambda it: hidden(it, 0, ACT.Gelu_apprx_sigmoid, vec, VB1, "ff1_pe", "ff1_done"),
                f3=lambda it: hidden(it, 1, ACT.Gelu_apprx_sigmoid, vec, VB1, "ff1_pe", "ff1_done"),
                tr3=tr3, e1=lambda it: expert_hidden(it, 0), e3=lambda it: expert_hidden(it, 1),
                tr4=tr4, u1=lambda it: silu(it, 0), u2=lambda it: silu(it, 1), win=win, down=down, exp=exp_,
                c1=c1, c2=c2)
            drive(act, "ACT", stages, {"next": next_softmax})

        @block.vector
        def _(dve):
            dve.memset(mean_w[:], 1.0 / P).then_inc(s["consts_v"], 1)
            dve.memset(vpad[:, 0], 0.0).then_inc(s["consts_v"], 1)
            dve.memset(vpad[:, 1], 0.0).then_inc(s["consts_v"], 1)
            pro = [0]

            def step(ins):
                pro[0] += 1
                ins.then_inc(s["pro_v"], 1)
                dve.wait_ge(s["pro_v"], pro[0])

            dve.wait_ge(s["w_cond"], 6 * DMA)
            step(dve.tensor_copy(t_f[:, 0, :], t_i))
            step(dve.tensor_scalar(ang[:, 0, :], t_f[:, 0, :], 40.0, None, ALU.mult))
            step(dve.tensor_scalar(ang[:, 1, :], t_f[:, 0, :], 40.0, None, ALU.mult))
            step(dve.tensor_scalar(ang[:, 2, :], t_f[:, 1, :], 5000.0, None, ALU.mult))
            wide = [P, 3, B]
            step(dve.tensor_tensor(ang, ang, fq[:, 0:3].unsqueeze(2).to_broadcast(wide), ALU.mult))
            step(dve.scalar_tensor_tensor(out=kk, in0=ang, scalar=1.0 / TWO_PI,
                                          in1=fq[:, 3:6].unsqueeze(2).to_broadcast(wide), op0=ALU.mult, op1=ALU.add))
            step(dve.tensor_scalar(kk, kk, ROUND, None, ALU.add))
            step(dve.tensor_scalar(kk, kk, ROUND, None, ALU.subtract))
            step(dve.scalar_tensor_tensor(out=red, in0=kk, scalar=-PI_1, in1=ang, op0=ALU.mult, op1=ALU.add))
            step(dve.scalar_tensor_tensor(out=red, in0=kk, scalar=-PI_2, in1=red, op0=ALU.mult, op1=ALU.add))
            step(dve.scalar_tensor_tensor(out=red, in0=kk, scalar=-PI_3, in1=red, op0=ALU.mult, op1=ALU.add))
            step(dve.tensor_scalar(ph2, fq[:, 3:6], TWO_PI, None, ALU.mult))
            step(dve.tensor_tensor(red, red, ph2.unsqueeze(2).to_broadcast(wide), ALU.add))
            step(dve.tensor_scalar(red, red, -PI_LIMIT, PI_LIMIT, ALU.max, ALU.min))
            assert pro[0] == PRO_ANGLE
            step(dve.tensor_scalar(ids_ok[:, 0:B], ids[:, 0:B], 0, NE1 - 1, ALU.max, ALU.min))
            step(dve.tensor_scalar(ids_ok[:, B:], ids[:, B:], 0, NE3 - 1, ALU.max, ALU.min))
            dve.wait_ge(s["w_vec"], DMA)
            step(dve.tensor_scalar(qkb[:], vec[:, VQ:VQ + 2], 0.25, None, ALU.mult))
            dve.wait_ge(s["pro_p"], 1)
            for m in range(4):
                step(dve.tensor_scalar(cond_cols[:, :, m], sc_ps[0][:, 0, m * B:(m + 1) * B], cvec[:, m:m + 1],
                                       1.0 if m < 2 else 0.0, ALU.add, ALU.add))
            assert pro[0] == PRO_COLS
            dve.wait_ge(s["consts_v"], 3)

            def split(src, parts, cut):
                dve.tensor_copy(parts[0][:, :, cut], src).then_inc(s["split"], 1)
                pro_split[0] += 1
                dve.wait_ge(s["split"], pro_split[0])
                dve.tensor_tensor(parts[1][:, :, cut], src, parts[0][:, :, cut].bitcast(F32), ALU.subtract)\
                    .then_inc(s["split"], 1)
                pro_split[0] += 1

            pro_split = [0]

            def split_qkv(it):
                dve.wait_ge(s["w_qk"], 2 * DMA)
                split(qkv_in[0][:], wq, slice(0, D))
                split(qkv_in[1][:], wk, slice(0, D))
                dve.wait_ge(s["w_v"], 2 * DMA)
                split(qkv_in[2][:], wv, slice(0, D))

            def split_w1(it):
                dve.wait_ge(s["w_1"], 4 * DMA)
                for c, tile_ in enumerate(w1_in):
                    split(tile_[:], w1, slice(c * D, (c + 1) * D))

            def high(ready, batch, dst, src, name):
                at(dve, ready, batch)
                dve.tensor_copy(dst[:], src[:]).then_inc(s[name], 1)

            def split_h1(it):
                high("h1T_done", it - 1, h1T_parts[0], h1T, "h1h_done")
                at(dve, "h1h_done", it - 1)
                dve.tensor_tensor(h1T_parts[1][:], h1T[:], h1T_parts[0][:].bitcast(F32), ALU.subtract)\
                    .then_inc(s["h1l_done"], 1)

            def c0(it):
                dve.wait_ge(s["pro_p"], 2)
                dve.wait_ge(s["w_rows"], 2 * DMA)
                step(dve.memset(ada_c[:, 0:D], 1.0))
                step(dve.tensor_tensor(emb_rows, mid_ps[0][0:B, :, :].rearrange("p a n -> p (a n)"), ada_b, ALU.add))
                step(dve.tensor_tensor(emb_rows, emb_rows, ada_c, ALU.add))
                assert pro[0] == PRO_ROWS

            def c3(it):
                dve.wait_ge(s["pro_p"], PRO_PE_ALL)
                for m in range(4):
                    step(dve.tensor_scalar(cond2_cols[:, :, m], mid_ps[0][:, 0, m * B:(m + 1) * B],
                                           cvec[:, 12 + m:13 + m], None, ALU.add))
                assert pro[0] == PRO_COLS2

            def maxima(batch, h):
                at(dve, "scored", batch, h + 1)
                at(dve, "masked", batch, h + 1)
                at(dve, "exped", batch, 2 * h - 6)
                settle(dve)
                for t in range(ST):
                    b = bias[:, h // 2 % RING, h % 2, t, :]
                    dve.tensor_tensor_reduce(b, sc_ps[h % 2][:, t, :], b, -1.0, BIG, ALU.add, ALU.min,
                                             nmax[:, h % 4, t:t + 1]).then_inc(s["maxed"], 1)

            def next_maxima(it, slot, phases):
                h = slot + SCORE_LEAD
                if "att" in phases and h < H:
                    maxima(it, h)
                if "pre" in phases and h >= H:
                    maxima(it + 1, h - H)

            def evacuate(it, slot, phases):
                if "att" in phases:
                    at(dve, "turned", it, slot + 1)
                    at(dve, "pv_done", it, QUADS * (slot // QUADS - 1))
                    dve.tensor_copy(probsT[:, slot % (2 * QUADS)], pt_ps[:]).then_inc(s["turned_sb"], 1)

            def rinv_(it):
                at(dve, "exped", it)
                at(dve, "rb_pe", it - 1)
                dve.reciprocal(rinv[:], rowsum[:]).then_inc(s["rinv_done"], 1)
                at(dve, "rinv_done", it, 1)
                dve.tensor_copy(rinv_wide[:].rearrange("p t (h d) -> p (t h) d", d=HD),
                                rinv[:].rearrange("p t h -> p (t h)").unsqueeze(2)
                                .to_broadcast([P, ST * H, HD])).then_inc(s["rinv_done"], 1)

            def row_stats(batch, src, tiles, name, k, eps):
                bn, mv, ve, rs = tiles
                for t in range(ST):
                    dve.bn_stats(bn[:, t, :], src[:, t, :]).then_inc(s[name], 1)
                for t in range(ST):
                    at(dve, name, batch, k + t + 1)
                    settle(dve)
                    dve.bn_aggr(mv[:, t, :], bn[:, t, :]).then_inc(s[name], 1)
                at(dve, name, batch, k + 4)
                dve.tensor_scalar(ve[:], mv[:, :, 1], eps, None, ALU.add).then_inc(s[name], 1)

            def row_norm(batch, src, tiles, name, rsq, dst):
                bn, mv, ve, rs = tiles
                at(dve, rsq, batch)
                for t in range(ST):
                    dve.tensor_scalar(dst[:, t, :], src[:, t, :], mv[:, t, 0:1], rs[:, t:t + 1],
                                      ALU.subtract, ALU.mult).then_inc(s[name], 1)

            def lnp(it):
                at(dve, "x_loaded", it + 1)
                row_stats(it + 1, x_in, stat_p, "lnp", 0, 1e-5)

            def np_(it):
                at(dve, "resid_done", it)
                at(dve, "trp_pe", it)
                row_norm(it + 1, x_in, stat_p, "lnp", "rsq_p", xn)

            def hi(it, n, dst):
                at(dve, "qkf_done", it + 1, 2 * n + 2)
                if n == 0:
                    at(dve, "stack0", it)
                    at(dve, "stack1", it)
                dve.tensor_copy(dst[:], qkf[:]).then_inc(s["hi_done"], 1)

            def vpad_(it):
                if isinstance(it, int) and it == 0:
                    dve.wait_ge(s["w_v"], 2 * DMA)
                at(dve, "v_pe", it)
                at(dve, "pv_done", it - 1)
                for k in range(ST):
                    for half in range(2):
                        def heads(ap):
                            return ap.rearrange("p (g f j d) -> p g f j d", g=DT, f=2, j=QUADS)[:, :, half]
                        dst = vpad[:, k, :, half * HD:(half + 1) * HD]\
                            .rearrange("p (g f j) d -> p g f j d", g=DT, f=2)[:, :, half]
                        dve.tensor_tensor(dst, heads(pre_ps[:, k, :]), heads(bv_row[:]), ALU.add)\
                            .then_inc(s["v_done"], 1)

            def rb(it):
                at(dve, "rb_sb", it - 1)
                at(dve, "pv_done", it - 1)
                at(dve, "wo_pe", it - 2)
                dve.tensor_tensor(ctxT[:], ctx_ps[:], rinv_sb[:], ALU.mult).then_inc(s["ctx_done"], 1)

            def wo_(it):
                at(dve, "wo_pe", it - 1)
                at(dve, "resid_done", it - 1)
                at(dve, "x2b_done", it - 2)
                dve.tensor_tensor(x2[:], mid_ps[0][:], resid[:], ALU.add).then_inc(s["ln2"], 1)
                at(dve, "ln2", it - 1, 1)
                row_stats(it - 1, x2, stat_2, "ln2", 1, 1e-5)

            def ff2(it, t):
                at(dve, "ff2_pe", it - 1, t + 1)
                at(dve, "x2b_done", it - 1, t + 1)
                at(dve, "x3b_done", it - 2)
                dve.tensor_tensor(x3[:, t, :], mid_ps[1 - t][:, t, :], x2b[:, t, :], ALU.add).then_inc(s["x3_done"], 1)

            def h(it, t):
                at(dve, "e2_pe", it - 2, t + 1)
                at(dve, "tr4_pe", it - 3)
                at(dve, "x3b_done", it - 2, t + 1)
                dve.tensor_tensor(x4[:, t, :], mid_ps[1 - t][:, t, :], x3b[:, t, :], ALU.add).then_inc(s["lne"], 1)
                if t == 1:
                    at(dve, "lne", it - 2, 2)
                    row_stats(it - 2, x4, stat_e, "lne", 2, 1e-12)

            def matrix_stats(it, n, src, ready):
                at(dve, *ready)
                k = 8 * n
                at(dve, "st_pe", it - 2 - (1 - n), 1 if n else 2)
                dve.bn_stats(g_bn[:], src[:].rearrange("p a n -> p (a n)")).then_inc(s["l2"], 1)
                at(dve, "l2", it - 2, k + 1)
                settle(dve)
                dve.bn_aggr(g_mv[:], g_bn[:]).then_inc(s["l2"], 1)
                at(dve, "l2", it - 2, k + 2)
                dve.scalar_tensor_tensor(out=g_mv[:, 1:2], in0=g_mv[:, 0:1], scalar=g_mv[:, 0:1], in1=g_mv[:, 1:2],
                                         op0=ALU.mult, op1=ALU.add).then_inc(s["l2"], 1)

            def matrix_norm(it, n, src):
                k = 8 * n
                at(dve, "st_pe", it - 2, n + 1)
                dve.tensor_copy(g_all[:], end_ps[:, 0, 0:2]).then_inc(s["l2"], 1)
                at(dve, "l2", it - 2, k + 4)
                dve.scalar_tensor_tensor(out=g_ve[:, 0:1], in0=g_all[:, 0:1], scalar=g_all[:, 0:1],
                                         in1=g_all[:, 1:2], op0=ALU.mult, op1=ALU.subtract).then_inc(s["l2"], 1)
                at(dve, "l2", it - 2, k + 5)
                dve.tensor_scalar(g_ve[:, 1:2], g_ve[:, 0:1], -1.0, 1e-5, ALU.mult, ALU.add).then_inc(s["l2"], 1)
                at(dve, "z_done", it - 2, 2 * n)
                dve.scalar_tensor_tensor(out=u[:], in0=src[:], scalar=g_all[:, 0:1], in1=gam2[:],
                                         op0=ALU.subtract, op1=ALU.mult).then_inc(s["l2"], 1)
                at(dve, "l2", it - 2, k + 7)
                at(dve, "rsq_g", it - 2, n + 1)
                dve.scalar_tensor_tensor(out=u[:], in0=u[:], scalar=g_rs[:, 0:1], in1=bet2[:],
                                         op0=ALU.mult, op1=ALU.add).then_inc(s["l2"], 1)

            def wout(it):
                at(dve, "wout_pe", it - 2)
                at(dve, "x5b_done", it - 3)
                for m in range(DT):
                    dve.scalar_tensor_tensor(out=x5T[:, m, :], in0=end_ps[:, m, :],
                                             scalar=vec[:, VBOUT + m:VBOUT + m + 1], in1=x4T[:, m, :],
                                             op0=ALU.add, op1=ALU.add).then_inc(s["l2"], 1)

            def select(it):
                at(dve, "l3_loaded", it - 2)
                at(dve, "id_loaded", it - 2)
                b = it - 2
                dve.tensor_scalar(sel[:, 0:1], idcol[:], 0.0, None, ALU.is_ge).then_inc(s["sel_done"], 1)
                at(dve, "sel_done", b, 1)
                dve.scalar_tensor_tensor(out=sel[:, 1:2], in0=idcol[:], scalar=float(NE3), in1=sel[:, 0:1],
                                         op0=ALU.is_lt, op1=ALU.mult).then_inc(s["sel_done"], 1)
                at(dve, "sel_done", b, 2)
                dve.tensor_scalar(sel[:, 2:3], sel[:, 1:2], -1.0, 1.0, ALU.mult, ALU.add).then_inc(s["sel_done"], 1)
                at(dve, "sel_done", b, 3)
                dve.tensor_scalar(wsel[:], ident[0:A3, 0:A3], sel[:, 2:3], None, ALU.mult).then_inc(s["sel_done"], 1)
                at(dve, "sel_done", b, 4)
                dve.scalar_tensor_tensor(out=wsel[:], in0=l3[:, 0:A3], scalar=sel[:, 1:2], in1=wsel[:],
                                         op0=ALU.mult, op1=ALU.add).then_inc(s["sel_done"], 1)
                dve.scalar_tensor_tensor(out=sel[:, 3:4], in0=l3[:, A3:A3 + 1], scalar=sel[:, 1:2],
                                         in1=l3[:, A3 + 1:A3 + 2], op0=ALU.mult, op1=ALU.add)\
                    .then_inc(s["sel_done"], 1)

            def tr5(it):
                at(dve, "tr5_pe", it - 2)
                dve.tensor_copy(x5[:], end_ps[:]).then_inc(s["x5_done"], 1)

            def up(it):
                at(dve, "up_pe", it - 2)
                at(dve, "x5_done", it - 2)
                at(dve, "out_stored", it - 3)
                dve.tensor_tensor(x6[:], end_ps[:], x5[:], ALU.add).then_inc(s["lnf"], 1)
                at(dve, "lnf", it - 2, 1)
                row_stats(it - 2, x6, stat_f, "lnf", 1, 1e-5)

            stages = dict(
                lnp=lnp, q=lambda it: hi(it, 0, q_hi), k=lambda it: hi(it, 1, k_hi), vpad=vpad_, rb=rb, wo=wo_,
                np=np_, n2=lambda it: row_norm(it - 1, x2, stat_2, "ln2", "rsq_2", x2n),
                g1=lambda it: ff2(it, 0), g3=lambda it: ff2(it, 1), h1=lambda it: h(it, 0), h3=lambda it: h(it, 1),
                ne=lambda it: row_norm(it - 2, x4, stat_e, "lne", "rsq_e", x4),
                nf=lambda it: row_norm(it - 2, x6, stat_f, "lnf", "rsq_f", x6),
                s1=lambda it: matrix_stats(it, 0, x4T, ("x4T_done", it - 2)), u1=lambda it: matrix_norm(it, 0, x4T),
                s2=lambda it: matrix_stats(it, 1, y, ("y_done", it - 2)), u2=lambda it: matrix_norm(it, 1, y),
                wout=wout, down=select, tr5=tr5, up=up, rinv=rinv_, c0=c0, c3=c3,
                split_qkv=split_qkv, split_w1=split_w1,
                trp=lambda it: high("x1T_done", it + 1, x1T_parts[0], x1T, "x1h_done"),
                tr2=split_h1)
            drive(dve, "DVE", stages, {"next": next_maxima, "turn": evacuate})

        @block.gpsimd
        def _(pool):
            pool.memset(neg_half[:], -0.5).then_inc(s["consts_p"], 1)
            pool.wait_ge(s["consts_p"], 1)

            def negate(batch):
                at(pool, "mask_loaded", batch)
                at(pool, "masked", batch - 1)
                settle(pool)
                pool.tensor_scalar(mask_add[:], mask_in[:], MASKED, None, ALU.mult).then_inc(s["negated"], 1)

            def add_mask(batch, h):
                pair = h // 2
                at(pool, "negated", batch)
                need(pool, s_bias[pair % RING], batch * 2 * DMA + DMA * (pair // RING + 1))
                b = bias[:, pair % RING, h % 2]
                pool.tensor_tensor(b, b, mask_add[:], ALU.add).then_inc(s["masked"], 1)

            def mask_ahead(it, slot, phases):
                ahead = slot + MASK_LEAD
                if ahead < H:
                    if "att" in phases:
                        add_mask(it, ahead)
                elif "pre" in phases:
                    if ahead == H:
                        negate(it + 1)
                    add_mask(it + 1, ahead - H)

            def inv_sqrt(batch, name, k, rsq, ve, rs):
                at(pool, name, batch, k)
                pool.tensor_tensor(rs, ve, neg_half[:, 0:ve.shape[1]], ALU.pow).then_inc(s[rsq], 1)

            def lo(it, n, dst, hi):
                at(pool, "hi_done", it + 1, n + 1)
                pool.tensor_tensor(dst[:], qkf[:], hi[:].bitcast(F32), ALU.subtract).then_inc(s["lo_done"], 1)

            def low(batch, dst, src, ready, name):
                at(pool, ready, batch)
                pool.tensor_tensor(dst[1][:], src[:], dst[0][:].bitcast(F32), ALU.subtract).then_inc(s[name], 1)

            def resid_(it):
                at(pool, "rows_loaded", it)
                at(pool, "lnp", it)
                at(pool, "ln2", it - 1, 1)
                for t in range(ST):
                    pool.tensor_tensor(resid[:, t, :], xn[:, t, :], rows[:, 0:D], ALU.mult)\
                        .then_inc(s["resid_done"], 1)
                for t in range(ST):
                    at(pool, "resid_done", it, t + 1)
                    pool.tensor_tensor(resid[:, t, :], resid[:, t, :], rows[:, D:], ALU.add)\
                        .then_inc(s["resid_done"], 1)

            def add_row(batch, dst, src, row, name):
                for t in range(ST):
                    pool.tensor_tensor(dst[:, t, :], src[:, t, :], row[:], ALU.add).then_inc(s[name], 1)

            def wo_(it):
                inv_sqrt(it - 1, "ln2", 6, "rsq_2", stat_2[2][:], stat_2[3][:])
                at(pool, "x3_done", it - 2)
                add_row(it - 1, x2b, x2, b2_row, "x2b_done")

            def g3(it):
                at(pool, "x3_done", it - 1)
                at(pool, "bo_loaded", it - 1)
                at(pool, "lne", it - 2, 2)
                add_row(it - 1, x3b, x3, bo_row, "x3b_done")

            def wout(it):
                at(pool, "l2", it - 2)
                at(pool, "tr5_pe", it - 3)
                settle(pool)
                for m in range(DT):
                    pool.tensor_scalar(x5b[:, m, :], x5T[:, m, :], vec[:, VUPB + m:VUPB + m + 1], None, ALU.add)\
                        .then_inc(s["x5b_done"], 1)

            def nf(it):
                for t in range(ST):
                    at(pool, "lnf", it - 2, 7 + t)
                    pool.tensor_tensor(x6[:, t, :], x6[:, t, :], lng_row[:], ALU.mult).then_inc(s["fin"], 1)
                for t in range(ST):
                    at(pool, "fin", it - 2, t + 1)
                    pool.tensor_tensor(x6[:, t, :], x6[:, t, :], lnb_row[:], ALU.add).then_inc(s["fin"], 1)

            stages = dict(
                lnp=lambda it: inv_sqrt(it + 1, "lnp", 5, "rsq_p", stat_p[2][:], stat_p[3][:]),
                q=lambda it: lo(it, 0, q_lo, q_hi), k=lambda it: lo(it, 1, k_lo, k_hi), resid=resid_,
                trp=lambda it: low(it + 1, x1T_parts, x1T, "x1h_done", "x1l_done"),
                wo=wo_, g3=g3,
                h3=lambda it: inv_sqrt(it - 2, "lne", 7, "rsq_e", stat_e[2][:], stat_e[3][:]),
                u1=lambda it: inv_sqrt(it - 2, "l2", 6, "rsq_g", g_ve[:, 1:2], g_rs[:]),
                u2=lambda it: inv_sqrt(it - 2, "l2", 14, "rsq_g", g_ve[:, 1:2], g_rs[:]),
                wout=wout, up=lambda it: inv_sqrt(it - 2, "lnf", 6, "rsq_f", stat_f[2][:], stat_f[3][:]), nf=nf)
            drive(pool, "POOL", stages, {"next": mask_ahead})


PRO_PE_ALL = 8
PRO_ANGLE = 14
PRO_COLS = PRO_ANGLE + 3 + 4
PRO_ROWS = PRO_COLS + 3
PRO_COLS2 = PRO_ROWS + 4


def kernel(**inputs):
    import concourse.bacc as bacc
    from concourse.bass_utils import run_bass_kernel_spmd

    g = {k: np.asarray(v) for k, v in inputs.items()}

    def columns(v):
        return v.reshape(-1, P).T

    def head_order(w):
        return w.reshape(w.shape[:-1] + (DT, HG, HD)).swapaxes(-1, -2).reshape(w.shape)

    def place_order(w):
        return w.reshape(DT, 2, QUADS, HD, -1).swapaxes(1, 2).reshape(w.shape)

    half0, half2 = D // 2, 64
    freq0 = np.exp(np.arange(half0, dtype=np.float32) * np.float32(-math.log(10000.0) / (half0 - 1)))
    freq2 = np.exp(np.arange(half2, dtype=np.float32) * np.float32(-math.log(10000.0) / (half2 - 1)))
    freqs = np.zeros((P, 6), np.float32)
    freqs[:, 0] = freqs[:, 1] = freq0
    freqs[:, 2] = np.concatenate([freq2, freq2])
    freqs[:, 4] = 0.25
    freqs[half2:, 5] = 0.25
    L0, L1, L2, L3 = (f"L{i}_cond_" for i in range(4))
    down_b = np.zeros((P, 1), np.float32)
    down_b[:A3, 0] = g[L3 + "down_b"]
    vec = np.concatenate([columns(head_order(g[L0 + "bq"])), columns(head_order(g[L0 + "bk"])),
                          columns(g[L0 + "g2"]), columns(g[L0 + "beta2"]), columns(g[L0 + "b1"]),
                          columns(g[L2 + "b_in"]), columns(g[L2 + "b_out"]), columns(g[L3 + "up_b"]), down_b,
                          np.zeros((P, 4), np.float32)], axis=1)
    cvec = np.concatenate([columns(g[L0 + "b_ada"]), columns(g[L2 + "b1"]), columns(g[L2 + "b2"]),
                           columns(g[L2 + "bsc"]), columns(g[L2 + "bsh"])], axis=1)
    ep = np.concatenate([g[L1 + n].reshape(NE1, -1, P).transpose(0, 2, 1) for n in ("bi", "gamma", "beta")], axis=2)
    l3 = np.concatenate([g[L3 + "expert_W"].transpose(0, 2, 1), g[L3 + "expert_b"][:, :, None],
                         g[L3 + "domain_emb"][:, :, None]], axis=2)
    data = {
        "x": g["x"], "fside": g["fside_Bx16xSxS_0"], "mask": g["mask_Bx1xSxS_bk0"],
        "timestep": g["itok_B_34_63"], "id1": g["itok_B_0_7"], "id3": g["itok_B_0_15"], "t2": g["condB_t"],
        "freqs": freqs, "ident": np.eye(P, dtype=np.float32), "vec": vec, "cvec": cvec,
        "W_ada": g[L0 + "W_ada"], "b_ada": g[L0 + "b_ada"], "bo": g[L0 + "bo"],
        "Wq": head_order(g[L0 + "Wq"]), "Wk": head_order(g[L0 + "Wk"]), "Wv": g[L0 + "Wv"], "bv": g[L0 + "bv"],
        "Wo": place_order(g[L0 + "Wo"]), "W1": g[L0 + "W1"], "W2": g[L0 + "W2"], "b2": g[L0 + "b2"],
        "Wi": g[L1 + "Wi"], "Woe": g[L1 + "Wo"], "boe": g[L1 + "bo"], "ep": ep,
        "W1c": g[L2 + "W1"], "W2c": g[L2 + "W2"], "Wsc": g[L2 + "Wsc"], "Wsh": g[L2 + "Wsh"],
        "W_in": g[L2 + "W_in"], "W_out": g[L2 + "W_out"], "gamT": g[L2 + "gamma"].T, "betT": g[L2 + "beta"].T,
        "down_wT": g[L3 + "down_W"].T, "up_wT": g[L3 + "up_W"].T, "l3": l3,
        "ln_g": g[L3 + "ln_gamma"], "ln_b": g[L3 + "ln_beta"],
    }
    nc = bacc.Bacc("TRN2", target_bir_lowering=False, num_devices=1)
    arrays, args = {}, {}
    for name, value in data.items():
        value = np.ascontiguousarray(value)
        arrays[f"in_{name}"] = value
        args[name] = nc.dram_tensor(f"in_{name}", value.shape, mybir.dt.from_np(value.dtype), kind="ExternalInput").ap()
    args["out"] = nc.dram_tensor("out_0", (B, S, D), F32, kind="ExternalOutput").ap()
    build(nc, args)
    result = run_bass_kernel_spmd(nc, [arrays], core_ids=[0])
    return result.results[0]["out_0"]
```
